# Optimizing a Trainium2 kernel written in Bass

```python
import numpy as np
import jax
import jax.numpy as jnp

def _softmax(x, axis=-1):
    return jax.nn.softmax(x, axis=axis)

def _gelu(x):
    return jax.nn.gelu(x, approximate=True)

def _silu(x):
    return jax.nn.silu(x)

def _sigmoid(x):
    return jax.nn.sigmoid(x)

def _layernorm(x, axis=-1, eps=1e-05):
    m = jnp.mean(x, axis=axis, keepdims=True)
    v = jnp.var(x, axis=axis, keepdims=True)
    return (x - m) / jnp.sqrt(v + eps)

def _scatter_add(tgt, idx, src, axis=0):
    return tgt.at[idx].add(src)

def _segment_sum(src, seg, n):
    return jax.ops.segment_sum(src, seg, n)
kernel_name = 'mk_adaln_attn_ffn_d1_seqx_r2_4bba6c'

def setup_inputs(seed: int=0):
    np.random.seed(seed)
    _w = jnp.asarray

    def _rec_inputs():
        import jax
        import jax.numpy as jnp
        _rk = jax.random.key(seed)
        x = -0.0002928 + 1 * jax.random.normal(jax.random.fold_in(_rk, 1), (4, 1024, 512), jnp.float32)
        _lenS = 1024 - jax.random.randint(jax.random.fold_in(_rk, 7), (4,), 0, max(1, 1024 // 4) + 1, jnp.int32)
        _lenS2 = 1024 - jax.random.randint(jax.random.fold_in(_rk, 8), (4,), 0, max(1, 1024 // 4) + 1, jnp.int32)
        itok_Sx32_0_1023 = jax.random.randint(jax.random.fold_in(_rk, 12), (1024, 32), 0, 512, jnp.int32)
        condB_uprev = -0.456674 + 0.753242 * jax.random.normal(jax.random.fold_in(_rk, 14), (4,), jnp.float32)
        itok_B_0_8 = jax.random.randint(jax.random.fold_in(_rk, 15), (4,), 0, 9, jnp.int32)
        _validS = jnp.arange(1024)[None, :] < _lenS[:, None]
        _validS2 = jnp.arange(1024)[None, :] < _lenS2[:, None]
        _causal = jnp.tril(jnp.ones((1024, 1024), dtype=bool))
        mask_SxS_bk0 = jnp.logical_not(jnp.broadcast_to(_validS[0:1, :], (1024, 1024)))
        mask_Sx32_bk1 = jnp.ones((1024, 32), dtype=bool)
        return (x, itok_Sx32_0_1023, condB_uprev, itok_B_0_8, mask_SxS_bk0, mask_Sx32_bk1)
    x, itok_Sx32_0_1023, condB_uprev, itok_B_0_8, mask_SxS_bk0, mask_Sx32_bk1 = _rec_inputs()

    def _L0_cond_setup():
        import jax, jax.numpy as jnp
        import numpy as np
        B, S, D, H = (4, 512, 512, 16)
        DH = D // H
        K_SPARSE = 32
        LAMBDA_MAX, ALPHA = (10.0, 5.0)
        SPARSE_THRESHOLD = 1.0
        key = jax.random.key(seed)
        ks = jax.random.split(key, 12)
        x = jax.random.normal(ks[0], (B, S, D), dtype=jnp.float32)
        prior_mask = jax.random.bernoulli(ks[1], 0.1, (S, S))
        prior_indices = jax.random.randint(ks[2], (S, K_SPARSE), 0, S)
        prior_index_mask = jax.random.bernoulli(ks[3], 0.9, (S, K_SPARSE))
        prior_index_mask = prior_index_mask.at[:, 0].set(True)
        u_prev = jax.random.normal(ks[4], (B, 1), dtype=jnp.float32)
        sc = 1.0 / np.sqrt(D)
        Wq = jax.random.normal(ks[5], (D, D), dtype=jnp.float32) * sc
        Wk = jax.random.normal(ks[6], (D, D), dtype=jnp.float32) * sc
        Wv = jax.random.normal(ks[7], (D, D), dtype=jnp.float32) * sc
        Wo = jax.random.normal(ks[8], (D, D), dtype=jnp.float32) * sc
        bq = jnp.zeros((D,), jnp.float32)
        bk = jnp.zeros((D,), jnp.float32)
        bv = jnp.zeros((D,), jnp.float32)
        bo = jnp.zeros((D,), jnp.float32)
        return {'x': x, 'prior_mask': prior_mask, 'prior_indices': prior_indices, 'prior_index_mask': prior_index_mask, 'u_prev': u_prev, 'Wq': Wq, 'bq': bq, 'Wk': Wk, 'bk': bk, 'Wv': Wv, 'bv': bv, 'Wo': Wo, 'bo': bo}
    _L0_cond_all = _L0_cond_setup()
    _L0_cond_in = {k: v for k, v in _L0_cond_all.items() if k in ('Wq', 'bq', 'Wk', 'bk', 'Wv', 'bv', 'Wo', 'bo')}
    del _L0_cond_all

    def _L0_attn_setup():
        import jax, jax.numpy as jnp
        import numpy as np
        EMBED_DIM = 512
        NUM_HEADS = 16
        D_K = EMBED_DIM // NUM_HEADS
        MAX_LEN = 512
        BATCH = 4
        SEQ = 512
        key = jax.random.key(seed)
        ks = jax.random.split(key, 6)
        s = 1.0 / np.sqrt(EMBED_DIM)
        return {'x': jax.random.normal(ks[0], (BATCH, SEQ, EMBED_DIM), jnp.float32), 'Wq': jax.random.normal(ks[1], (EMBED_DIM, EMBED_DIM), jnp.float32) * s, 'bq': jnp.zeros((EMBED_DIM,), jnp.float32), 'Wk': jax.random.normal(ks[2], (EMBED_DIM, EMBED_DIM), jnp.float32) * s, 'bk': jnp.zeros((EMBED_DIM,), jnp.float32), 'Wv': jax.random.normal(ks[3], (EMBED_DIM, EMBED_DIM), jnp.float32) * s, 'bv': jnp.zeros((EMBED_DIM,), jnp.float32), 'Wo': jax.random.normal(ks[4], (EMBED_DIM, EMBED_DIM), jnp.float32) * s, 'bo': jnp.zeros((EMBED_DIM,), jnp.float32), 'rel_table': jax.random.normal(ks[5], (2 * MAX_LEN - 1, D_K), jnp.float32)}
    _L0_attn_all = _L0_attn_setup()
    _L0_attn_in = {k: v for k, v in _L0_attn_all.items() if k in ('Wq', 'bq', 'Wk', 'bk', 'Wv', 'bv', 'Wo', 'bo', 'rel_table')}
    del _L0_attn_all

    def _L0_cond2_setup():
        import jax, jax.numpy as jnp
        import numpy as np
        LN_EPS = 1e-05
        key = jax.random.key(seed)
        ks = jax.random.split(key, 8)
        B, S, H, A, L = (32, 1024, 512, 128, 10)
        return {'hidden_states': jax.random.normal(ks[0], (B, S, H), dtype=jnp.float32), 'language_ids': jax.random.randint(ks[1], (B,), 0, L, dtype=jnp.int64), 'W1': jax.random.normal(ks[2], (L, H, A), dtype=jnp.float32) * (1.0 / np.sqrt(H)), 'b1': jnp.zeros((L, A), dtype=jnp.float32), 'W2': jax.random.normal(ks[3], (L, A, H), dtype=jnp.float32) * (1.0 / np.sqrt(A)), 'b2': jnp.zeros((L, H), dtype=jnp.float32), 'gamma': jnp.ones((L, H), dtype=jnp.float32), 'beta': jnp.zeros((L, H), dtype=jnp.float32)}
    _L0_cond2_all = _L0_cond2_setup()
    _L0_cond2_in = {k: v for k, v in _L0_cond2_all.items() if k in ('W1', 'b1', 'W2', 'b2', 'gamma', 'beta')}
    del _L0_cond2_all

    def _L0_ffn_setup():
        import jax, jax.numpy as jnp
        import numpy as np
        D_MODEL = 512
        N_EXPERTS = 8
        TOP_K = 2
        B, S = (4, 1024)
        key = jax.random.key(seed)
        k_x, k_g, k_w = jax.random.split(key, 3)
        x = jax.random.normal(k_x, (B, S, D_MODEL), dtype=jnp.float32)
        gate_w = jax.random.normal(k_g, (N_EXPERTS, D_MODEL), dtype=jnp.float32) * (1.0 / np.sqrt(D_MODEL))
        bound = float(np.sqrt(6.0 / (D_MODEL + D_MODEL)))
        weight = jax.random.uniform(k_w, (N_EXPERTS, D_MODEL, D_MODEL), dtype=jnp.float32, minval=-bound, maxval=bound)
        return {'x': x, 'gate_w': gate_w, 'weight': weight}
    _L0_ffn_all = _L0_ffn_setup()
    _L0_ffn_in = {k: v for k, v in _L0_ffn_all.items() if k in ('gate_w', 'weight')}
    del _L0_ffn_all
    return {'x': x, 'itok_Sx32_0_1023': itok_Sx32_0_1023, 'condB_uprev': condB_uprev, 'itok_B_0_8': itok_B_0_8, 'mask_SxS_bk0': mask_SxS_bk0, 'mask_Sx32_bk1': mask_Sx32_bk1, 'L0_cond_Wq': _L0_cond_in['Wq'], 'L0_cond_bq': _L0_cond_in['bq'], 'L0_cond_Wk': _L0_cond_in['Wk'], 'L0_cond_bk': _L0_cond_in['bk'], 'L0_cond_Wv': _L0_cond_in['Wv'], 'L0_cond_bv': _L0_cond_in['bv'], 'L0_cond_Wo': _L0_cond_in['Wo'], 'L0_cond_bo': _L0_cond_in['bo'], 'L0_attn_Wq': _L0_attn_in['Wq'], 'L0_attn_bq': _L0_attn_in['bq'], 'L0_attn_Wk': _L0_attn_in['Wk'], 'L0_attn_bk': _L0_attn_in['bk'], 'L0_attn_Wv': _L0_attn_in['Wv'], 'L0_attn_bv': _L0_attn_in['bv'], 'L0_attn_Wo': _L0_attn_in['Wo'], 'L0_attn_bo': _L0_attn_in['bo'], 'L0_attn_rel_table': _L0_attn_in['rel_table'], 'L0_cond2_W1': _L0_cond2_in['W1'], 'L0_cond2_b1': _L0_cond2_in['b1'], 'L0_cond2_W2': _L0_cond2_in['W2'], 'L0_cond2_b2': _L0_cond2_in['b2'], 'L0_cond2_gamma': _L0_cond2_in['gamma'], 'L0_cond2_beta': _L0_cond2_in['beta'], 'L0_ffn_gate_w': _L0_ffn_in['gate_w'], 'L0_ffn_weight': _L0_ffn_in['weight']}

def reference(x, itok_Sx32_0_1023, condB_uprev, itok_B_0_8, mask_SxS_bk0, mask_Sx32_bk1, L0_cond_Wq, L0_cond_bq, L0_cond_Wk, L0_cond_bk, L0_cond_Wv, L0_cond_bv, L0_cond_Wo, L0_cond_bo, L0_attn_Wq, L0_attn_bq, L0_attn_Wk, L0_attn_bk, L0_attn_Wv, L0_attn_bv, L0_attn_Wo, L0_attn_bo, L0_attn_rel_table, L0_cond2_W1, L0_cond2_b1, L0_cond2_W2, L0_cond2_b2, L0_cond2_gamma, L0_cond2_beta, L0_ffn_gate_w, L0_ffn_weight):
    import jax
    import jax.numpy as jnp

    def _L0_cond_ref(x, prior_mask, prior_indices, prior_index_mask, u_prev, Wq, bq, Wk, bk, Wv, bv, Wo, bo):
        import jax, jax.numpy as jnp
        import numpy as np
        B, S, D, H = (4, 512, 512, 16)
        DH = D // H
        K_SPARSE = 32
        LAMBDA_MAX, ALPHA = (10.0, 5.0)
        SPARSE_THRESHOLD = 1.0
        Bb, Ss, Dd = x.shape
        scale = 1.0 / jnp.sqrt(jnp.asarray(DH, x.dtype))

        def proj(W, b):
            return (x @ W.T + b).reshape(Bb, Ss, H, DH).transpose(0, 2, 1, 3)
        Q, K, V = (proj(Wq, bq), proj(Wk, bk), proj(Wv, bv))
        lam = LAMBDA_MAX * jnp.exp(-ALPHA * u_prev.reshape(Bb))
        use_sparse = lam >= SPARSE_THRESHOLD
        scores = jnp.einsum('bhqd,bhkd->bhqk', Q, K) * scale
        prior_bias = jnp.where(prior_mask[:Ss, :Ss], 0.0, -1.0).astype(x.dtype)
        bias = lam[:, None, None, None] * prior_bias[None, None]
        dense_out = jnp.einsum('bhqk,bhkd->bhqd', jax.nn.softmax(scores + bias, axis=-1), V)
        idx = prior_indices[:Ss]
        Kg = K[:, :, idx]
        Vg = V[:, :, idx]
        s_scores = jnp.einsum('bhsd,bhskd->bhsk', Q, Kg) * scale
        s_scores = jnp.where(prior_index_mask[:Ss][None, None], s_scores, jnp.asarray(-jnp.inf, x.dtype))
        sparse_out = jnp.einsum('bhsk,bhskd->bhsd', jax.nn.softmax(s_scores, axis=-1), Vg)
        out = jnp.where(use_sparse[:, None, None, None], sparse_out, dense_out)
        out = out.transpose(0, 2, 1, 3).reshape(Bb, Ss, Dd)
        return out @ Wo.T + bo

    def _L0_attn_ref(x, Wq, bq, Wk, bk, Wv, bv, Wo, bo, rel_table):
        import jax, jax.numpy as jnp
        import numpy as np
        EMBED_DIM = 512
        NUM_HEADS = 16
        D_K = EMBED_DIM // NUM_HEADS
        MAX_LEN = 512
        BATCH = 4
        SEQ = 512
        b, n, e = x.shape
        h, d = (NUM_HEADS, D_K)

        def proj(W, bias):
            y = jnp.einsum('bne,fe->bnf', x, W) + bias
            return y.reshape(b, n, h, d).transpose(0, 2, 1, 3)
        Q = proj(Wq, bq)
        K = proj(Wk, bk)
        V = proj(Wv, bv)
        scores_content = jnp.einsum('bhid,bhjd->bhij', Q, K)
        pos = jnp.arange(n)
        rel_pos = jnp.clip(pos[:, None] - pos[None, :] + MAX_LEN - 1, 0, 2 * MAX_LEN - 2)
        rel_emb = rel_table[rel_pos]
        scores_pos = jnp.einsum('bhid,ijd->bhij', Q, rel_emb)
        scores = (scores_content + scores_pos) / np.sqrt(d).astype(np.float32)
        attn = jax.nn.softmax(scores, axis=-1)
        out = jnp.einsum('bhij,bhjd->bhid', attn, V)
        out = out.transpose(0, 2, 1, 3).reshape(b, n, e)
        return jnp.einsum('bne,fe->bnf', out, Wo) + bo

    def _L0_cond2_ref(hidden_states, language_ids, W1, b1, W2, b2, gamma, beta):
        import jax, jax.numpy as jnp
        import numpy as np
        LN_EPS = 1e-05
        w1 = W1[language_ids]
        w2 = W2[language_ids]
        h = jnp.einsum('bsh,bha->bsa', hidden_states, w1) + b1[language_ids][:, None, :]
        h = jax.nn.relu(h)
        adapted = jnp.einsum('bsa,bah->bsh', h, w2) + b2[language_ids][:, None, :]
        x = hidden_states + adapted
        mean = jnp.mean(x, axis=-1, keepdims=True)
        var = jnp.mean(jnp.square(x - mean), axis=-1, keepdims=True)
        normed = (x - mean) * jax.lax.rsqrt(var + LN_EPS)
        return normed * gamma[language_ids][:, None, :] + beta[language_ids][:, None, :]

    def _L0_ffn_ref(x, gate_w, weight):
        import jax, jax.numpy as jnp
        import numpy as np
        D_MODEL = 512
        N_EXPERTS = 8
        TOP_K = 2
        B, S = (4, 1024)
        logits = jnp.einsum('bsd,ed->bse', x, gate_w)
        topk_vals, topk_idx = jax.lax.top_k(logits, TOP_K)
        topk_weights = jax.nn.softmax(topk_vals, axis=-1)
        one_hot = jax.nn.one_hot(topk_idx, N_EXPERTS, dtype=x.dtype)
        weights_full = jnp.einsum('bsk,bske->bse', topk_weights, one_hot)
        expert_out = jnp.einsum('bsd,edh->bseh', x, weight)
        out = jnp.einsum('bse,bseh->bsh', weights_full, expert_out)
        return out
    x = x + _L0_attn_ref(_L0_cond_ref(x, mask_SxS_bk0, itok_Sx32_0_1023, mask_Sx32_bk1, condB_uprev[:, None], L0_cond_Wq, L0_cond_bq, L0_cond_Wk, L0_cond_bk, L0_cond_Wv, L0_cond_bv, L0_cond_Wo, L0_cond_bo), L0_attn_Wq, L0_attn_bq, L0_attn_Wk, L0_attn_bk, L0_attn_Wv, L0_attn_bv, L0_attn_Wo, L0_attn_bo, L0_attn_rel_table)
    x = x + _L0_ffn_ref(_L0_cond2_ref(x, itok_B_0_8, L0_cond2_W1, L0_cond2_b1, L0_cond2_W2, L0_cond2_b2, L0_cond2_gamma, L0_cond2_beta), L0_ffn_gate_w, L0_ffn_weight)
    return x

_drawn_inputs = setup_inputs


def setup_inputs(seed=0):
    import zlib

    import numpy as np

    out = dict(_drawn_inputs(seed))
    spreads = {'L0_cond_bq': (0.0, 0.1),
     'L0_cond_bk': (0.0, 0.8),
     'L0_cond_bv': (0.0, 0.1),
     'L0_cond_bo': (0.0, 0.1),
     'L0_attn_bq': (0.0, 0.8),
     'L0_attn_bk': (0.0, 0.8),
     'L0_attn_bv': (0.0, 0.1),
     'L0_attn_bo': (0.0, 0.1),
     'L0_cond2_b1': (0.0, 0.1),
     'L0_cond2_b2': (0.0, 0.1),
     'L0_cond2_gamma': (1.0, 0.2),
     'L0_cond2_beta': (0.0, 0.1)}
    factors = {'L0_attn_Wq': 2.894, 'L0_attn_Wk': 3.531, 'L0_attn_rel_table': 5.639}
    for name, (base, spread) in spreads.items():
        noise = np.random.default_rng([zlib.crc32(name.encode()), seed]).standard_normal(out[name].shape)
        drawn = base * np.exp(spread * noise) if base else spread * noise
        out[name] = jnp.asarray(drawn.astype(out[name].dtype))
    for name, factor in factors.items():
        out[name] = (out[name] * factor).astype(out[name].dtype)
    return out
```

```python
from contextlib import ExitStack

import concourse.bass as bass
from concourse import mybir

F32 = mybir.dt.float32
F32R = mybir.dt.float32r
I32 = mybir.dt.int32
U8 = mybir.dt.uint8
U32 = mybir.dt.uint32
ALU = mybir.AluOpType
ACT = mybir.ActivationFunctionType

P = 128
B, S, D = 4, 1024, 512
H, DH = 16, 32
HG = P // DH
NG = H // HG
KT = D // P
CH = 512
NQ = S // P
NI = B * NG
SCALE = float(DH) ** -0.5
NSPARSE = 32
LAM_MAX, ALPHA, THRESHOLD = 10.0, 5.0, 1.0
MAXLEN = 512
NREL = 2 * MAXLEN - 1
RELW = 2 * S
UW = S + P
UC = UW // 3
NE, TOPK = 8, 2
LANGS, AD = 10, 128
LN_EPS = 1e-5
MASKED = -1e30


class Memory:

    def __init__(self, nc, ctx, tag):
        self.nc, self.ctx, self.tag = nc, ctx, tag

    def sb(self, name, shape, dt=F32):
        return self.ctx.enter_context(self.nc.sbuf_tensor(f"{self.tag}_{name}", shape, dt))

    def ps(self, name, shape, dt=F32):
        return self.ctx.enter_context(self.nc.psum_tensor(f"{self.tag}_{name}", shape, dt))

    def sem(self, name):
        return self.ctx.enter_context(self.nc.semaphore(f"{self.tag}_{name}"))


def prior_block(nc, io, bias_d):
    with ExitStack() as ctx:
        m = Memory(nc, ctx, "pr")
        iota1 = m.sb("iota1", [P, S])
        named_i = m.sb("named_i", [P, NQ, NSPARSE], I32)
        valid_u = m.sb("valid_u", [P, NQ, NSPARSE], U8)
        named_f = m.sb("named_f", [P, NQ, NSPARSE])
        valid_f = m.sb("valid_f", [P, NQ, NSPARSE])
        key1 = m.sb("key1", [P, NQ, NSPARSE])
        mask_w = m.sb("mask_w", [P, NQ, S // 4], I32)
        mask_u = mask_w[:, :, :].bitcast(U8)
        up = m.sb("up", [P, B])
        lam = m.sb("lam", [P, B])
        sparse = m.sb("sparse", [P, B])
        dense_lam = m.sb("dense_lam", [P, B])
        lam1 = m.sb("lam1", [P, B])
        is_dense = m.sb("is_dense", [P, B])
        count = m.sb("count", [P, 2, 2, S])
        floor = m.sb("floor", [P, 2, S])
        lnc = m.sb("lnc", [P, 2, S])
        pen = m.sb("pen", [P, 2, S])
        off = m.sb("off", [P, S])
        dense_part = m.sb("dense_part", [P, S])
        bias = m.sb("bias", [P, B, S])
        loaded, lam_exp, chain = m.sem("loaded"), m.sem("lam_exp"), m.sem("chain")
        floor_ready, ln_ready, bias_ready = m.sem("floor_ready"), m.sem("ln_ready"), m.sem("bias_ready")
        stored = [m.sem(f"stored{b}") for b in range(B)]
        with nc.Block() as block:

            @block.sync
            def _(sp):
                for dst, src in (
                    (iota1[:, :], io["iota1"]),
                    (named_i[:, :, :], io["prior_idx"].rearrange("(t p) j -> p t j", p=P)),
                    (valid_u[:, :, :], io["prior_valid"].rearrange("(t p) j -> p t j", p=P)),
                    (mask_w[:, :, :], io["prior_mask"].rearrange("(t p) k -> p t k", p=P)),
                    (up[:, :], io["uprev"]),
                ):
                    sp.dma_start(dst, src).then_inc(loaded, 16)
                for t in range(NQ):
                    for b in range(B):
                        sp.wait_ge(bias_ready, t * B + b + 1)
                        sp.dma_start(bias_d[b, t * P:(t + 1) * P, :], bias[:, b, :]).then_inc(stored[b], 16)
                for b in range(B):
                    sp.wait_ge(stored[b], 16 * NQ)

            @block.scalar
            def _(act):
                act.wait_ge(loaded, 80)
                act.activation(lam[:, :], up[:, :], ACT.Exp, scale=-ALPHA).then_inc(lam_exp, 1)
                for t in range(NQ):
                    act.wait_ge(floor_ready, t + 1)
                    act.activation(lnc[:, t % 2, :], floor[:, t % 2, :], ACT.Ln).then_inc(ln_ready, 1)

            @block.vector
            def _(dve):
                done = [0]

                def then(ins):
                    done[0] += 1
                    ins.then_inc(chain, 1)
                    dve.wait_ge(chain, done[0])

                dve.wait_ge(loaded, 80)
                dve.tensor_copy(named_f[:, :, :], named_i[:, :, :])
                then(dve.tensor_copy(valid_f[:, :, :], valid_u[:, :, :]))
                then(dve.scalar_tensor_tensor(out=key1[:, :, :], in0=named_f[:, :, :], scalar=1.0,
                                              in1=valid_f[:, :, :], op0=ALU.add, op1=ALU.mult))
                dve.wait_ge(lam_exp, 1)
                then(dve.tensor_scalar(lam1[:, :], lam[:, :], LAM_MAX, None, ALU.mult))
                dve.tensor_scalar(sparse[:, :], lam1[:, :], THRESHOLD, None, ALU.is_ge)
                then(dve.tensor_scalar(is_dense[:, :], lam1[:, :], THRESHOLD, None, ALU.is_lt))
                then(dve.scalar_tensor_tensor(out=dense_lam[:, :], in0=lam1[:, :], scalar=THRESHOLD,
                                              in1=is_dense[:, :], op0=ALU.min, op1=ALU.mult))
                for t in range(NQ):
                    w = t % 2
                    then(dve.tensor_scalar(count[:, w, 0, :], iota1[:, :], key1[:, t, 0:1], None, ALU.is_equal))
                    for j in range(1, NSPARSE):
                        then(dve.scalar_tensor_tensor(out=count[:, w, j % 2, :], in0=iota1[:, :],
                                                      scalar=key1[:, t, j:j + 1],
                                                      in1=count[:, w, (j + 1) % 2, :],
                                                      op0=ALU.is_equal, op1=ALU.add))
                    total = count[:, w, (NSPARSE - 1) % 2, :]
                    dve.tensor_scalar(floor[:, w, :], total, 0.5, None, ALU.max).then_inc(floor_ready, 1)
                    dve.tensor_scalar(pen[:, w, :], total, 0.5, MASKED, ALU.is_lt, ALU.mult)
                    then(dve.tensor_scalar(off[:, :], mask_u[:, t, :], 1.0, 1.0 / SCALE,
                                           ALU.subtract, ALU.mult))
                    dve.wait_ge(ln_ready, t + 1)
                    then(dve.scalar_tensor_tensor(out=lnc[:, w, :], in0=lnc[:, w, :], scalar=1.0 / SCALE,
                                                  in1=pen[:, w, :], op0=ALU.mult, op1=ALU.add))
                    for b in range(B):
                        then(dve.tensor_scalar(dense_part[:, :], off[:, :], dense_lam[:, b:b + 1], None,
                                               ALU.mult))
                        dve.wait_ge(stored[b], 16 * t)
                        dve.scalar_tensor_tensor(out=bias[:, b, :], in0=lnc[:, w, :],
                                                 scalar=sparse[:, b:b + 1], in1=dense_part[:, :],
                                                 op0=ALU.mult, op1=ALU.add).then_inc(bias_ready, 1)
                        dve.wait_ge(bias_ready, t * B + b + 1)


def projection_block(nc, io, tag, source, weights, biases, out, q_d, k_d, v_d):
    wq_d, wk_d, wv_d = weights
    stages = (["o"] if out else []) + ["q", "k", "v"]
    with ExitStack() as ctx:
        m = Memory(nc, ctx, tag)
        w_in = [m.sb(f"w_in{i}", [P, KT, D]) for i in range(2)]
        w_hi = {n: m.sb(f"w{n}_hi", [P, KT, D], F32R) for n in stages}
        w_lo = {n: m.sb(f"w{n}_lo", [P, KT, D], F32R) for n in stages}
        cols = m.sb("cols", [P, 4, KT])
        x_in = [m.sb(f"x_in{s}", [P, KT, CH]) for s in range(2)]
        x_hi = [m.sb(f"x_hi{s}", [P, KT, CH], F32R) for s in range(2)]
        x_lo = [m.sb(f"x_lo{s}", [P, KT, CH], F32R) for s in range(2)]
        c_hi = m.sb("c_hi", [P, KT, CH], F32R)
        c_lo = m.sb("c_lo", [P, KT, CH], F32R)
        NST = 4
        st_hi = [m.sb(f"st_hi{i}", [P, CH], F32R) for i in range(NST)]
        st_lo = [m.sb(f"st_lo{i}", [P, CH], F32R) for i in range(NST)]
        st_v = [m.sb(f"st_v{i}", [P, CH]) for i in range(NST)]
        NBANK = 4
        bank = [m.ps(f"bank{i}", [P, CH]) for i in range(NBANK)]
        w_loaded = [m.sem(f"w_loaded{i}") for i in range(2)]
        w_hi_done, w_lo_done, cols_loaded = m.sem("w_hi_done"), m.sem("w_lo_done"), m.sem("cols_loaded")
        x_loaded = [m.sem(f"x_loaded{s}") for s in range(2)]
        x_hi_done = m.sem("x_hi_done")
        x_lo_done = [m.sem(f"x_lo_done{s}") for s in range(2)]
        chunk_done = [m.sem(f"chunk_done{s}") for s in range(2)]
        group_done, hi_done, bank_free = m.sem("group_done"), m.sem("hi_done"), m.sem("bank_free")
        stored = [m.sem(f"stored{i}") for i in range(NST)]
        passed = m.sem("passed")

        groups = [(n, j) for n in stages for j in range(4)]
        body = [(s, n, j) for s in range(2) for n, j in groups]
        GT = len(body)
        exported = [g for g, (_, n, _) in enumerate(body) if n != "o"]
        with_hi = [g for g, (_, n, _) in enumerate(body) if n != "v"]
        NEX, NHI = len(exported), len(with_hi)
        w_d = {"o": out[0] if out else None, "q": wq_d, "k": wk_d, "v": wv_d}
        bias_col = {"o": 1, "q": 2, "k": 3}

        with nc.Block() as block:

            @block.gpsimd
            def _(pool):
                with pool.Fori(0, B) as b:
                    for s in range(2):
                        pool.wait_ge(x_lo_done[s], b)
                        pool.sem_inc(passed)
                        pool.dma_start(x_in[s][:, :, :], source(b, s)).then_inc(x_loaded[s], 16)

            @block.sync
            def _(sp):
                for n, src in enumerate(biases):
                    sp.dma_start(cols[:, n, :], src).then_inc(cols_loaded, 16)
                for n, name in enumerate(stages):
                    sp.wait_ge(w_lo_done, max(0, n - 1))
                    sp.dma_start(w_in[n % 2][:, :, :], w_d[name].rearrange("(k p) n -> p k n", p=P))\
                        .then_inc(w_loaded[n % 2], 16)
                with sp.Fori(0, B) as b:
                    for e, g in enumerate(exported):
                        s, name, j = body[g]
                        i = e % NST
                        sp.wait_ge(bank_free, b * GT + (NBANK + g + 1))
                        sp.sem_inc(passed)
                        if name == "v":
                            rows = slice(s * CH + j * P, s * CH + (j + 1) * P)
                            for a in range(2):
                                sp.dma_start(v_d[bass.ds(b * NG + 2 * a, 2), rows, :].rearrange("g p c -> p g c"),
                                             st_v[i][:, 2 * a * P:2 * (a + 1) * P].rearrange("p (g c) -> p g c", g=2))\
                                    .then_inc(stored[i], 16)
                        else:
                            d = q_d if name == "q" else k_d
                            for a, st in enumerate((st_hi, st_lo)):
                                sp.dma_start(d[a, b * NG + j, :, s * CH:(s + 1) * CH],
                                             st[i][:, :].bitcast(F32)).then_inc(stored[i], 16)
                for i in range(NST):
                    sp.wait_ge(stored[i], 32 * B * NEX // NST)

            @block.scalar
            def _(act):
                for n, name in enumerate(stages):
                    act.wait_ge(w_loaded[n % 2], 16 * (n // 2 + 1))
                    act.activation(w_hi[name][:, :, :], w_in[n % 2][:, :, :], ACT.Identity)\
                        .then_inc(w_hi_done, 1)
                act.wait_ge(cols_loaded, 16 * len(biases))

                def split(b, s):
                    act.wait_ge(x_loaded[s], b * 16 + 16)
                    act.wait_ge(chunk_done[s], b)
                    for k in range(KT):
                        act.activation(x_hi[s][:, k, :], x_in[s][:, k, :], ACT.Identity,
                                       bias=cols[:, 0, k:k + 1]).then_inc(x_hi_done, 1)

                with act.Fori(0, B) as b:
                    split(b, 0)
                    for g, (s, name, j) in enumerate(body):
                        if g == GT // 4:
                            split(b, 1)
                        if name == "v":
                            continue
                        if name != "o":
                            e = exported.index(g)
                            act.wait_ge(stored[e % NST], b * (32 * NEX // NST) + 32 * (e // NST))
                            dst = st_hi[e % NST][:, :]
                        else:
                            dst = c_hi[:, j, :]
                        act.wait_ge(group_done, b * GT + (g + 1))
                        act.activation(dst, bank[g % NBANK][:, :], ACT.Identity,
                                       bias=cols[:, bias_col[name], j:j + 1]).then_inc(hi_done, 1)

            @block.vector
            def _(dve):
                for n, name in enumerate(stages):
                    dve.wait_ge(w_hi_done, n + 1)
                    dve.tensor_tensor(w_lo[name][:, :, :], w_in[n % 2][:, :, :],
                                      w_hi[name][:, :, :].bitcast(F32), ALU.subtract).then_inc(w_lo_done, 1)
                dve.wait_ge(cols_loaded, 16 * len(biases))
                dve.sem_inc(bank_free, NBANK)

                def split(b, s):
                    dve.wait_ge(x_hi_done, b * (2 * KT) + (s + 1) * KT)
                    for k in range(KT):
                        ins = dve.scalar_tensor_tensor(out=x_lo[s][:, k, :], in0=x_in[s][:, k, :],
                                                       scalar=cols[:, 0, k:k + 1],
                                                       in1=x_hi[s][:, k, :].bitcast(F32),
                                                       op0=ALU.add, op1=ALU.subtract)
                    ins.then_inc(x_lo_done[s], 1)

                with dve.Fori(0, B) as b:
                    split(b, 0)
                    for g, (s, name, j) in enumerate(body):
                        if g == GT // 4:
                            split(b, 1)
                        src = bank[g % NBANK][:, :]
                        if name == "v":
                            e = exported.index(g)
                            dve.wait_ge(stored[e % NST], b * (32 * NEX // NST) + 32 * (e // NST))
                            dve.wait_ge(group_done, b * GT + (g + 1))
                            dve.tensor_copy(st_v[e % NST][:, :], src).then_inc(bank_free, 1)
                            continue
                        if name == "o":
                            hi, lo = c_hi[:, j, :], c_lo[:, j, :]
                        else:
                            e = exported.index(g)
                            hi, lo = st_hi[e % NST][:, :], st_lo[e % NST][:, :]
                        dve.wait_ge(hi_done, b * NHI + (with_hi.index(g) + 1))
                        dve.scalar_tensor_tensor(out=lo, in0=src, scalar=cols[:, bias_col[name], j:j + 1],
                                                 in1=hi.bitcast(F32), op0=ALU.add, op1=ALU.subtract)\
                            .then_inc(bank_free, 1)

            @block.tensor
            def _(pe):
                pe.wait_ge(w_lo_done, len(stages))
                with pe.Fori(0, B) as b:
                    for g, (s, name, j) in enumerate(body):
                        if g % len(groups) == 0:
                            pe.wait_ge(x_lo_done[s], b + 1)
                        if out and g % len(groups) == 4:
                            pe.wait_ge(bank_free, b * GT + (NBANK + g))
                        pe.wait_ge(bank_free, b * GT + (g + 1))
                        a_hi, a_lo = (c_hi, c_lo) if out and name != "o" else (x_hi[s], x_lo[s])
                        tile = slice(j * P, (j + 1) * P)
                        last = None
                        for k in range(KT):
                            for wa, xa in ((w_hi, a_hi), (w_hi, a_lo), (w_lo, a_hi)):
                                if name == "v":
                                    lhs, rhs = xa[:, k, tile], wa[name][:, k, :]
                                else:
                                    lhs, rhs = wa[name][:, k, tile], xa[:, k, :]
                                first = last is None
                                last = pe.matmul(bank[g % NBANK][:, :], lhs, rhs, start=first,
                                                 stop=(k == KT - 1 and wa is w_lo))
                        last.then_inc(group_done, 1)
                        if g % len(groups) == len(groups) - 1:
                            pe.drain().then_inc(chunk_done[s], 1)


def attention_block(nc, io, tag, q_d, k_d, v_d, o_d, bias_d=None, skew_d=None):
    rel = skew_d is not None
    NT = 2 * NQ
    NU = NT * HG
    NIT = NI // 2
    LAG = 2
    NPT = 2 if rel else 3
    NP = 3
    NADD = 4 if rel else 2
    ULAG = 5
    NSK = skew_d.shape[0] if rel else 0
    with ExitStack() as ctx:
        m = Memory(nc, ctx, tag)
        q4 = [m.sb(f"q4_{s}", [P, HG, S], F32R) for s in range(2)]
        k4 = [m.sb(f"k4_{s}", [P, HG, S], F32R) for s in range(2)]
        v = [m.sb(f"v{s}", [P, NQ, P]) for s in range(2)]
        added = [m.sb(f"added{i}", [P, S]) for i in range(NADD)]
        prob = [m.sb(f"prob{i}", [P, S]) for i in range(NP)]
        probT = [m.sb(f"probT{i}", [P, HG, NQ, P]) for i in range(2)]
        o_sb = [m.sb(f"o_sb{s}", [P, S]) for s in range(2)]
        ident = m.sb("ident", [P, P])
        negmax = m.sb("negmax", [P, 4])
        den = m.sb("den", [P, 2, HG])
        rden = m.sb("rden", [P, 2, HG])
        rden_wide = m.sb("rden_wide", [P, 2, HG, DH])
        rT = m.sb("rT", [P, P])
        scores = [m.ps(f"scores{i}", [P, S]) for i in range(2)]
        pT = [m.ps(f"pT{i}", [P, 4, P]) for i in range(NPT)]
        oT = m.ps("oT", [P, 512])
        if rel:
            r_in = m.sb("r_in", [P, RELW])
            r_hi = m.sb("r_hi", [P, RELW], F32R)
            r4 = m.sb("r4", [P, RELW], F32R)
            u_sb = [m.sb(f"u_sb{i}", [P, UW]) for i in range(2)]
            u_ps = m.ps("u_ps", [P, 512])
            r_hi_done, r4_done, u_ready = m.sem("r_hi_done"), m.sem("r4_done"), m.sem("u_ready")
            u_left = m.sem("u_left")
            u_stored = [m.sem(f"u_stored{i}") for i in range(2)]
        passed = m.sem("passed")
        consts = m.sem("consts")
        in_loaded = [m.sem(f"in_loaded{s}") for s in range(2)]
        slot_done = [m.sem(f"slot_done{s}") for s in range(2)]
        add_loaded = [m.sem(f"add_loaded{i}") for i in range(NADD)]
        scores_ready, added_done, probs_ready = m.sem("scores_ready"), m.sem("added_done"), m.sem("probs_ready")
        pT_ready, left_dve, left_act = m.sem("pT_ready"), m.sem("left_dve"), m.sem("left_act")
        rden_done, rden_ready, o_ready = m.sem("rden_done"), m.sem("rden_ready"), m.sem("o_ready")
        rT_ready, o_done = m.sem("rT_ready"), m.sem("o_done")
        o_stored = [m.sem(f"o_stored{s}") for s in range(2)]
        NC = 5 if rel else 1

        def parts(u):
            return u // (NU // 2), u // HG % NQ, u % HG, u // HG

        with nc.Block() as block:

            @block.gpsimd
            def _(pool):
                def load_inputs(s, i):
                    for dst, src, half in ((q4[s], q_d, (0, 0, 1, 1)), (k4[s], k_d, (0, 1, 0, 1))):
                        for g in range(4):
                            pool.dma_start(dst[g * DH:(g + 1) * DH, :, :].bitcast(F32),
                                           src[half[g], i, :, :].rearrange("(h d) n -> d h n", h=HG))\
                                .then_inc(in_loaded[s], 16)
                    pool.dma_start(v[s][:, :, :], v_d[i, :, :].rearrange("(t p) c -> p t c", p=P))\
                        .then_inc(in_loaded[s], 16)

                load_inputs(0, 0)
                with pool.Fori(0, NIT) as it:
                    pool.wait_ge(slot_done[1], it)
                    pool.sem_inc(passed)
                    load_inputs(1, it * 2 + 1)
                    for w in range(NU):
                        if w == NU * 5 // 8:
                            pool.wait_ge(slot_done[0], it + 1)
                            pool.sem_inc(passed)
                            load_inputs(0, (it * 2 + 2) % NI)
                        if rel:
                            pool.wait_ge(u_left, it * (3 * NU) + 3 * (w + 1))
                            pool.sem_inc(passed)
                            if w >= NSK:
                                pool.wait_ge(add_loaded[w % NADD],
                                             it * (16 * NU // NADD) + 16 * ((w - NSK) // NADD + 1))
                                pool.sem_inc(passed)
                            pool.dma_start(skew_d[w % NSK, :].rearrange("(p c) -> p c", p=P), u_sb[w % 2][:, :])\
                                .then_inc(u_stored[w % 2], 16)
                pool.wait_ge(in_loaded[0], 16 * 9 * (NIT + 1))

            @block.sync
            def _(sp):
                sp.dma_start(ident[:, :], io["ident"]).then_inc(consts, 16)
                if rel:
                    for g in range(4):
                        sp.dma_start(r_in[g * DH:(g + 1) * DH, :], io["relT"]).then_inc(consts, 16)
                with sp.Fori(0, NIT) as it:
                    for u in range(NU):
                        s, t, h, tt = parts(u)
                        if rel:
                            if u >= NADD:
                                sp.wait_ge(added_done, it * NU + (u - NADD + 1))
                                sp.sem_inc(passed)
                            sp.wait_ge(u_stored[u % 2], it * (8 * NU) + 16 * (u // 2 + 1))
                            sp.sem_inc(passed)
                            sp.dma_start(added[u % NADD][:, :],
                                         bass.AP(skew_d.tensor, (u % NSK) * P * UW + P - 1,
                                                 [[UW - 1, P], [1, S]]))\
                                .then_inc(add_loaded[u % NADD], 16)
                        elif h == 0:
                            sp.wait_ge(added_done, it * NU + (HG * (tt - 1) if tt >= 2 else 0))
                            sp.sem_inc(passed)
                            sp.dma_start(added[tt % 2][:, :], bias_d[it // 2, t * P:(t + 1) * P, :])\
                                .then_inc(add_loaded[tt % 2], 16)
                        if (t, h) == (2, 3) and s == 1:
                            sp.wait_ge(o_done, it * NT + NQ)
                            sp.sem_inc(passed)
                            sp.dma_start(o_d[it * 2, :, :], o_sb[0][:, :]).then_inc(o_stored[0], 16)
                    sp.wait_ge(o_done, it * NT + NT)
                    sp.sem_inc(passed)
                    sp.dma_start(o_d[it * 2 + 1, :, :], o_sb[1][:, :]).then_inc(o_stored[1], 16)
                for s in range(2):
                    sp.wait_ge(o_stored[s], 16 * NIT)

            @block.scalar
            def _(act):
                act.wait_ge(consts, 16 * NC)
                if rel:
                    act.activation(r_hi[:, :], r_in[:, :], ACT.Identity).then_inc(r_hi_done, 1)

                def positions(it, w):
                    for c in range(3):
                        if c == 0:
                            act.wait_ge(u_stored[w % 2], it * (8 * NU) + 16 * (w // 2))
                        act.wait_ge(u_ready, it * (3 * NU) + (3 * w + c + 1))
                        act.activation(u_sb[w % 2][:, c * UC:(c + 1) * UC], u_ps[:, 0:UC], ACT.Copy)\
                            .then_inc(u_left, 1)

                with act.Fori(0, NIT) as it:
                    if rel:
                        for w in range(ULAG):
                            positions(it, w)
                    for step in range(NU + 3):
                        u, x = step, step - LAG
                        if u < NU:
                            s, t, h, tt = parts(u)
                            if u >= NP:
                                act.wait_ge(pT_ready, it * (2 * NU) + 2 * (u - NP + 1))
                            act.wait_ge(added_done, it * NU + (u + 1))
                            act.activation(prob[u % NP][:, :], scores[u % 2][:, :], ACT.Exp,
                                           bias=negmax[:, u % 4:u % 4 + 1], scale=-1.0,
                                           accum_out=den[:, tt % 2, h:h + 1]).then_inc(probs_ready, 1)
                        if rel and u + ULAG < NU:
                            positions(it, u + ULAG)
                        if 0 <= x < NU:
                            s, t, h, tt = parts(x)
                            if tt >= 2 and h == 0:
                                act.wait_ge(o_ready, it * NT + (tt - 1))
                            act.wait_ge(pT_ready, it * (2 * NU) + (2 * x + 2))
                            act.activation(probT[tt % 2][:, h, 4:8, :], pT[(2 * x + 1) % NPT][:, :, :],
                                           ACT.Copy).then_inc(left_act, 1)
                        if x >= 5 and x % 4 == 1 or step == NU + 2:
                            tt = x // 4 - 1 if step < NU + 2 else NT - 1
                            act.wait_ge(o_ready, it * NT + (tt + 1))
                            act.activation(rT[:, :], oT[:, 256:384], ACT.Copy).then_inc(rT_ready, 1)

            @block.vector
            def _(dve):
                dve.wait_ge(consts, 16 * NC)
                if rel:
                    dve.wait_ge(r_hi_done, 1)
                    for g in range(4):
                        rows = slice(g * DH, (g + 1) * DH)
                        if g % 2 == 0:
                            dve.tensor_copy(r4[rows, :], r_hi[rows, :].bitcast(F32)).then_inc(r4_done, 1)
                        else:
                            dve.tensor_tensor(r4[rows, :], r_in[rows, :], r_hi[rows, :].bitcast(F32),
                                              ALU.subtract).then_inc(r4_done, 1)

                def normalise(it, tt):
                    s, t = tt // NQ, tt % NQ
                    if t == 0:
                        dve.wait_ge(o_stored[s], it * 16)
                    dve.wait_ge(rT_ready, it * NT + (tt + 1))
                    dve.tensor_tensor(o_sb[s][:, t * P:(t + 1) * P], oT[:, 0:P], rT[:, :], ALU.mult)\
                        .then_inc(o_done, 1)

                with dve.Fori(0, NIT) as it:
                    for step in range(NU + 3):
                        u, x = step, step - LAG
                        if u < NU:
                            s, t, h, tt = parts(u)
                            if rel:
                                dve.wait_ge(add_loaded[u % NADD], it * (16 * NU // NADD) + 16 * (u // NADD + 1))
                            elif h == 0:
                                dve.wait_ge(add_loaded[tt % 2], it * (16 * NQ) + 16 * (tt // 2 + 1))
                            dve.wait_ge(scores_ready, it * NU + (u + 1))
                            dve.sem_inc(passed)
                            dve.tensor_tensor_reduce(out=scores[u % 2][:, :], in0=scores[u % 2][:, :],
                                                     in1=added[(u if rel else tt) % NADD][:, :],
                                                     scale=-SCALE, scalar=3e38, op0=ALU.add, op1=ALU.min,
                                                     accum_out=negmax[:, u % 4:u % 4 + 1])\
                                .then_inc(added_done, 1)
                        if 0 <= x < NU:
                            s, t, h, tt = parts(x)
                            if tt >= 2 and h == 0:
                                dve.wait_ge(o_ready, it * NT + (tt - 1))
                            dve.wait_ge(pT_ready, it * (2 * NU) + (2 * x + 1))
                            dve.tensor_copy(probT[tt % 2][:, h, 0:4, :], pT[(2 * x) % NPT][:, :, :])\
                                .then_inc(left_dve, 1)
                            if h == HG - 1:
                                dve.wait_ge(probs_ready, it * NU + (x + 1))
                                dve.reciprocal(rden[:, tt % 2, :], den[:, tt % 2, :]).then_inc(rden_done, 1)
                                dve.wait_ge(rden_done, it * NT + (tt + 1))
                                dve.tensor_copy(rden_wide[:, tt % 2, :, :],
                                                rden[:, tt % 2, :].rearrange("p (h a) -> p h a", a=1)
                                                .to_broadcast([P, HG, DH])).then_inc(rden_ready, 1)
                        if x >= 5 and x % 4 == 1:
                            normalise(it, x // 4 - 1)
                    normalise(it, NT - 1)

            @block.tensor
            def _(pe):
                pe.wait_ge(consts, 16 * NC)
                if rel:
                    pe.wait_ge(r4_done, 4)

                def positions(it, w, c):
                    s, t, h, _ = parts(w)
                    if w % (NU // 2) == 0 and c == 0:
                        pe.wait_ge(in_loaded[s], (it + 1) * (16 * 9))
                    pe.wait_ge(u_left, it * (3 * NU) + (3 * w + c))
                    at = S - P - P * t + c * UC
                    pe.matmul(u_ps[:, 0:UC], q4[s][:, h, t * P:(t + 1) * P], r4[:, at:at + UC],
                              start=True, stop=True).then_inc(u_ready, 1)

                def transposes(it, x, half):
                    g = 2 * x + half
                    if g >= NPT:
                        left, n = (left_act if (g - NPT) % 2 else left_dve), (g - NPT) // 2 + 1
                        pe.wait_ge(left, it * NU + n)
                    for j in range(4):
                        a = (4 * half + j) * P
                        last = pe.transpose(pT[g % NPT][:, j, :], prob[x % NP][:, a:a + P], ident[:, :])
                    last.then_inc(pT_ready, 1)

                def values(it, tt):
                    s = tt // NQ
                    pe.wait_ge(left_dve, it * NU + HG * (tt + 1))
                    pe.wait_ge(left_act, it * NU + HG * (tt + 1))
                    pe.wait_ge(o_done, it * NT + tt)
                    for k in range(NQ):
                        for h in range(HG):
                            last = pe.matmul(oT[h * DH:(h + 1) * DH, 0:P], v[s][:, k, h * DH:(h + 1) * DH],
                                             probT[tt % 2][:, h, k, :], start=(k == 0), stop=(k == NQ - 1))
                    if tt % NQ == NQ - 1:
                        last.then_inc(slot_done[s], 1)
                    pe.wait_ge(rden_ready, it * NT + (tt + 1))
                    pe.transpose(oT[:, 256:384], rden_wide[:, tt % 2, :, :].rearrange("p h d -> p (h d)"),
                                 ident[:, :]).then_inc(o_ready, 1)

                with pe.Fori(0, NIT) as it:
                    if rel:
                        for w in range(ULAG):
                            for c in range(3):
                                positions(it, w, c)
                    for step in range(NU + LAG):
                        u, x = step, step - LAG
                        if u < NU:
                            s, t, h, tt = parts(u)
                            if u % (NU // 2) == 0:
                                pe.wait_ge(in_loaded[s], (it + 1) * (16 * 9))
                            if u >= 2:
                                pe.wait_ge(probs_ready, it * NU + (u - 1))
                            for n in range(2):
                                last = pe.matmul(scores[u % 2][:, n * CH:(n + 1) * CH],
                                                 q4[s][:, h, t * P:(t + 1) * P],
                                                 k4[s][:, h, n * CH:(n + 1) * CH], start=True, stop=True)
                            last.then_inc(scores_ready, 1)
                        w = u + ULAG
                        if rel and w < NU:
                            positions(it, w, 0)
                        if x >= 0:
                            pe.wait_ge(probs_ready, it * NU + (x + 1))
                            transposes(it, x, 0)
                        if rel and w < NU:
                            positions(it, w, 1)
                        if x >= 0:
                            transposes(it, x, 1)
                        if rel and w < NU:
                            positions(it, w, 2)
                        if x >= 4 and x % 4 == 0:
                            values(it, x // 4 - 1)
                    values(it, NT - 1)


def adapter_block(nc, io, o_d, x1_d, y_d, gates_d):
    NCH = B * 2
    with ExitStack() as ctx:
        m = Memory(nc, ctx, "ad")
        w_in = m.sb("w_in", [P, KT, D])
        wo_hi, wo_lo = m.sb("wo_hi", [P, KT, D], F32R), m.sb("wo_lo", [P, KT, D], F32R)
        g_in = m.sb("g_in", [P, KT, NE])
        g_hi, g_lo = m.sb("g_hi", [P, KT, NE], F32R), m.sb("g_lo", [P, KT, NE], F32R)
        cols = m.sb("cols", [P, 2, KT])
        ident = m.sb("ident", [P, P])
        iota8 = m.sb("iota8", [P, NE])
        ids = m.sb("ids", [1, B], I32)
        w1_in, w2_in = m.sb("w1_in", [P, KT, AD]), m.sb("w2_in", [P, D])
        w1_hi, w1_lo = m.sb("w1_hi", [P, KT, AD], F32R), m.sb("w1_lo", [P, KT, AD], F32R)
        w2_hi, w2_lo = m.sb("w2_hi", [P, D], F32R), m.sb("w2_lo", [P, D], F32R)
        ac = m.sb("ac", [P, 1 + 3 * KT])
        o_in, xT = m.sb("o_in", [P, KT, CH]), m.sb("xT", [P, KT, CH])
        o_hi, o_lo = m.sb("o_hi", [P, KT, CH], F32R), m.sb("o_lo", [P, KT, CH], F32R)
        x1 = m.sb("x1", [P, KT, CH])
        x1_hi, x1_lo = m.sb("x1_hi", [P, KT, CH], F32R), m.sb("x1_lo", [P, KT, CH], F32R)
        h = m.sb("h", [P, CH])
        h_hi, h_lo = m.sb("h_hi", [P, CH], F32R), m.sb("h_lo", [P, CH], F32R)
        xx = m.sb("xx", [P, KT, CH])
        x1n = [m.sb(f"x1n{i}", [P, D]) for i in range(2)]
        stats = m.sb("stats", [P, 4, 6])
        mv = m.sb("mv", [P, 4, 2])
        var, rvar, root, rstd = (m.sb(n, [P, 4]) for n in ("var", "rvar", "root", "rstd"))
        yn = [m.sb(f"yn{i}", [P, D]) for i in range(2)]
        yT = m.sb("yT", [P, KT, CH])
        y_hi, y_lo = m.sb("y_hi", [P, KT, CH], F32R), m.sb("y_lo", [P, KT, CH], F32R)
        lg = m.sb("lg", [P, 4, NE])
        top = m.sb("top", [P, 4, 8])
        top_i = m.sb("top_i", [P, 4, 8], U32)
        top_f = m.sb("top_f", [P, 4, 8])
        diff, e2 = m.sb("diff", [P, 4]), m.sb("e2", [P, 4])
        tot, wt = m.sb("tot", [P, 4]), m.sb("wt", [P, 2, 4])
        hot = m.sb("hot", [P, 4, NE])
        gates = m.sb("gates", [P, 4, NE])
        bank = [m.ps(f"bank{i}", [P, CH]) for i in range(8)]
        names = ("consts w_hi_done w_lo_done ad_loaded o_loaded xT_loaded o_hi_done o_lo_done adw_hi_done "
                 "adw_lo_done o_groups x1_done x1_hi_done x1_lo_done up_done h_done h_hi_done h_lo_done "
                 "down_done xx_done x1_turned x1n_done xx_turned rvar_ready root_ready yn_done y_turned yT_done y_hi_done y_lo_done "
                 "logits_done diff_ready e2_ready gates_done chain").split()
        sm = {n: m.sem(n) for n in names}
        x1_stored = [m.sem(f"x1_stored{i}") for i in range(2)]
        y_stored, gates_stored = m.sem("y_stored"), m.sem("gates_stored")
        passed = m.sem("passed")
        NCONST = 7
        with nc.Block() as block:

            @block.gpsimd
            def _(pool):
                with pool.Fori(0, NCH) as c:
                    pool.wait_ge(sm["o_lo_done"], c)
                    pool.sem_inc(passed)
                    pool.dma_start(o_in[:, :, :], o_d[bass.ds(c // 2 * NG, NG), :, bass.ds(c % 2 * CH, CH)]
                                   .rearrange("k p n -> p k n")).then_inc(sm["o_loaded"], 16)
                    pool.wait_ge(sm["x1_done"], c * 4)
                    pool.sem_inc(passed)
                    pool.dma_start(xT[:, :, :], io["xT"][:, bass.ds(c * CH, CH)]
                                   .rearrange("(k p) n -> p k n", p=P)).then_inc(sm["xT_loaded"], 16)

            @block.sync
            def _(sp):
                for dst, src in (
                    (ids[:, :], io["lang"]), (w_in[:, :, :], io["bWo"].rearrange("(k p) n -> p k n", p=P)),
                    (g_in[:, :, :], io["gateT"].rearrange("(k p) n -> p k n", p=P)),
                    (cols[:, 0, :], io["bbv"]), (cols[:, 1, :], io["bbo"]), (ident[:, :], io["ident"]),
                    (iota8[:, :], io["iota8"]),
                ):
                    sp.dma_start(dst, src).then_inc(sm["consts"], 16)
                sp.wait_ge(sm["consts"], 16 * NCONST)
                with sp.Fori(0, NCH) as c:
                    lang = sp.value_load(ids[0:1, bass.ds(c // 2, 1)], min_val=0, max_val=LANGS - 1)
                    sp.wait_ge(sm["yT_done"], c * 4)
                    sp.sem_inc(passed)
                    sp.dma_start(w1_in[:, :, :], io["W1"][bass.ds(lang, 1), :, :]
                                 .rearrange("a (k p) n -> p (a k) n", p=P)).then_inc(sm["ad_loaded"], 16)
                    sp.dma_start(w2_in[:, :], io["W2"][bass.ds(lang, 1), :, :]
                                 .rearrange("a p n -> p (a n)")).then_inc(sm["ad_loaded"], 16)
                    sp.dma_start(ac[:, :], io["adcols"][bass.ds(lang, 1), :, :]
                                 .rearrange("a p n -> p (a n)")).then_inc(sm["ad_loaded"], 16)
                    for r in range(4):
                        sp.wait_ge(sm["x1n_done"], c * 4 + (r + 1))
                        sp.sem_inc(passed)
                        sp.dma_start(x1_d[c, :, r, :], x1n[r % 2][:, :]).then_inc(x1_stored[r % 2], 16)
                    sp.wait_ge(sm["y_lo_done"], c + 1)
                    sp.sem_inc(passed)
                    sp.dma_start(y_d[0, c, :, :, :], y_hi[:, :, :].bitcast(F32)).then_inc(y_stored, 16)
                    sp.dma_start(y_d[1, c, :, :, :], y_lo[:, :, :].bitcast(F32)).then_inc(y_stored, 16)
                    sp.wait_ge(sm["gates_done"], c + 1)
                    sp.sem_inc(passed)
                    sp.dma_start(gates_d[c, :, :, :], gates[:, :, :]).then_inc(gates_stored, 16)
                for i in range(2):
                    sp.wait_ge(x1_stored[i], 16 * 2 * NCH)
                sp.wait_ge(y_stored, 32 * NCH)
                sp.wait_ge(gates_stored, 16 * NCH)

            @block.scalar
            def _(act):
                ident_fn = ACT.Identity
                act.wait_ge(sm["consts"], 16 * NCONST)
                act.activation(wo_hi[:, :, :], w_in[:, :, :], ident_fn)
                act.activation(g_hi[:, :, :], g_in[:, :, :], ident_fn).then_inc(sm["w_hi_done"], 1)
                with act.Fori(0, NCH) as c:
                    act.wait_ge(sm["o_loaded"], c * 16 + 16)
                    act.wait_ge(sm["o_groups"], c * 4)
                    for k in range(KT):
                        last = act.activation(o_hi[:, k, :], o_in[:, k, :], ident_fn, bias=cols[:, 0, k:k + 1])
                    last.then_inc(sm["o_hi_done"], 1)
                    act.wait_ge(sm["ad_loaded"], c * 48 + 48)
                    act.activation(w1_hi[:, :, :], w1_in[:, :, :], ident_fn)
                    act.activation(w2_hi[:, :], w2_in[:, :], ident_fn).then_inc(sm["adw_hi_done"], 1)
                    for k in range(KT):
                        act.wait_ge(sm["x1_done"], c * 4 + (k + 1))
                        act.activation(x1_hi[:, k, :], x1[:, k, :], ident_fn).then_inc(sm["x1_hi_done"], 1)
                    act.wait_ge(sm["up_done"], c + 1)
                    act.activation(h[:, :], bank[4][:, :], ACT.Relu, bias=ac[:, 0:1]).then_inc(sm["h_done"], 1)
                    act.wait_ge(sm["h_done"], c + 1)
                    act.activation(h_hi[:, :], h[:, :], ident_fn).then_inc(sm["h_hi_done"], 1)
                    for r in range(4):
                        act.wait_ge(x1_stored[r % 2], c * 32 + 16 * (r // 2))
                        act.wait_ge(sm["x1_turned"], c * 4 + (r + 1))
                        act.activation(x1n[r % 2][:, :], bank[5 + r % 2][:, :], ACT.Copy)\
                            .then_inc(sm["x1n_done"], 1)
                    act.wait_ge(sm["rvar_ready"], c + 1)
                    act.activation(root[:, :], rvar[:, :], ACT.Sqrt).then_inc(sm["root_ready"], 1)
                    for r in range(4):
                        act.wait_ge(sm["y_turned"], c * 4 + (r + 1))
                        for k in range(KT):
                            last = act.activation(yT[:, k, r * P:(r + 1) * P],
                                                  bank[4 + r][:, k * P:(k + 1) * P], ident_fn,
                                                  scale=ac[:, 1 + KT + k:2 + KT + k],
                                                  bias=ac[:, 1 + 2 * KT + k:2 + 2 * KT + k])
                        last.then_inc(sm["yT_done"], 1)
                    act.wait_ge(sm["yT_done"], c * 4 + 4)
                    act.wait_ge(y_stored, c * 32)
                    act.activation(y_hi[:, :, :], yT[:, :, :], ident_fn).then_inc(sm["y_hi_done"], 1)
                    act.wait_ge(sm["diff_ready"], c + 1)
                    act.activation(e2[:, :], diff[:, :], ACT.Exp).then_inc(sm["e2_ready"], 1)

            @block.vector
            def _(dve):
                f32 = lambda t: t.bitcast(F32)
                dve.wait_ge(sm["w_hi_done"], 1)
                dve.tensor_tensor(wo_lo[:, :, :], w_in[:, :, :], f32(wo_hi[:, :, :]), ALU.subtract)
                dve.tensor_tensor(g_lo[:, :, :], g_in[:, :, :], f32(g_hi[:, :, :]), ALU.subtract)\
                    .then_inc(sm["w_lo_done"], 1)
                NCHAIN = 7 + 12
                with dve.Fori(0, NCH) as c:
                    links = [0]

                    def then(ins):
                        links[0] += 1
                        ins.then_inc(sm["chain"], 1)
                        dve.wait_ge(sm["chain"], c * NCHAIN + links[0])
                        dve.sem_inc(passed)

                    dve.wait_ge(sm["o_hi_done"], c + 1)
                    for k in range(KT):
                        last = dve.scalar_tensor_tensor(out=o_lo[:, k, :], in0=o_in[:, k, :],
                                                        scalar=cols[:, 0, k:k + 1], in1=f32(o_hi[:, k, :]),
                                                        op0=ALU.add, op1=ALU.subtract)
                    last.then_inc(sm["o_lo_done"], 1)
                    dve.wait_ge(sm["adw_hi_done"], c + 1)
                    dve.tensor_tensor(w1_lo[:, :, :], w1_in[:, :, :], f32(w1_hi[:, :, :]), ALU.subtract)
                    dve.tensor_tensor(w2_lo[:, :], w2_in[:, :], f32(w2_hi[:, :]), ALU.subtract)\
                        .then_inc(sm["adw_lo_done"], 1)
                    dve.wait_ge(sm["xT_loaded"], c * 16 + 16)
                    for k in range(KT):
                        dve.wait_ge(sm["o_groups"], c * 4 + (k + 1))
                        dve.scalar_tensor_tensor(out=x1[:, k, :], in0=bank[k][:, :], scalar=cols[:, 1, k:k + 1],
                                                 in1=xT[:, k, :], op0=ALU.add, op1=ALU.add)\
                            .then_inc(sm["x1_done"], 1)
                    for k in range(KT):
                        dve.wait_ge(sm["x1_hi_done"], c * 4 + (k + 1))
                        dve.tensor_tensor(x1_lo[:, k, :], x1[:, k, :], f32(x1_hi[:, k, :]), ALU.subtract)\
                            .then_inc(sm["x1_lo_done"], 1)
                    dve.wait_ge(sm["h_hi_done"], c + 1)
                    dve.tensor_tensor(h_lo[:, :], h[:, :], f32(h_hi[:, :]), ALU.subtract)\
                        .then_inc(sm["h_lo_done"], 1)
                    for k in range(KT):
                        dve.wait_ge(sm["down_done"], c * 4 + (k + 1))
                        dve.scalar_tensor_tensor(out=xx[:, k, :], in0=bank[k][:, :], scalar=ac[:, 1 + k:2 + k],
                                                 in1=x1[:, k, :], op0=ALU.add, op1=ALU.add)\
                            .then_inc(sm["xx_done"], 1)
                    for r in range(4):
                        dve.wait_ge(sm["xx_turned"], c * 4 + (r + 1))
                        dve.sem_inc(passed)
                        last = dve.bn_stats(stats[:, r, :], bank[r][:, :])
                    then(last)
                    for r in range(4):
                        last = dve.bn_aggr(mv[:, r, :], stats[:, r, :])
                    then(last)
                    then(dve.tensor_scalar(var[:, :], mv[:, :, 1], LN_EPS, None, ALU.add))
                    dve.reciprocal(rvar[:, :], var[:, :]).then_inc(sm["rvar_ready"], 1)
                    dve.wait_ge(sm["root_ready"], c + 1)
                    then(dve.tensor_tensor(rstd[:, :], root[:, :], root[:, :], ALU.mult))
                    then(dve.tensor_tensor(rstd[:, :], rstd[:, :], var[:, :], ALU.mult))
                    then(dve.tensor_scalar(rstd[:, :], rstd[:, :], -0.5, 1.5, ALU.mult, ALU.add))
                    then(dve.tensor_tensor(rstd[:, :], rstd[:, :], root[:, :], ALU.mult))
                    for r in range(4):
                        if r >= 2:
                            dve.wait_ge(sm["y_turned"], c * 4 + (r - 1))
                        dve.tensor_scalar(yn[r % 2][:, :], bank[r][:, :], mv[:, r, 0:1], rstd[:, r:r + 1],
                                          ALU.subtract, ALU.mult).then_inc(sm["yn_done"], 1)
                    dve.wait_ge(sm["y_hi_done"], c + 1)
                    dve.tensor_tensor(y_lo[:, :, :], yT[:, :, :], f32(y_hi[:, :, :]), ALU.subtract)\
                        .then_inc(sm["y_lo_done"], 1)
                    dve.wait_ge(sm["logits_done"], c + 1)
                    then(dve.tensor_copy(lg[:, :, :], bank[4][:, 0:4 * NE].rearrange("p (r e) -> p r e", r=4)))
                    for r in range(4):
                        last = dve.max(top[:, r, :], lg[:, r, :])
                    then(last)
                    for r in range(4):
                        last = dve.max_index(top_i[:, r, :], top[:, r, :], lg[:, r, :])
                    then(last)
                    dve.tensor_tensor(diff[:, :], top[:, :, 1], top[:, :, 0], ALU.subtract)\
                        .then_inc(sm["diff_ready"], 1)
                    then(dve.tensor_copy(top_f[:, :, :], top_i[:, :, :]))
                    dve.wait_ge(sm["e2_ready"], c + 1)
                    then(dve.tensor_scalar(tot[:, :], e2[:, :], 1.0, None, ALU.add))
                    then(dve.reciprocal(wt[:, 0, :], tot[:, :]))
                    then(dve.tensor_tensor(wt[:, 1, :], wt[:, 0, :], e2[:, :], ALU.mult))
                    dve.wait_ge(gates_stored, c * 16)
                    for r in range(4):
                        last = dve.tensor_scalar(hot[:, r, :], iota8[:, :], top_f[:, r, 1:2], wt[:, 1, r:r + 1],
                                                 ALU.is_equal, ALU.mult)
                    then(last)
                    for r in range(4):
                        last = dve.tensor_scalar(gates[:, r, :], iota8[:, :], top_f[:, r, 0:1],
                                                 wt[:, 0, r:r + 1], ALU.is_equal, ALU.mult)
                    then(last)
                    dve.tensor_tensor(gates[:, :, :], gates[:, :, :], hot[:, :, :], ALU.add)\
                        .then_inc(sm["gates_done"], 1)
                    for _ in range(NCHAIN - links[0]):
                        dve.sem_inc(sm["chain"], 1)

            @block.tensor
            def _(pe):
                pe.wait_ge(sm["w_lo_done"], 1)

                def product(out, pairs):
                    n = len(pairs)
                    for i, (lhs, rhs) in enumerate(pairs):
                        last = pe.matmul(out, lhs, rhs, start=(i == 0), stop=(i == n - 1))
                    return last

                def turn(dst, src):
                    for k in range(KT):
                        last = pe.transpose(dst[:, k * P:(k + 1) * P], src(k), ident[:, :])
                    return last

                def tile(k):
                    return slice(k * P, (k + 1) * P)

                with pe.Fori(0, NCH) as c:
                    pe.wait_ge(sm["o_lo_done"], c + 1)
                    for j in range(KT):
                        product(bank[j][:, :], [(w[:, k, tile(j)], a[:, k, :]) for k in range(KT)
                                                for w, a in ((wo_hi, o_hi), (wo_hi, o_lo), (wo_lo, o_hi))])\
                            .then_inc(sm["o_groups"], 1)
                    pe.wait_ge(sm["adw_lo_done"], c + 1)
                    pe.wait_ge(sm["x1_lo_done"], c * 4 + 4)
                    product(bank[4][:, :], [(w[:, k, :], a[:, k, :]) for k in range(KT)
                                            for w, a in ((w1_hi, x1_hi), (w1_hi, x1_lo), (w1_lo, x1_hi))])\
                        .then_inc(sm["up_done"], 1)
                    for r in range(4):
                        if r < 2:
                            turn(bank[5 + r % 2], lambda k: x1[:, k, tile(r)]).then_inc(sm["x1_turned"], 1)
                    pe.wait_ge(sm["h_lo_done"], c + 1)
                    for j in range(KT):
                        product(bank[j][:, :], [(w[:, tile(j)], a[:, :])
                                                for w, a in ((w2_hi, h_hi), (w2_hi, h_lo), (w2_lo, h_hi))])\
                            .then_inc(sm["down_done"], 1)
                    for r in range(2, 4):
                        pe.wait_ge(sm["x1n_done"], c * 4 + (r - 1))
                        turn(bank[5 + r % 2], lambda k: x1[:, k, tile(r)]).then_inc(sm["x1_turned"], 1)
                    pe.wait_ge(sm["xx_done"], c * 4 + 4)
                    for r in range(4):
                        turn(bank[r], lambda k: xx[:, k, tile(r)]).then_inc(sm["xx_turned"], 1)
                    pe.wait_ge(sm["x1n_done"], c * 4 + 4)
                    for r in range(4):
                        pe.wait_ge(sm["yn_done"], c * 4 + (r + 1))
                        turn(bank[4 + r], lambda k: yn[r % 2][:, tile(k)]).then_inc(sm["y_turned"], 1)
                    pe.wait_ge(sm["y_lo_done"], c + 1)
                    for r in range(4):
                        last = product(bank[4][:, r * NE:(r + 1) * NE],
                                       [(a[:, k, tile(r)], w[:, k, :]) for k in range(KT)
                                        for w, a in ((g_hi, y_hi), (g_hi, y_lo), (g_lo, y_hi))])
                    last.then_inc(sm["logits_done"], 1)


def experts_block(nc, io, x1_d, y_d, gates_d, out_d):
    with ExitStack() as ctx:
        m = Memory(nc, ctx, "ex")
        w_hi = [m.sb(f"w_hi{e}", [P, KT, D], F32R) for e in range(NE)]
        w_lo = [m.sb(f"w_lo{e}", [P, KT, D], F32R) for e in range(NE)]
        w_in = m.sb("w_in", [P, KT, D])
        y = [[m.sb(f"y{s}_{a}", [P, KT, CH], F32R) for a in range(2)] for s in range(2)]
        x1 = [m.sb(f"x1_{s}", [P, 4, D]) for s in range(2)]
        gates = [m.sb(f"gates{s}", [P, 4, NE]) for s in range(2)]
        acc = [m.sb(f"acc{i}", [P, D]) for i in range(2)]
        out_sb = [m.sb(f"out_sb{i}", [P, D]) for i in range(2)]
        NBANK = 8
        bank = [m.ps(f"bank{i}", [P, D]) for i in range(NBANK)]
        w_loaded, w_hi_done, w_lo_done = m.sem("w_loaded"), m.sem("w_hi_done"), m.sem("w_lo_done")
        loaded = [m.sem(f"loaded{s}") for s in range(2)]
        group_done, added, chunk_done = m.sem("group_done"), m.sem("added"), m.sem("chunk_done")
        stored = [m.sem(f"stored{i}") for i in range(2)]
        passed = m.sem("passed")
        GC = 4 * NE
        GT = 2 * GC
        with nc.Block() as block:

            @block.gpsimd
            def _(pool):
                with pool.Fori(0, B) as b:
                    for s in range(2):
                        pool.wait_ge(added, b * GT + (s * GC if s == 0 else 0))
                        pool.sem_inc(passed)
                        if s == 1:
                            pool.wait_ge(chunk_done, b * 2)
                            pool.sem_inc(passed)
                        c = b * 2 + s
                        for a in range(2):
                            pool.dma_start(y[s][a][:, :, :].bitcast(F32), y_d[a, c, :, :, :]).then_inc(loaded[s], 16)
                        pool.dma_start(x1[s][:, :, :], x1_d[c, :, :, :]).then_inc(loaded[s], 16)
                        pool.dma_start(gates[s][:, :, :], gates_d[c, :, :, :]).then_inc(loaded[s], 16)

            @block.sync
            def _(sp):
                for e in range(NE):
                    sp.wait_ge(w_lo_done, e)
                    sp.dma_start(w_in[:, :, :], io["weight"][e, :, :].rearrange("(k p) n -> p k n", p=P))\
                        .then_inc(w_loaded, 16)
                with sp.Fori(0, B) as b:
                    for s in range(2):
                        for r in range(4):
                            sp.wait_ge(added, b * GT + (s * GC + (r + 1) * NE))
                            sp.sem_inc(passed)
                            sp.dma_start(out_d[b, s * CH + r * P:s * CH + (r + 1) * P, :], out_sb[r % 2][:, :])\
                                .then_inc(stored[r % 2], 16)
                for i in range(2):
                    sp.wait_ge(stored[i], 16 * 4 * B)

            @block.scalar
            def _(act):
                for e in range(NE):
                    act.wait_ge(w_loaded, 16 * (e + 1))
                    act.activation(w_hi[e][:, :, :], w_in[:, :, :], ACT.Identity).then_inc(w_hi_done, 1)

            @block.vector
            def _(dve):
                for e in range(NE):
                    dve.wait_ge(w_hi_done, e + 1)
                    dve.tensor_tensor(w_lo[e][:, :, :], w_in[:, :, :], w_hi[e][:, :, :].bitcast(F32),
                                      ALU.subtract).then_inc(w_lo_done, 1)
                with dve.Fori(0, B) as b:
                    for g in range(GT):
                        s, r, e = g // GC, g // NE % 4, g % NE
                        if g % GC == 0:
                            dve.wait_ge(loaded[s], b * 64 + 64)
                        if e == NE - 1:
                            dve.wait_ge(stored[r % 2], b * 64 + 16 * ((s * 4 + r) // 2))
                        dve.wait_ge(added, b * GT + g)
                        dve.wait_ge(group_done, b * GT + (g + 1))
                        src = x1[s][:, r, :] if e == 0 else acc[(e + 1) % 2][:, :]
                        dst = out_sb[r % 2][:, :] if e == NE - 1 else acc[e % 2][:, :]
                        dve.scalar_tensor_tensor(out=dst, in0=bank[g % NBANK][:, :], scalar=gates[s][:, r, e:e + 1],
                                                 in1=src, op0=ALU.mult, op1=ALU.add).then_inc(added, 1)

            @block.tensor
            def _(pe):
                with pe.Fori(0, B) as b:
                    for g in range(GT):
                        s, r, e = g // GC, g // NE % 4, g % NE
                        if g % GC == 0:
                            pe.wait_ge(loaded[s], b * 64 + 64)
                        if r == 0 and s == 0:
                            pe.wait_ge(w_lo_done, e + 1)
                        if g >= NBANK:
                            pe.wait_ge(added, b * GT + (g - NBANK + 1))
                        else:
                            pe.wait_ge(added, b * GT)
                        n = 0
                        for k in range(KT):
                            for a, w in ((0, w_hi), (0, w_lo), (1, w_hi)):
                                last = pe.matmul(bank[g % NBANK][:, :], y[s][a][:, k, r * P:(r + 1) * P],
                                                 w[e][:, k, :], start=(n == 0), stop=(n == 3 * KT - 1))
                                n += 1
                        last.then_inc(group_done, 1)
                        if g % GC == GC - 1:
                            pe.drain().then_inc(chunk_done, 1)


def build_program(nc, io, out_d):
    def scratch(name, shape):
        return nc.dram_tensor(name, shape, F32, kind="Internal").ap()

    q_d, k_d = scratch("q_parts", (2, NI, P, S)), scratch("k_parts", (2, NI, P, S))
    v_d = scratch("values", (NI, S, P))
    q2_d, k2_d = scratch("q2_parts", (2, NI, P, S)), scratch("k2_parts", (2, NI, P, S))
    v2_d = scratch("values2", (NI, S, P))
    bias_d = scratch("prior_bias", (B, S, S))
    o_d, o2_d = scratch("attended", (NI, P, S)), scratch("attended2", (NI, P, S))
    skew_d = scratch("position_scores", (8, P * UW))
    x1_d = scratch("x1", (B * 2, P, 4, D))
    y_d = scratch("normed", (2, B * 2, P, KT, CH))
    gates_d = scratch("gates", (B * 2, P, 4, NE))

    prior_block(nc, io, bias_d)
    projection_block(
        nc, io, "pa",
        lambda b, s: io["xT"][:, bass.ds(b * S + s * CH, CH)].rearrange("(k p) n -> p k n", p=P),
        (io["aWq"], io["aWk"], io["aWv"]), (io["zero_cols"], io["zero_cols"], io["abq"], io["abk"]),
        None, q_d, k_d, v_d)
    attention_block(nc, io, "aa", q_d, k_d, v_d, o_d, bias_d=bias_d)
    projection_block(
        nc, io, "pb",
        lambda b, s: o_d[bass.ds(b * NG, NG), :, s * CH:(s + 1) * CH].rearrange("k p n -> p k n"),
        (io["bWq"], io["bWk"], io["bWv"]), (io["abv"], io["abo"], io["bbq"], io["bbk"]),
        (io["aWo"],), q2_d, k2_d, v2_d)
    attention_block(nc, io, "ab", q2_d, k2_d, v2_d, o2_d, skew_d=skew_d)
    adapter_block(nc, io, o2_d, x1_d, y_d, gates_d)
    experts_block(nc, io, x1_d, y_d, gates_d, out_d)




def _layout(inputs):
    import numpy as np

    a = {k: np.asarray(v) for k, v in inputs.items()}

    def cols(v):
        return v.reshape(-1, P).T

    x = a["x"].reshape(B * S, D)
    out = {"xT": x.T}
    for short, name in (("a", "L0_cond_"), ("b", "L0_attn_")):
        for n in "qkvo":
            out[f"{short}W{n}"] = a[f"{name}W{n}"].T
            out[f"{short}b{n}"] = cols(a[f"{name}b{n}"])
    w = np.arange(RELW)
    out["relT"] = a["L0_attn_rel_table"][np.clip(NREL - 1 - (w - MAXLEN), 0, NREL - 1)].T
    out["zero_cols"] = np.zeros((P, KT), np.float32)
    out["ident"] = np.eye(P, dtype=np.float32)
    out["iota1"] = np.broadcast_to(np.arange(1, S + 1, dtype=np.float32), (P, S))
    out["iota8"] = np.broadcast_to(np.arange(NE, dtype=np.float32), (P, NE))
    out["prior_idx"] = a["itok_Sx32_0_1023"]
    out["prior_valid"] = a["mask_Sx32_bk1"].view(np.uint8)
    out["prior_mask"] = a["mask_SxS_bk0"].view(np.int32)
    out["uprev"] = np.broadcast_to(a["condB_uprev"].reshape(1, B), (P, B))
    out["lang"] = a["itok_B_0_8"].reshape(1, B)
    out["W1"], out["W2"] = a["L0_cond2_W1"], a["L0_cond2_W2"]
    by_p = [a["L0_cond2_b1"].reshape(LANGS, 1, P)]
    by_p += [a[f"L0_cond2_{n}"].reshape(LANGS, KT, P) for n in ("b2", "gamma", "beta")]
    out["adcols"] = np.concatenate(by_p, axis=1).transpose(0, 2, 1)
    out["gateT"] = a["L0_ffn_gate_w"].T
    out["weight"] = a["L0_ffn_weight"]
    return {k: np.ascontiguousarray(v) for k, v in out.items()}


def kernel(**inputs):
    import concourse.bacc as _bacc
    from concourse.bass_utils import run_bass_kernel_spmd as _run

    nc = _bacc.Bacc("TRN2", target_bir_lowering=False, num_devices=1)
    arrays, io = {}, {}
    for name, a in _layout(inputs).items():
        arrays[f"in_{name}"] = a
        io[name] = nc.dram_tensor(f"in_{name}", a.shape, mybir.dt.from_np(a.dtype), kind="ExternalInput").ap()
    out_d = nc.dram_tensor("out_0", (B, S, D), F32, kind="ExternalOutput").ap()
    build_program(nc, io, out_d)
    r = _run(nc, [arrays], core_ids=[0])
    return r.results[0]["out_0"]
```

```python
from contextlib import ExitStack

import concourse.bass as bass
from concourse import mybir

F32 = mybir.dt.float32
F32R = mybir.dt.float32r
I32 = mybir.dt.int32
U8 = mybir.dt.uint8
U32 = mybir.dt.uint32
ALU = mybir.AluOpType
ACT = mybir.ActivationFunctionType

P = 128
B, S, D = 4, 1024, 512
H, DH = 16, 32
HG = P // DH
NG = H // HG
KT = D // P
CH = 512
NQ = S // P
NI = B * NG
SCALE = float(DH) ** -0.5
NSPARSE = 32
LAM_MAX, ALPHA, THRESHOLD = 10.0, 5.0, 1.0
MAXLEN = 512
NREL = 2 * MAXLEN - 1
RELW = 2 * S
UW = S + P
NE, TOPK = 8, 2
LANGS, AD = 10, 128
LN_EPS = 1e-5
MASKED = -1e30
ONE = 1


class Memory:

    def __init__(self, nc, ctx, tag):
        self.nc, self.ctx, self.tag = nc, ctx, tag

    def sb(self, name, shape, dt=F32):
        return self.ctx.enter_context(self.nc.sbuf_tensor(f"{self.tag}_{name}", shape, dt))

    def ps(self, name, shape, dt=F32):
        return self.ctx.enter_context(self.nc.psum_tensor(f"{self.tag}_{name}", shape, dt))

    def sem(self, name):
        return self.ctx.enter_context(self.nc.semaphore(f"{self.tag}_{name}"))


def prior_block(nc, io, bias_d):
    with ExitStack() as ctx:
        m = Memory(nc, ctx, "pr")
        iota1 = m.sb("iota1", [P, S])
        named_i = m.sb("named_i", [P, NQ, NSPARSE], I32)
        valid_u = m.sb("valid_u", [P, NQ, NSPARSE], U8)
        named_f = m.sb("named_f", [P, NQ, NSPARSE])
        valid_f = m.sb("valid_f", [P, NQ, NSPARSE])
        key1 = m.sb("key1", [P, NQ, NSPARSE])
        mask_w = m.sb("mask_w", [P, NQ, S // 4], I32)
        mask_u = mask_w[:, :, :].bitcast(U8)
        up = m.sb("up", [P, B])
        lam = m.sb("lam", [P, B])
        sparse = m.sb("sparse", [P, B])
        dense_lam = m.sb("dense_lam", [P, B])
        lam1 = m.sb("lam1", [P, B])
        is_dense = m.sb("is_dense", [P, B])
        count = m.sb("count", [P, 2, 2, S])
        floor = m.sb("floor", [P, 2, S])
        lnc = m.sb("lnc", [P, 2, S])
        pen = m.sb("pen", [P, 2, S])
        off = m.sb("off", [P, S])
        dense_part = m.sb("dense_part", [P, S])
        bias = m.sb("bias", [P, B, S])
        loaded, lam_exp, chain = m.sem("loaded"), m.sem("lam_exp"), m.sem("chain")
        floor_ready, ln_ready, bias_ready = m.sem("floor_ready"), m.sem("ln_ready"), m.sem("bias_ready")
        stored = [m.sem(f"stored{b}") for b in range(B)]
        with nc.Block() as block:

            @block.sync
            def _(sp):
                for dst, src in (
                    (iota1[:, :], io["iota1"]),
                    (named_i[:, :, :], io["prior_idx"].rearrange("(t p) j -> p t j", p=P)),
                    (valid_u[:, :, :], io["prior_valid"].rearrange("(t p) j -> p t j", p=P)),
                    (mask_w[:, :, :], io["prior_mask"].rearrange("(t p) k -> p t k", p=P)),
                    (up[:, :], io["uprev"]),
                ):
                    sp.dma_start(dst, src).then_inc(loaded, 16)
                for t in range(NQ):
                    for b in range(B):
                        sp.wait_ge(bias_ready, t * B + b + 1)
                        sp.dma_start(bias_d[b, t * P:(t + 1) * P, :], bias[:, b, :]).then_inc(stored[b], 16)
                for b in range(B):
                    sp.wait_ge(stored[b], 16 * NQ)

            @block.scalar
            def _(act):
                act.wait_ge(loaded, 80)
                act.activation(lam[:, :], up[:, :], ACT.Exp, scale=-ALPHA).then_inc(lam_exp, 1)
                for t in range(NQ):
                    act.wait_ge(floor_ready, t + 1)
                    act.activation(lnc[:, t % 2, :], floor[:, t % 2, :], ACT.Ln).then_inc(ln_ready, 1)

            @block.vector
            def _(dve):
                done = [0]

                def then(ins):
                    done[0] += 1
                    ins.then_inc(chain, 1)
                    dve.wait_ge(chain, done[0])

                dve.wait_ge(loaded, 80)
                dve.tensor_copy(named_f[:, :, :], named_i[:, :, :])
                then(dve.tensor_copy(valid_f[:, :, :], valid_u[:, :, :]))
                then(dve.scalar_tensor_tensor(out=key1[:, :, :], in0=named_f[:, :, :], scalar=1.0,
                                              in1=valid_f[:, :, :], op0=ALU.add, op1=ALU.mult))
                dve.wait_ge(lam_exp, 1)
                then(dve.tensor_scalar(lam1[:, :], lam[:, :], LAM_MAX, None, ALU.mult))
                dve.tensor_scalar(sparse[:, :], lam1[:, :], THRESHOLD, None, ALU.is_ge)
                then(dve.tensor_scalar(is_dense[:, :], lam1[:, :], THRESHOLD, None, ALU.is_lt))
                then(dve.scalar_tensor_tensor(out=dense_lam[:, :], in0=lam1[:, :], scalar=THRESHOLD,
                                              in1=is_dense[:, :], op0=ALU.min, op1=ALU.mult))
                for t in range(NQ):
                    w = t % 2
                    then(dve.tensor_scalar(count[:, w, 0, :], iota1[:, :], key1[:, t, 0:1], None, ALU.is_equal))
                    for j in range(1, NSPARSE):
                        then(dve.scalar_tensor_tensor(out=count[:, w, j % 2, :], in0=iota1[:, :],
                                                      scalar=key1[:, t, j:j + 1],
                                                      in1=count[:, w, (j + 1) % 2, :],
                                                      op0=ALU.is_equal, op1=ALU.add))
                    total = count[:, w, (NSPARSE - 1) % 2, :]
                    dve.tensor_scalar(floor[:, w, :], total, 0.5, None, ALU.max).then_inc(floor_ready, 1)
                    dve.tensor_scalar(pen[:, w, :], total, 0.5, MASKED, ALU.is_lt, ALU.mult)
                    then(dve.tensor_scalar(off[:, :], mask_u[:, t, :], 1.0, 1.0 / SCALE,
                                           ALU.subtract, ALU.mult))
                    dve.wait_ge(ln_ready, t + 1)
                    then(dve.scalar_tensor_tensor(out=lnc[:, w, :], in0=lnc[:, w, :], scalar=1.0 / SCALE,
                                                  in1=pen[:, w, :], op0=ALU.mult, op1=ALU.add))
                    for b in range(B):
                        then(dve.tensor_scalar(dense_part[:, :], off[:, :], dense_lam[:, b:b + 1], None,
                                               ALU.mult))
                        dve.wait_ge(stored[b], 16 * t)
                        dve.scalar_tensor_tensor(out=bias[:, b, :], in0=lnc[:, w, :],
                                                 scalar=sparse[:, b:b + 1], in1=dense_part[:, :],
                                                 op0=ALU.mult, op1=ALU.add).then_inc(bias_ready, 1)
                        dve.wait_ge(bias_ready, t * B + b + 1)


def projection_block(nc, io, tag, source, weights, biases, out, q_d, k_d, v_d):
    wq_d, wk_d, wv_d = weights
    stages = (["o"] if out else []) + ["q", "k", "v"]
    with ExitStack() as ctx:
        m = Memory(nc, ctx, tag)
        w_in = [m.sb(f"w_in{i}", [P, KT, D]) for i in range(2)]
        w_hi = {n: m.sb(f"w{n}_hi", [P, KT, D], F32R) for n in stages}
        w_lo = {n: m.sb(f"w{n}_lo", [P, KT, D], F32R) for n in stages}
        cols = m.sb("cols", [P, 4, KT])
        x_in = [m.sb(f"x_in{s}", [P, KT, CH]) for s in range(2)]
        x_hi = [m.sb(f"x_hi{s}", [P, KT, CH], F32R) for s in range(2)]
        x_lo = [m.sb(f"x_lo{s}", [P, KT, CH], F32R) for s in range(2)]
        c_hi = m.sb("c_hi", [P, KT, CH], F32R)
        c_lo = m.sb("c_lo", [P, KT, CH], F32R)
        NST = 4
        st_hi = [m.sb(f"st_hi{i}", [P, CH], F32R) for i in range(NST)]
        st_lo = [m.sb(f"st_lo{i}", [P, CH], F32R) for i in range(NST)]
        st_v = [m.sb(f"st_v{i}", [P, CH]) for i in range(NST)]
        NBANK = 4
        bank = [m.ps(f"bank{i}", [P, CH]) for i in range(NBANK)]
        w_loaded = [m.sem(f"w_loaded{i}") for i in range(2)]
        w_hi_done, w_lo_done, cols_loaded = m.sem("w_hi_done"), m.sem("w_lo_done"), m.sem("cols_loaded")
        x_loaded = [m.sem(f"x_loaded{s}") for s in range(2)]
        x_hi_done = m.sem("x_hi_done")
        x_lo_done = [m.sem(f"x_lo_done{s}") for s in range(2)]
        chunk_done = [m.sem(f"chunk_done{s}") for s in range(2)]
        group_done, hi_done, bank_free = m.sem("group_done"), m.sem("hi_done"), m.sem("bank_free")
        stored = [m.sem(f"stored{i}") for i in range(NST)]
        passed = m.sem("passed")

        groups = [(n, j) for n in stages for j in range(4)]
        body = [(s, n, j) for s in range(2) for n, j in groups]
        GT = len(body)
        exported = [g for g, (_, n, _) in enumerate(body) if n != "o"]
        with_hi = [g for g, (_, n, _) in enumerate(body) if n != "v"]
        NEX, NHI = len(exported), len(with_hi)
        w_d = {"o": out[0] if out else None, "q": wq_d, "k": wk_d, "v": wv_d}
        bias_col = {"o": 1, "q": 2, "k": 3}

        with nc.Block() as block:

            @block.gpsimd
            def _(pool):
                for sem in x_lo_done + chunk_done + stored:
                    pool.sem_inc(sem, ONE)
                with pool.Fori(0, B) as b:
                    for s in range(2):
                        pool.wait_ge(x_lo_done[s], b + ONE)
                        pool.sem_inc(passed)
                        pool.dma_start(x_in[s][:, :, :], source(b, s)).then_inc(x_loaded[s], 16)

            @block.sync
            def _(sp):
                for n, src in enumerate(biases):
                    sp.dma_start(cols[:, n, :], src).then_inc(cols_loaded, 16)
                for n, name in enumerate(stages):
                    sp.wait_ge(w_lo_done, max(0, n - 1))
                    sp.dma_start(w_in[n % 2][:, :, :], w_d[name].rearrange("(k p) n -> p k n", p=P))\
                        .then_inc(w_loaded[n % 2], 16)
                with sp.Fori(0, B) as b:
                    for e, g in enumerate(exported):
                        s, name, j = body[g]
                        i = e % NST
                        sp.wait_ge(bank_free, b * GT + (NBANK + g + 1))
                        sp.sem_inc(passed)
                        if name == "v":
                            rows = slice(s * CH + j * P, s * CH + (j + 1) * P)
                            for a in range(2):
                                sp.dma_start(v_d[bass.ds(b * NG + 2 * a, 2), rows, :].rearrange("g p c -> p g c"),
                                             st_v[i][:, 2 * a * P:2 * (a + 1) * P].rearrange("p (g c) -> p g c", g=2))\
                                    .then_inc(stored[i], 16)
                        else:
                            d = q_d if name == "q" else k_d
                            for a, st in enumerate((st_hi, st_lo)):
                                sp.dma_start(d[a, b * NG + j, :, s * CH:(s + 1) * CH],
                                             st[i][:, :].bitcast(F32)).then_inc(stored[i], 16)
                for i in range(NST):
                    sp.wait_ge(stored[i], 32 * B * NEX // NST + ONE)

            @block.scalar
            def _(act):
                for n, name in enumerate(stages):
                    act.wait_ge(w_loaded[n % 2], 16 * (n // 2 + 1))
                    act.activation(w_hi[name][:, :, :], w_in[n % 2][:, :, :], ACT.Identity)\
                        .then_inc(w_hi_done, 1)
                act.wait_ge(cols_loaded, 16 * len(biases))

                def split(b, s):
                    act.wait_ge(x_loaded[s], b * 16 + 16)
                    act.wait_ge(chunk_done[s], b + ONE)
                    for k in range(KT):
                        act.activation(x_hi[s][:, k, :], x_in[s][:, k, :], ACT.Identity,
                                       bias=cols[:, 0, k:k + 1]).then_inc(x_hi_done, 1)

                with act.Fori(0, B) as b:
                    split(b, 0)
                    for g, (s, name, j) in enumerate(body):
                        if g == GT // 4:
                            split(b, 1)
                        if name == "v":
                            continue
                        if name != "o":
                            e = exported.index(g)
                            act.wait_ge(stored[e % NST], b * (32 * NEX // NST) + (32 * (e // NST) + ONE))
                            dst = st_hi[e % NST][:, :]
                        else:
                            dst = c_hi[:, j, :]
                        act.wait_ge(group_done, b * GT + (g + 1))
                        act.activation(dst, bank[g % NBANK][:, :], ACT.Identity,
                                       bias=cols[:, bias_col[name], j:j + 1]).then_inc(hi_done, 1)

            @block.vector
            def _(dve):
                for n, name in enumerate(stages):
                    dve.wait_ge(w_hi_done, n + 1)
                    dve.tensor_tensor(w_lo[name][:, :, :], w_in[n % 2][:, :, :],
                                      w_hi[name][:, :, :].bitcast(F32), ALU.subtract).then_inc(w_lo_done, 1)
                dve.wait_ge(cols_loaded, 16 * len(biases))
                dve.sem_inc(bank_free, NBANK)

                def split(b, s):
                    dve.wait_ge(x_hi_done, b * (2 * KT) + (s + 1) * KT)
                    for k in range(KT):
                        ins = dve.scalar_tensor_tensor(out=x_lo[s][:, k, :], in0=x_in[s][:, k, :],
                                                       scalar=cols[:, 0, k:k + 1],
                                                       in1=x_hi[s][:, k, :].bitcast(F32),
                                                       op0=ALU.add, op1=ALU.subtract)
                    ins.then_inc(x_lo_done[s], 1)

                with dve.Fori(0, B) as b:
                    split(b, 0)
                    for g, (s, name, j) in enumerate(body):
                        if g == GT // 4:
                            split(b, 1)
                        src = bank[g % NBANK][:, :]
                        if name == "v":
                            e = exported.index(g)
                            dve.wait_ge(stored[e % NST], b * (32 * NEX // NST) + (32 * (e // NST) + ONE))
                            dve.wait_ge(group_done, b * GT + (g + 1))
                            dve.tensor_copy(st_v[e % NST][:, :], src).then_inc(bank_free, 1)
                            continue
                        if name == "o":
                            hi, lo = c_hi[:, j, :], c_lo[:, j, :]
                        else:
                            e = exported.index(g)
                            hi, lo = st_hi[e % NST][:, :], st_lo[e % NST][:, :]
                        dve.wait_ge(hi_done, b * NHI + (with_hi.index(g) + 1))
                        dve.scalar_tensor_tensor(out=lo, in0=src, scalar=cols[:, bias_col[name], j:j + 1],
                                                 in1=hi.bitcast(F32), op0=ALU.add, op1=ALU.subtract)\
                            .then_inc(bank_free, 1)

            @block.tensor
            def _(pe):
                pe.wait_ge(w_lo_done, len(stages))
                with pe.Fori(0, B) as b:
                    for g, (s, name, j) in enumerate(body):
                        if g % len(groups) == 0:
                            pe.wait_ge(x_lo_done[s], b + (1 + ONE))
                        if out and g % len(groups) == 4:
                            pe.wait_ge(bank_free, b * GT + (NBANK + g))
                        pe.wait_ge(bank_free, b * GT + (g + 1))
                        a_hi, a_lo = (c_hi, c_lo) if out and name != "o" else (x_hi[s], x_lo[s])
                        tile = slice(j * P, (j + 1) * P)
                        last = None
                        for k in range(KT):
                            for wa, xa in ((w_hi, a_hi), (w_hi, a_lo), (w_lo, a_hi)):
                                if name == "v":
                                    lhs, rhs = xa[:, k, tile], wa[name][:, k, :]
                                else:
                                    lhs, rhs = wa[name][:, k, tile], xa[:, k, :]
                                first = last is None
                                last = pe.matmul(bank[g % NBANK][:, :], lhs, rhs, start=first,
                                                 stop=(k == KT - 1 and wa is w_lo))
                        last.then_inc(group_done, 1)
                        if g % len(groups) == len(groups) - 1:
                            pe.drain().then_inc(chunk_done[s], 1)


def attention_block(nc, io, tag, q_d, k_d, v_d, o_d, bias_d=None, skew_d=None):
    rel = skew_d is not None
    NT = 2 * NQ
    NU = NT * HG
    NIT = NI // 2
    LAG = 2
    NRING = 3
    NP = 3
    NADD = 4 if rel else 2
    ULAG = 6
    RLAG = 2
    NUS = 4
    NSK = skew_d.shape[0] if rel else 0

    def parts(u):
        return u // (NU // 2), u // HG % NQ, u % HG, u // HG

    def band(u):
        t = parts(u)[1]
        return (max(0, t - MAXLEN // P) * P, min(NQ, t + MAXLEN // P + 1) * P) if rel else (0, S)

    def pieces(u):
        lo, hi = band(u)
        width = hi - lo + P
        n = -(-width // 512)
        return n, width // n

    def in_step(step):
        x, w = step - LAG, step + ULAG
        t = [("T", x, half) for half in range(2)] if 0 <= x < NU else []
        up = [("U", w, c) for c in range(pieces(w)[0])] if rel and w < NU else []
        return t[:1] + up[:1] + t[1:] + up[1:]

    ring = [("U", w, c) for w in range(ULAG) for c in range(pieces(w)[0])] if rel else []
    for step in range(NU + LAG):
        ring += in_step(step)
    RT = len(ring)
    at = {item: q for q, item in enumerate(ring)}

    def taker(item):
        kind, _, n = item
        return "dve" if (kind, n) in (("T", 1), ("U", 2)) else "act"

    taken, total = {}, {"act": 0, "dve": 0}
    for item in ring:
        total[taker(item)] += 1
        taken[item] = total[taker(item)]

    with ExitStack() as ctx:
        m = Memory(nc, ctx, tag)
        q4 = [m.sb(f"q4_{s}", [P, HG, S], F32R) for s in range(2)]
        k4 = [m.sb(f"k4_{s}", [P, HG, S], F32R) for s in range(2)]
        v = [m.sb(f"v{s}", [P, NQ, P]) for s in range(2)]
        added = [m.sb(f"added{i}", [P, S]) for i in range(NADD)]
        prob = [m.sb(f"prob{i}", [P, S]) for i in range(NP)]
        probT = [m.sb(f"probT{i}", [P, HG, NQ, P]) for i in range(2)]
        o_sb = [m.sb(f"o_sb{s}", [P, S]) for s in range(2)]
        ident = m.sb("ident", [P, P])
        negmax = m.sb("negmax", [P, 4])
        den = m.sb("den", [P, 2, HG])
        rden = m.sb("rden", [P, 2, HG])
        rden_wide = m.sb("rden_wide", [P, 2, HG, DH])
        rT = m.sb("rT", [P, P])
        scores = [m.ps(f"scores{i}", [P, S]) for i in range(2)]
        bank = [m.ps(f"bank{i}", [P, 512]) for i in range(NRING)]
        oT = m.ps("oT", [P, 512])
        if rel:
            table = probT[0][:, :, :, :].rearrange("p h k n -> p (h k n)")
            r_in, r_hi = table[:, 0:RELW], table[:, RELW:2 * RELW].bitcast(F32R)
            r4 = m.sb("r4", [P, RELW], F32R)
            zeros = m.sb("zeros", [P, S - (MAXLEN // P + 1) * P])
            far = m.sb("far", [P, 4])
            u_sb = [m.sb(f"u_sb{i}", [P, UW]) for i in range(NUS)]
            r_hi_done, r4_done, far_done = m.sem("r_hi_done"), m.sem("r4_done"), m.sem("far_done")
            u_stored = [m.sem(f"u_stored{i}") for i in range(NUS)]
        passed = m.sem("passed")
        consts = m.sem("consts")
        in_loaded = [m.sem(f"in_loaded{s}") for s in range(2)]
        slot_done = [m.sem(f"slot_done{s}") for s in range(2)]
        add_loaded = [m.sem(f"add_loaded{i}") for i in range(NADD)]
        scores_ready, added_done, probs_ready = m.sem("scores_ready"), m.sem("added_done"), m.sem("probs_ready")
        ring_ready = m.sem("ring_ready")
        left = {"dve": m.sem("left_dve"), "act": m.sem("left_act")}
        rden_done, rden_ready, o_ready = m.sem("rden_done"), m.sem("rden_ready"), m.sem("o_ready")
        rT_ready, o_done = m.sem("rT_ready"), m.sem("o_done")
        o_stored = [m.sem(f"o_stored{s}") for s in range(2)]
        NC = 5 if rel else 1
        from_one = slot_done + [added_done, o_done] + o_stored + (u_stored if rel else [])

        with nc.Block() as block:

            @block.gpsimd
            def _(pool):
                for sem in from_one:
                    pool.sem_inc(sem, ONE)
                if rel:
                    pool.memset(zeros[:, :], 0.0).then_inc(far_done, 1)

                def load_inputs(s, i):
                    for dst, src, half in ((q4[s], q_d, (0, 0, 1, 1)), (k4[s], k_d, (0, 1, 0, 1))):
                        for g in range(4):
                            pool.dma_start(dst[g * DH:(g + 1) * DH, :, :].bitcast(F32),
                                           src[half[g], i, :, :].rearrange("(h d) n -> d h n", h=HG))\
                                .then_inc(in_loaded[s], 16)
                    pool.dma_start(v[s][:, :, :], v_d[i, :, :].rearrange("(t p) c -> p t c", p=P))\
                        .then_inc(in_loaded[s], 16)

                load_inputs(0, 0)
                with pool.Fori(0, NIT) as it:
                    pool.wait_ge(slot_done[1], it + ONE)
                    pool.sem_inc(passed)
                    load_inputs(1, it * 2 + 1)
                    pool.wait_ge(slot_done[0], it + (1 + ONE))
                    pool.sem_inc(passed)
                    load_inputs(0, (it * 2 + 2) % NI)
                pool.wait_ge(in_loaded[0], 16 * 9 * (NIT + 1))

            @block.sync
            def _(sp):
                sp.dma_start(ident[:, :], io["ident"]).then_inc(consts, 16)
                if rel:
                    for g in range(4):
                        sp.dma_start(r_in[g * DH:(g + 1) * DH, :], io["relT"]).then_inc(consts, 16)
                with sp.Fori(0, NIT) as it:
                    for u in range(NU + RLAG if rel else NU):
                        if rel and u < NU:
                            width = pieces(u)[0] * pieces(u)[1]
                            for c in range(pieces(u)[0])[-2:]:
                                who = taker(("U", u, c))
                                sp.wait_ge(left[who], it * total[who] + taken["U", u, c])
                                sp.sem_inc(passed)
                            if u >= NSK:
                                sp.wait_ge(add_loaded[u % NADD],
                                           it * (16 * NU // NADD) + 16 * ((u - NSK) // NADD + 1))
                                sp.sem_inc(passed)
                            sp.dma_start(skew_d[u % NSK, 0:P * width].rearrange("(p c) -> p c", p=P),
                                         u_sb[u % NUS][:, 0:width]).then_inc(u_stored[u % NUS], 16)
                        if rel and u >= RLAG:
                            r = u - RLAG
                            lo, hi = band(r)
                            width = hi - lo + P
                            if r >= NADD:
                                sp.wait_ge(added_done, it * NU + (r - NADD + 1 + ONE))
                                sp.sem_inc(passed)
                            sp.wait_ge(u_stored[r % NUS], it * (16 * NU // NUS) + (16 * (r // NUS + 1) + ONE))
                            sp.sem_inc(passed)
                            sp.dma_start(added[r % NADD][:, lo:hi],
                                         bass.AP(skew_d.tensor, (r % NSK) * P * UW + P - 1,
                                                 [[width - 1, P], [1, hi - lo]]))\
                                .then_inc(add_loaded[r % NADD], 16)
                        if u >= NU:
                            continue
                        s, t, h, tt = parts(u)
                        if not rel and h == 0:
                            sp.wait_ge(added_done, it * NU + ((HG * (tt - 1) if tt >= 2 else 0) + ONE))
                            sp.sem_inc(passed)
                            sp.dma_start(added[tt % 2][:, :], bias_d[it // 2, t * P:(t + 1) * P, :])\
                                .then_inc(add_loaded[tt % 2], 16)
                        if (t, h) == (4, 3) and s == 1:
                            sp.wait_ge(o_done, it * NT + (NQ + ONE))
                            sp.sem_inc(passed)
                            sp.dma_start(o_d[it * 2, :, :], o_sb[0][:, :]).then_inc(o_stored[0], 16)
                    sp.wait_ge(o_done, it * NT + (NT + ONE))
                    sp.sem_inc(passed)
                    sp.dma_start(o_d[it * 2 + 1, :, :], o_sb[1][:, :]).then_inc(o_stored[1], 16)
                for s in range(2):
                    sp.wait_ge(o_stored[s], 16 * NIT + ONE)

            @block.scalar
            def _(act):
                act.wait_ge(consts, 16 * NC)
                if rel:
                    act.activation(r_hi, r_in, ACT.Identity).then_inc(r_hi_done, 1)

                def take(it, item):
                    act.wait_ge(ring_ready, it * RT + (at[item] + 1))
                    kind, n, c = item
                    src = bank[at[item] % NRING]
                    if kind == "T":
                        dst, src = probT[parts(n)[3] % 2][:, parts(n)[2], 4 * c:4 * c + 4, :], src[:, :].rearrange("p (k n) -> p k n", k=4)
                    else:
                        width = pieces(n)[1]
                        dst, src = u_sb[n % NUS][:, c * width:(c + 1) * width], src[:, 0:width]
                    act.activation(dst, src, ACT.Copy).then_inc(left["act"], 1)

                def take_all(it, items):
                    for item in items:
                        kind, n, c = item
                        if kind == "U" and c == 0:
                            act.wait_ge(u_stored[n % NUS], it * (16 * NU // NUS) + (16 * (n // NUS) + ONE))
                        if kind == "T" and parts(n)[3] >= 2 and parts(n)[2] == 0:
                            act.wait_ge(o_ready, it * NT + (parts(n)[3] - 1))
                        if taker(item) == "act":
                            take(it, item)

                def turn_den(it, tt):
                    act.wait_ge(o_ready, it * NT + (tt + 1))
                    act.activation(rT[:, :], oT[:, 256:384], ACT.Copy).then_inc(rT_ready, 1)

                with act.Fori(0, NIT) as it:
                    take_all(it, ring[:at["T", 0, 0]])
                    for step in range(NU + LAG):
                        u, x = step, step - LAG
                        items = in_step(step) if x >= 0 else []
                        if x >= 8 and x % 4 == 0:
                            turn_den(it, x // 4 - 2)
                        take_all(it, items[:2])
                        if u < NU:
                            s, t, h, tt = parts(u)
                            if u >= NP:
                                act.wait_ge(ring_ready, it * RT + (at["T", u - NP, 1] + 1))
                            act.wait_ge(added_done, it * NU + (u + 1 + ONE))
                            act.activation(prob[u % NP][:, :], scores[u % 2][:, :], ACT.Exp,
                                           bias=negmax[:, u % 4:u % 4 + 1], scale=-1.0,
                                           accum_out=den[:, tt % 2, h:h + 1]).then_inc(probs_ready, 1)
                        take_all(it, items[2:])
                    for tt in range(NT - 2, NT):
                        turn_den(it, tt)

            @block.vector
            def _(dve):
                dve.wait_ge(consts, 16 * NC)
                if rel:
                    dve.wait_ge(r_hi_done, 1)
                    for g in range(4):
                        rows = slice(g * DH, (g + 1) * DH)
                        if g % 2 == 0:
                            dve.tensor_copy(r4[rows, :], r_hi[rows, :].bitcast(F32)).then_inc(r4_done, 1)
                        else:
                            dve.tensor_tensor(r4[rows, :], r_in[rows, :], r_hi[rows, :].bitcast(F32),
                                              ALU.subtract).then_inc(r4_done, 1)
                    dve.wait_ge(far_done, 1)

                def normalise(it, tt):
                    s, t = tt // NQ, tt % NQ
                    if t == 0:
                        dve.wait_ge(o_stored[s], it * 16 + ONE)
                    dve.wait_ge(rT_ready, it * NT + (tt + 1))
                    dve.tensor_tensor(o_sb[s][:, t * P:(t + 1) * P], oT[:, 0:P], rT[:, :], ALU.mult)\
                        .then_inc(o_done, 1)

                def third(it, w):
                    width = pieces(w)[1]
                    dve.wait_ge(u_stored[w % NUS], it * (16 * NU // NUS) + (16 * (w // NUS) + ONE))
                    dve.wait_ge(ring_ready, it * RT + (at["U", w, 2] + 1))
                    dve.tensor_copy(u_sb[w % NUS][:, 2 * width:3 * width], bank[at["U", w, 2] % NRING][:, 0:width])\
                        .then_inc(left["dve"], 1)

                def scale_min(dst, lo, hi, add, first, least):
                    return dve.tensor_tensor_reduce(out=dst[:, lo:hi], in0=dst[:, lo:hi], in1=add, scale=-SCALE,
                                                    scalar=first, op0=ALU.add, op1=ALU.min, accum_out=least)

                NFAR = sum(band(u) != (0, S) for u in range(NU))
                with dve.Fori(0, NIT) as it:
                    fars = 0
                    for step in range(NU + LAG):
                        u, x = step, step - LAG
                        if u < NU:
                            s, t, h, tt = parts(u)
                            lo, hi = band(u)
                            dst, least = scores[u % 2], negmax[:, u % 4:u % 4 + 1]
                            dve.wait_ge(scores_ready, it * NU + (u + 1))
                            dve.sem_inc(passed)
                            first = 3e38
                            if (lo, hi) != (0, S):
                                a, b = (0, lo) if lo else (hi, S)
                                first = far[:, u % 4:u % 4 + 1]
                                scale_min(dst, a, b, zeros[:, 0:b - a], 3e38, first).then_inc(far_done, 1)
                                fars += 1
                                dve.wait_ge(far_done, it * NFAR + (fars + 1))
                            if rel:
                                dve.wait_ge(add_loaded[u % NADD], it * (16 * NU // NADD) + 16 * (u // NADD + 1))
                            elif h == 0:
                                dve.wait_ge(add_loaded[tt % 2], it * (16 * NQ) + 16 * (tt // 2 + 1))
                            dve.sem_inc(passed)
                            scale_min(dst, lo, hi, added[(u if rel else tt) % NADD][:, lo:hi], first, least)\
                                .then_inc(added_done, 1)
                        if 0 <= x < NU:
                            s, t, h, tt = parts(x)
                            if tt >= 2 and h == 0:
                                dve.wait_ge(o_ready, it * NT + (tt - 1))
                            dve.wait_ge(ring_ready, it * RT + (at["T", x, 1] + 1))
                            dve.tensor_copy(probT[tt % 2][:, h, 4:8, :],
                                            bank[at["T", x, 1] % NRING][:, :].rearrange("p (k n) -> p k n", k=4))\
                                .then_inc(left["dve"], 1)
                            if ("U", step + ULAG, 2) in at:
                                third(it, step + ULAG)
                            if h == HG - 1:
                                dve.wait_ge(probs_ready, it * NU + (x + 1))
                                dve.reciprocal(rden[:, tt % 2, :], den[:, tt % 2, :]).then_inc(rden_done, 1)
                                dve.wait_ge(rden_done, it * NT + (tt + 1))
                                dve.tensor_copy(rden_wide[:, tt % 2, :, :],
                                                rden[:, tt % 2, :].rearrange("p (h a) -> p h a", a=1)
                                                .to_broadcast([P, HG, DH])).then_inc(rden_ready, 1)
                        if x >= 8 and x % 4 == 0:
                            normalise(it, x // 4 - 2)
                    for tt in range(NT - 2, NT):
                        normalise(it, tt)

            @block.tensor
            def _(pe):
                pe.wait_ge(consts, 16 * NC)
                if rel:
                    pe.wait_ge(r4_done, 4)

                def into_ring(it, item):
                    q = at[item]
                    kind, n, c = item
                    if q >= NRING:
                        who = taker(ring[q - NRING])
                        pe.wait_ge(left[who], it * total[who] + taken[ring[q - NRING]])
                    if kind == "T":
                        for j in range(4):
                            a = (4 * c + j) * P
                            last = pe.transpose(bank[q % NRING][:, j * P:(j + 1) * P], prob[n % NP][:, a:a + P],
                                                ident[:, :])
                    else:
                        s, t, h, _ = parts(n)
                        width = pieces(n)[1]
                        if n % (NU // 2) == 0 and c == 0:
                            pe.wait_ge(in_loaded[s], (it + 1) * (16 * 9))
                        a = S - P - P * t + band(n)[0] + c * width
                        last = pe.matmul(bank[q % NRING][:, 0:width], q4[s][:, h, t * P:(t + 1) * P],
                                         r4[:, a:a + width], start=True, stop=True)
                    last.then_inc(ring_ready, 1)

                def product(u):
                    s, t, h, tt = parts(u)
                    lo, hi = band(u)
                    query = q4[s][:, h, t * P:(t + 1) * P]
                    for n in range(2):
                        at = n * CH
                        a, b, row = (0, min(lo, CH), 0) if n == 0 else (max(hi, CH), S, RELW - MAXLEN)
                        last = pe.matmul(scores[u % 2][:, at:at + CH], query, k4[s][:, h, at:at + CH],
                                         start=True, stop=(a == b))
                        if a < b:
                            last = pe.matmul(scores[u % 2][:, a:b], query, r4[:, row:row + b - a],
                                             start=False, stop=True)
                    return last

                def values(it, tt, part):
                    s = tt // NQ
                    if part == 0:
                        for half in range(2):
                            who = taker(("T", 0, half))
                            pe.wait_ge(left[who], it * total[who] + taken["T", HG * (tt + 1) - 1, half])
                        pe.wait_ge(o_done, it * NT + (tt + ONE))
                    for k in range(2 * part, 2 * part + 2):
                        for h in range(HG):
                            last = pe.matmul(oT[h * DH:(h + 1) * DH, 0:P], v[s][:, k, h * DH:(h + 1) * DH],
                                             probT[tt % 2][:, h, k, :], start=(k == 0), stop=(k == NQ - 1))
                    if part == 3:
                        if tt % NQ == NQ - 1:
                            last.then_inc(slot_done[s], 1)
                        pe.wait_ge(rden_ready, it * NT + (tt + 1))
                        pe.transpose(oT[:, 256:384], rden_wide[:, tt % 2, :, :].rearrange("p h d -> p (h d)"),
                                     ident[:, :]).then_inc(o_ready, 1)

                with pe.Fori(0, NIT) as it:
                    for item in ring[:at["T", 0, 0]]:
                        into_ring(it, item)
                    for step in range(NU + LAG):
                        u, x = step, step - LAG
                        if u < NU:
                            s, t, h, tt = parts(u)
                            if u % (NU // 2) == 0:
                                pe.wait_ge(in_loaded[s], (it + 1) * (16 * 9))
                            if u >= 2:
                                pe.wait_ge(probs_ready, it * NU + (u - 1))
                            product(u).then_inc(scores_ready, 1)
                        if x >= 0:
                            pe.wait_ge(probs_ready, it * NU + (x + 1))
                            for item in in_step(step):
                                into_ring(it, item)
                        if x >= 4:
                            values(it, x // 4 - 1, x % 4)
                    for part in range(4):
                        values(it, NT - 1, part)


def adapter_block(nc, io, o_d, x1_d, y_d, gates_d):
    NCH = B * 2
    with ExitStack() as ctx:
        m = Memory(nc, ctx, "ad")
        w_in = m.sb("w_in", [P, KT, D])
        wo_hi, wo_lo = m.sb("wo_hi", [P, KT, D], F32R), m.sb("wo_lo", [P, KT, D], F32R)
        g_in = m.sb("g_in", [P, KT, NE])
        g_hi, g_lo = m.sb("g_hi", [P, KT, NE], F32R), m.sb("g_lo", [P, KT, NE], F32R)
        cols = m.sb("cols", [P, 2, KT])
        ident = m.sb("ident", [P, P])
        iota8 = m.sb("iota8", [P, NE])
        ids = m.sb("ids", [1, B], I32)
        w1_in, w2_in = m.sb("w1_in", [P, KT, AD]), m.sb("w2_in", [P, D])
        w1_hi, w1_lo = m.sb("w1_hi", [P, KT, AD], F32R), m.sb("w1_lo", [P, KT, AD], F32R)
        w2_hi, w2_lo = m.sb("w2_hi", [P, D], F32R), m.sb("w2_lo", [P, D], F32R)
        ac = m.sb("ac", [P, 1 + 3 * KT])
        o_in, xT = m.sb("o_in", [P, KT, CH]), m.sb("xT", [P, KT, CH])
        o_hi, o_lo = m.sb("o_hi", [P, KT, CH], F32R), m.sb("o_lo", [P, KT, CH], F32R)
        x1 = m.sb("x1", [P, KT, CH])
        x1_hi, x1_lo = m.sb("x1_hi", [P, KT, CH], F32R), m.sb("x1_lo", [P, KT, CH], F32R)
        h = m.sb("h", [P, CH])
        h_hi, h_lo = m.sb("h_hi", [P, CH], F32R), m.sb("h_lo", [P, CH], F32R)
        xx = m.sb("xx", [P, KT, CH])
        x1n = [m.sb(f"x1n{i}", [P, D]) for i in range(2)]
        stats = m.sb("stats", [P, 4, 6])
        mv = m.sb("mv", [P, 4, 2])
        var, rvar, root, rstd = (m.sb(n, [P, 4]) for n in ("var", "rvar", "root", "rstd"))
        yn = [m.sb(f"yn{i}", [P, D]) for i in range(2)]
        yT = m.sb("yT", [P, KT, CH])
        y_hi, y_lo = m.sb("y_hi", [P, KT, CH], F32R), m.sb("y_lo", [P, KT, CH], F32R)
        lg = m.sb("lg", [P, 4, NE])
        top = m.sb("top", [P, 4, 8])
        top_i = m.sb("top_i", [P, 4, 8], U32)
        top_f = m.sb("top_f", [P, 4, 8])
        diff, e2 = m.sb("diff", [P, 4]), m.sb("e2", [P, 4])
        tot, wt = m.sb("tot", [P, 4]), m.sb("wt", [P, 2, 4])
        hot = m.sb("hot", [P, 4, NE])
        gates = m.sb("gates", [P, 4, NE])
        bank = [m.ps(f"bank{i}", [P, CH]) for i in range(8)]
        names = ("consts w_hi_done w_lo_done ad_loaded o_loaded xT_loaded o_hi_done o_lo_done adw_hi_done "
                 "adw_lo_done o_groups x1_done x1_hi_done x1_lo_done up_done h_done h_hi_done h_lo_done "
                 "down_done xx_done x1_turned x1n_done xx_turned rvar_ready root_ready yn_done y_turned yT_done y_hi_done y_lo_done "
                 "logits_done diff_ready e2_ready gates_done chain").split()
        sm = {n: m.sem(n) for n in names}
        x1_stored = [m.sem(f"x1_stored{i}") for i in range(2)]
        y_stored, gates_stored = m.sem("y_stored"), m.sem("gates_stored")
        passed = m.sem("passed")
        NCONST = 7
        from_one = [sm[n] for n in ("o_lo_done", "x1_done", "yT_done", "o_groups")]
        from_one += x1_stored + [y_stored, gates_stored]
        with nc.Block() as block:

            @block.gpsimd
            def _(pool):
                for sem in from_one:
                    pool.sem_inc(sem, ONE)
                with pool.Fori(0, NCH) as c:
                    pool.wait_ge(sm["o_lo_done"], c + ONE)
                    pool.sem_inc(passed)
                    pool.dma_start(o_in[:, :, :], o_d[bass.ds(c // 2 * NG, NG), :, bass.ds(c % 2 * CH, CH)]
                                   .rearrange("k p n -> p k n")).then_inc(sm["o_loaded"], 16)
                    pool.wait_ge(sm["x1_done"], c * 4 + ONE)
                    pool.sem_inc(passed)
                    pool.dma_start(xT[:, :, :], io["xT"][:, bass.ds(c * CH, CH)]
                                   .rearrange("(k p) n -> p k n", p=P)).then_inc(sm["xT_loaded"], 16)

            @block.sync
            def _(sp):
                for dst, src in (
                    (ids[:, :], io["lang"]), (w_in[:, :, :], io["bWo"].rearrange("(k p) n -> p k n", p=P)),
                    (g_in[:, :, :], io["gateT"].rearrange("(k p) n -> p k n", p=P)),
                    (cols[:, 0, :], io["bbv"]), (cols[:, 1, :], io["bbo"]), (ident[:, :], io["ident"]),
                    (iota8[:, :], io["iota8"]),
                ):
                    sp.dma_start(dst, src).then_inc(sm["consts"], 16)
                sp.wait_ge(sm["consts"], 16 * NCONST)
                with sp.Fori(0, NCH) as c:
                    lang = sp.value_load(ids[0:1, bass.ds(c // 2, 1)], min_val=0, max_val=LANGS - 1)
                    sp.wait_ge(sm["yT_done"], c * 4 + ONE)
                    sp.sem_inc(passed)
                    sp.dma_start(w1_in[:, :, :], io["W1"][bass.ds(lang, 1), :, :]
                                 .rearrange("a (k p) n -> p (a k) n", p=P)).then_inc(sm["ad_loaded"], 16)
                    sp.dma_start(w2_in[:, :], io["W2"][bass.ds(lang, 1), :, :]
                                 .rearrange("a p n -> p (a n)")).then_inc(sm["ad_loaded"], 16)
                    sp.dma_start(ac[:, :], io["adcols"][bass.ds(lang, 1), :, :]
                                 .rearrange("a p n -> p (a n)")).then_inc(sm["ad_loaded"], 16)
                    for r in range(4):
                        sp.wait_ge(sm["x1n_done"], c * 4 + (r + 1))
                        sp.sem_inc(passed)
                        sp.dma_start(x1_d[c, :, r, :], x1n[r % 2][:, :]).then_inc(x1_stored[r % 2], 16)
                    sp.wait_ge(sm["y_lo_done"], c + 1)
                    sp.sem_inc(passed)
                    sp.dma_start(y_d[0, c, :, :, :], y_hi[:, :, :].bitcast(F32)).then_inc(y_stored, 16)
                    sp.dma_start(y_d[1, c, :, :, :], y_lo[:, :, :].bitcast(F32)).then_inc(y_stored, 16)
                    sp.wait_ge(sm["gates_done"], c + 1)
                    sp.sem_inc(passed)
                    sp.dma_start(gates_d[c, :, :, :], gates[:, :, :]).then_inc(gates_stored, 16)
                for i in range(2):
                    sp.wait_ge(x1_stored[i], 16 * 2 * NCH + ONE)
                sp.wait_ge(y_stored, 32 * NCH + ONE)
                sp.wait_ge(gates_stored, 16 * NCH + ONE)

            @block.scalar
            def _(act):
                ident_fn = ACT.Identity
                act.wait_ge(sm["consts"], 16 * NCONST)
                act.activation(wo_hi[:, :, :], w_in[:, :, :], ident_fn)
                act.activation(g_hi[:, :, :], g_in[:, :, :], ident_fn).then_inc(sm["w_hi_done"], 1)
                with act.Fori(0, NCH) as c:
                    act.wait_ge(sm["o_loaded"], c * 16 + 16)
                    act.wait_ge(sm["o_groups"], c * 4 + ONE)
                    for k in range(KT):
                        last = act.activation(o_hi[:, k, :], o_in[:, k, :], ident_fn, bias=cols[:, 0, k:k + 1])
                    last.then_inc(sm["o_hi_done"], 1)
                    act.wait_ge(sm["ad_loaded"], c * 48 + 48)
                    act.activation(w1_hi[:, :, :], w1_in[:, :, :], ident_fn)
                    act.activation(w2_hi[:, :], w2_in[:, :], ident_fn).then_inc(sm["adw_hi_done"], 1)
                    for k in range(KT):
                        act.wait_ge(sm["x1_done"], c * 4 + (k + 1 + ONE))
                        act.activation(x1_hi[:, k, :], x1[:, k, :], ident_fn).then_inc(sm["x1_hi_done"], 1)
                    act.wait_ge(sm["up_done"], c + 1)
                    act.activation(h[:, :], bank[4][:, :], ACT.Relu, bias=ac[:, 0:1]).then_inc(sm["h_done"], 1)
                    act.wait_ge(sm["h_done"], c + 1)
                    act.activation(h_hi[:, :], h[:, :], ident_fn).then_inc(sm["h_hi_done"], 1)
                    for r in range(4):
                        act.wait_ge(x1_stored[r % 2], c * 32 + (16 * (r // 2) + ONE))
                        act.wait_ge(sm["x1_turned"], c * 4 + (r + 1))
                        act.activation(x1n[r % 2][:, :], bank[5 + r % 2][:, :], ACT.Copy)\
                            .then_inc(sm["x1n_done"], 1)
                    act.wait_ge(sm["rvar_ready"], c + 1)
                    act.activation(root[:, :], rvar[:, :], ACT.Sqrt).then_inc(sm["root_ready"], 1)
                    for r in range(4):
                        act.wait_ge(sm["y_turned"], c * 4 + (r + 1))
                        for k in range(KT):
                            last = act.activation(yT[:, k, r * P:(r + 1) * P],
                                                  bank[4 + r][:, k * P:(k + 1) * P], ident_fn,
                                                  scale=ac[:, 1 + KT + k:2 + KT + k],
                                                  bias=ac[:, 1 + 2 * KT + k:2 + 2 * KT + k])
                        last.then_inc(sm["yT_done"], 1)
                    act.wait_ge(sm["yT_done"], c * 4 + (4 + ONE))
                    act.wait_ge(y_stored, c * 32 + ONE)
                    act.activation(y_hi[:, :, :], yT[:, :, :], ident_fn).then_inc(sm["y_hi_done"], 1)
                    act.wait_ge(sm["diff_ready"], c + 1)
                    act.activation(e2[:, :], diff[:, :], ACT.Exp).then_inc(sm["e2_ready"], 1)

            @block.vector
            def _(dve):
                f32 = lambda t: t.bitcast(F32)
                dve.wait_ge(sm["w_hi_done"], 1)
                dve.tensor_tensor(wo_lo[:, :, :], w_in[:, :, :], f32(wo_hi[:, :, :]), ALU.subtract)
                dve.tensor_tensor(g_lo[:, :, :], g_in[:, :, :], f32(g_hi[:, :, :]), ALU.subtract)\
                    .then_inc(sm["w_lo_done"], 1)
                NCHAIN = 7 + 12
                with dve.Fori(0, NCH) as c:
                    links = [0]

                    def then(ins):
                        links[0] += 1
                        ins.then_inc(sm["chain"], 1)
                        dve.wait_ge(sm["chain"], c * NCHAIN + links[0])
                        dve.sem_inc(passed)

                    dve.wait_ge(sm["o_hi_done"], c + 1)
                    for k in range(KT):
                        last = dve.scalar_tensor_tensor(out=o_lo[:, k, :], in0=o_in[:, k, :],
                                                        scalar=cols[:, 0, k:k + 1], in1=f32(o_hi[:, k, :]),
                                                        op0=ALU.add, op1=ALU.subtract)
                    last.then_inc(sm["o_lo_done"], 1)
                    dve.wait_ge(sm["adw_hi_done"], c + 1)
                    dve.tensor_tensor(w1_lo[:, :, :], w1_in[:, :, :], f32(w1_hi[:, :, :]), ALU.subtract)
                    dve.tensor_tensor(w2_lo[:, :], w2_in[:, :], f32(w2_hi[:, :]), ALU.subtract)\
                        .then_inc(sm["adw_lo_done"], 1)
                    dve.wait_ge(sm["xT_loaded"], c * 16 + 16)
                    for k in range(KT):
                        dve.wait_ge(sm["o_groups"], c * 4 + (k + 1 + ONE))
                        dve.scalar_tensor_tensor(out=x1[:, k, :], in0=bank[k][:, :], scalar=cols[:, 1, k:k + 1],
                                                 in1=xT[:, k, :], op0=ALU.add, op1=ALU.add)\
                            .then_inc(sm["x1_done"], 1)
                    for k in range(KT):
                        dve.wait_ge(sm["x1_hi_done"], c * 4 + (k + 1))
                        dve.tensor_tensor(x1_lo[:, k, :], x1[:, k, :], f32(x1_hi[:, k, :]), ALU.subtract)\
                            .then_inc(sm["x1_lo_done"], 1)
                    dve.wait_ge(sm["h_hi_done"], c + 1)
                    dve.tensor_tensor(h_lo[:, :], h[:, :], f32(h_hi[:, :]), ALU.subtract)\
                        .then_inc(sm["h_lo_done"], 1)
                    for k in range(KT):
                        dve.wait_ge(sm["down_done"], c * 4 + (k + 1))
                        dve.scalar_tensor_tensor(out=xx[:, k, :], in0=bank[k][:, :], scalar=ac[:, 1 + k:2 + k],
                                                 in1=x1[:, k, :], op0=ALU.add, op1=ALU.add)\
                            .then_inc(sm["xx_done"], 1)
                    for r in range(4):
                        dve.wait_ge(sm["xx_turned"], c * 4 + (r + 1))
                        dve.sem_inc(passed)
                        last = dve.bn_stats(stats[:, r, :], bank[r][:, :])
                    then(last)
                    for r in range(4):
                        last = dve.bn_aggr(mv[:, r, :], stats[:, r, :])
                    then(last)
                    then(dve.tensor_scalar(var[:, :], mv[:, :, 1], LN_EPS, None, ALU.add))
                    dve.reciprocal(rvar[:, :], var[:, :]).then_inc(sm["rvar_ready"], 1)
                    dve.wait_ge(sm["root_ready"], c + 1)
                    then(dve.tensor_tensor(rstd[:, :], root[:, :], root[:, :], ALU.mult))
                    then(dve.tensor_tensor(rstd[:, :], rstd[:, :], var[:, :], ALU.mult))
                    then(dve.tensor_scalar(rstd[:, :], rstd[:, :], -0.5, 1.5, ALU.mult, ALU.add))
                    then(dve.tensor_tensor(rstd[:, :], rstd[:, :], root[:, :], ALU.mult))
                    for r in range(4):
                        if r >= 2:
                            dve.wait_ge(sm["y_turned"], c * 4 + (r - 1))
                        dve.tensor_scalar(yn[r % 2][:, :], bank[r][:, :], mv[:, r, 0:1], rstd[:, r:r + 1],
                                          ALU.subtract, ALU.mult).then_inc(sm["yn_done"], 1)
                    dve.wait_ge(sm["y_hi_done"], c + 1)
                    dve.tensor_tensor(y_lo[:, :, :], yT[:, :, :], f32(y_hi[:, :, :]), ALU.subtract)\
                        .then_inc(sm["y_lo_done"], 1)
                    dve.wait_ge(sm["logits_done"], c + 1)
                    then(dve.tensor_copy(lg[:, :, :], bank[4][:, 0:4 * NE].rearrange("p (r e) -> p r e", r=4)))
                    for r in range(4):
                        last = dve.max(top[:, r, :], lg[:, r, :])
                    then(last)
                    for r in range(4):
                        last = dve.max_index(top_i[:, r, :], top[:, r, :], lg[:, r, :])
                    then(last)
                    dve.tensor_tensor(diff[:, :], top[:, :, 1], top[:, :, 0], ALU.subtract)\
                        .then_inc(sm["diff_ready"], 1)
                    then(dve.tensor_copy(top_f[:, :, :], top_i[:, :, :]))
                    dve.wait_ge(sm["e2_ready"], c + 1)
                    then(dve.tensor_scalar(tot[:, :], e2[:, :], 1.0, None, ALU.add))
                    then(dve.reciprocal(wt[:, 0, :], tot[:, :]))
                    then(dve.tensor_tensor(wt[:, 1, :], wt[:, 0, :], e2[:, :], ALU.mult))
                    dve.wait_ge(gates_stored, c * 16 + ONE)
                    for r in range(4):
                        last = dve.tensor_scalar(hot[:, r, :], iota8[:, :], top_f[:, r, 1:2], wt[:, 1, r:r + 1],
                                                 ALU.is_equal, ALU.mult)
                    then(last)
                    for r in range(4):
                        last = dve.tensor_scalar(gates[:, r, :], iota8[:, :], top_f[:, r, 0:1],
                                                 wt[:, 0, r:r + 1], ALU.is_equal, ALU.mult)
                    then(last)
                    dve.tensor_tensor(gates[:, :, :], gates[:, :, :], hot[:, :, :], ALU.add)\
                        .then_inc(sm["gates_done"], 1)
                    for _ in range(NCHAIN - links[0]):
                        dve.sem_inc(sm["chain"], 1)

            @block.tensor
            def _(pe):
                pe.wait_ge(sm["w_lo_done"], 1)

                def product(out, pairs):
                    n = len(pairs)
                    for i, (lhs, rhs) in enumerate(pairs):
                        last = pe.matmul(out, lhs, rhs, start=(i == 0), stop=(i == n - 1))
                    return last

                def turn(dst, src):
                    for k in range(KT):
                        last = pe.transpose(dst[:, k * P:(k + 1) * P], src(k), ident[:, :])
                    return last

                def tile(k):
                    return slice(k * P, (k + 1) * P)

                with pe.Fori(0, NCH) as c:
                    pe.wait_ge(sm["o_lo_done"], c + (1 + ONE))
                    for j in range(KT):
                        product(bank[j][:, :], [(w[:, k, tile(j)], a[:, k, :]) for k in range(KT)
                                                for w, a in ((wo_hi, o_hi), (wo_hi, o_lo), (wo_lo, o_hi))])\
                            .then_inc(sm["o_groups"], 1)
                    pe.wait_ge(sm["adw_lo_done"], c + 1)
                    pe.wait_ge(sm["x1_lo_done"], c * 4 + 4)
                    product(bank[4][:, :], [(w[:, k, :], a[:, k, :]) for k in range(KT)
                                            for w, a in ((w1_hi, x1_hi), (w1_hi, x1_lo), (w1_lo, x1_hi))])\
                        .then_inc(sm["up_done"], 1)
                    for r in range(4):
                        if r < 2:
                            turn(bank[5 + r % 2], lambda k: x1[:, k, tile(r)]).then_inc(sm["x1_turned"], 1)
                    pe.wait_ge(sm["h_lo_done"], c + 1)
                    for j in range(KT):
                        product(bank[j][:, :], [(w[:, tile(j)], a[:, :])
                                                for w, a in ((w2_hi, h_hi), (w2_hi, h_lo), (w2_lo, h_hi))])\
                            .then_inc(sm["down_done"], 1)
                    for r in range(2, 4):
                        pe.wait_ge(sm["x1n_done"], c * 4 + (r - 1))
                        turn(bank[5 + r % 2], lambda k: x1[:, k, tile(r)]).then_inc(sm["x1_turned"], 1)
                    pe.wait_ge(sm["xx_done"], c * 4 + 4)
                    for r in range(4):
                        turn(bank[r], lambda k: xx[:, k, tile(r)]).then_inc(sm["xx_turned"], 1)
                    pe.wait_ge(sm["x1n_done"], c * 4 + 4)
                    for r in range(4):
                        pe.wait_ge(sm["yn_done"], c * 4 + (r + 1))
                        turn(bank[4 + r], lambda k: yn[r % 2][:, tile(k)]).then_inc(sm["y_turned"], 1)
                    pe.wait_ge(sm["y_lo_done"], c + 1)
                    for r in range(4):
                        last = product(bank[4][:, r * NE:(r + 1) * NE],
                                       [(a[:, k, tile(r)], w[:, k, :]) for k in range(KT)
                                        for w, a in ((g_hi, y_hi), (g_hi, y_lo), (g_lo, y_hi))])
                    last.then_inc(sm["logits_done"], 1)


def experts_block(nc, io, x1_d, y_d, gates_d, out_d):
    with ExitStack() as ctx:
        m = Memory(nc, ctx, "ex")
        w_hi = [m.sb(f"w_hi{e}", [P, KT, D], F32R) for e in range(NE)]
        w_lo = [m.sb(f"w_lo{e}", [P, KT, D], F32R) for e in range(NE)]
        w_in = m.sb("w_in", [P, KT, D])
        y = [[m.sb(f"y{s}_{a}", [P, KT, CH], F32R) for a in range(2)] for s in range(2)]
        x1 = [m.sb(f"x1_{s}", [P, 4, D]) for s in range(2)]
        gates = [m.sb(f"gates{s}", [P, 4, NE]) for s in range(2)]
        acc = [m.sb(f"acc{i}", [P, D]) for i in range(2)]
        out_sb = [m.sb(f"out_sb{i}", [P, D]) for i in range(2)]
        NBANK = 8
        bank = [m.ps(f"bank{i}", [P, D]) for i in range(NBANK)]
        w_loaded, w_hi_done, w_lo_done = m.sem("w_loaded"), m.sem("w_hi_done"), m.sem("w_lo_done")
        loaded = [m.sem(f"loaded{s}") for s in range(2)]
        group_done, added = m.sem("group_done"), m.sem("added")
        chunk_done = [m.sem(f"chunk_done{s}") for s in range(2)]
        summed = [m.sem(f"summed{s}") for s in range(2)]
        stored = [m.sem(f"stored{i}") for i in range(2)]
        passed = m.sem("passed")
        GC = 4 * NE
        GT = 2 * GC
        with nc.Block() as block:

            @block.gpsimd
            def _(pool):
                for sem in [added] + chunk_done + summed + stored:
                    pool.sem_inc(sem, ONE)
                with pool.Fori(0, B) as b:
                    for s in range(2):
                        pool.wait_ge(chunk_done[s], b + ONE)
                        pool.sem_inc(passed)
                        pool.wait_ge(summed[s], b + ONE)
                        pool.sem_inc(passed)
                        c = b * 2 + s
                        for a in range(2):
                            pool.dma_start(y[s][a][:, :, :].bitcast(F32), y_d[a, c, :, :, :]).then_inc(loaded[s], 16)
                        pool.dma_start(x1[s][:, :, :], x1_d[c, :, :, :]).then_inc(loaded[s], 16)
                        pool.dma_start(gates[s][:, :, :], gates_d[c, :, :, :]).then_inc(loaded[s], 16)

            @block.sync
            def _(sp):
                for e in range(NE):
                    sp.wait_ge(w_lo_done, e)
                    sp.dma_start(w_in[:, :, :], io["weight"][e, :, :].rearrange("(k p) n -> p k n", p=P))\
                        .then_inc(w_loaded, 16)
                with sp.Fori(0, B) as b:
                    for s in range(2):
                        for r in range(4):
                            sp.wait_ge(added, b * GT + (s * GC + (r + 1) * NE + ONE))
                            sp.sem_inc(passed)
                            sp.dma_start(out_d[b, s * CH + r * P:s * CH + (r + 1) * P, :], out_sb[r % 2][:, :])\
                                .then_inc(stored[r % 2], 16)
                for i in range(2):
                    sp.wait_ge(stored[i], 16 * 4 * B + ONE)

            @block.scalar
            def _(act):
                for e in range(NE):
                    act.wait_ge(w_loaded, 16 * (e + 1))
                    act.activation(w_hi[e][:, :, :], w_in[:, :, :], ACT.Identity).then_inc(w_hi_done, 1)

            @block.vector
            def _(dve):
                for e in range(NE):
                    dve.wait_ge(w_hi_done, e + 1)
                    dve.tensor_tensor(w_lo[e][:, :, :], w_in[:, :, :], w_hi[e][:, :, :].bitcast(F32),
                                      ALU.subtract).then_inc(w_lo_done, 1)
                with dve.Fori(0, B) as b:
                    for g in range(GT):
                        s, r, e = g // GC, g // NE % 4, g % NE
                        if g % GC == 0:
                            dve.wait_ge(loaded[s], b * 64 + 64)
                        if e == NE - 1:
                            dve.wait_ge(stored[r % 2], b * 64 + (16 * ((s * 4 + r) // 2) + ONE))
                        dve.wait_ge(added, b * GT + (g + ONE))
                        dve.wait_ge(group_done, b * GT + (g + 1))
                        src = x1[s][:, r, :] if e == 0 else acc[(e + 1) % 2][:, :]
                        dst = out_sb[r % 2][:, :] if e == NE - 1 else acc[e % 2][:, :]
                        dve.scalar_tensor_tensor(out=dst, in0=bank[g % NBANK][:, :], scalar=gates[s][:, r, e:e + 1],
                                                 in1=src, op0=ALU.mult, op1=ALU.add).then_inc(added, 1)
                        if g % GC == GC - 1:
                            dve.drain().then_inc(summed[s], 1)

            @block.tensor
            def _(pe):
                with pe.Fori(0, B) as b:
                    for g in range(GT):
                        s, r, e = g // GC, g // NE % 4, g % NE
                        if g % GC == 0:
                            pe.wait_ge(loaded[s], b * 64 + 64)
                        if r == 0 and s == 0:
                            pe.wait_ge(w_lo_done, e + 1)
                        if g >= NBANK:
                            pe.wait_ge(added, b * GT + (g - NBANK + 1 + ONE))
                        else:
                            pe.wait_ge(added, b * GT + ONE)
                        n = 0
                        for k in range(KT):
                            for a, w in ((0, w_hi), (0, w_lo), (1, w_hi)):
                                last = pe.matmul(bank[g % NBANK][:, :], y[s][a][:, k, r * P:(r + 1) * P],
                                                 w[e][:, k, :], start=(n == 0), stop=(n == 3 * KT - 1))
                                n += 1
                        last.then_inc(group_done, 1)
                        if g % GC == GC - 1:
                            pe.drain().then_inc(chunk_done[s], 1)


def build_program(nc, io, out_d):
    def scratch(name, shape):
        return nc.dram_tensor(name, shape, F32, kind="Internal").ap()

    q_d, k_d = scratch("q_parts", (2, NI, P, S)), scratch("k_parts", (2, NI, P, S))
    v_d = scratch("values", (NI, S, P))
    q2_d, k2_d = scratch("q2_parts", (2, NI, P, S)), scratch("k2_parts", (2, NI, P, S))
    v2_d = scratch("values2", (NI, S, P))
    bias_d = scratch("prior_bias", (B, S, S))
    o_d, o2_d = scratch("attended", (NI, P, S)), scratch("attended2", (NI, P, S))
    skew_d = scratch("position_scores", (8, P * UW))
    x1_d = scratch("x1", (B * 2, P, 4, D))
    y_d = scratch("normed", (2, B * 2, P, KT, CH))
    gates_d = scratch("gates", (B * 2, P, 4, NE))

    prior_block(nc, io, bias_d)
    projection_block(
        nc, io, "pa",
        lambda b, s: io["xT"][:, bass.ds(b * S + s * CH, CH)].rearrange("(k p) n -> p k n", p=P),
        (io["aWq"], io["aWk"], io["aWv"]), (io["zero_cols"], io["zero_cols"], io["abq"], io["abk"]),
        None, q_d, k_d, v_d)
    attention_block(nc, io, "aa", q_d, k_d, v_d, o_d, bias_d=bias_d)
    projection_block(
        nc, io, "pb",
        lambda b, s: o_d[bass.ds(b * NG, NG), :, s * CH:(s + 1) * CH].rearrange("k p n -> p k n"),
        (io["bWq"], io["bWk"], io["bWv"]), (io["abv"], io["abo"], io["bbq"], io["bbk"]),
        (io["aWo"],), q2_d, k2_d, v2_d)
    attention_block(nc, io, "ab", q2_d, k2_d, v2_d, o2_d, skew_d=skew_d)
    adapter_block(nc, io, o2_d, x1_d, y_d, gates_d)
    experts_block(nc, io, x1_d, y_d, gates_d, out_d)




def _layout(inputs):
    import numpy as np

    a = {k: np.asarray(v) for k, v in inputs.items()}

    def cols(v):
        return v.reshape(-1, P).T

    x = a["x"].reshape(B * S, D)
    out = {"xT": x.T}
    for short, name in (("a", "L0_cond_"), ("b", "L0_attn_")):
        for n in "qkvo":
            out[f"{short}W{n}"] = a[f"{name}W{n}"].T
            out[f"{short}b{n}"] = cols(a[f"{name}b{n}"])
    w = np.arange(RELW)
    out["relT"] = a["L0_attn_rel_table"][np.clip(NREL - 1 - (w - MAXLEN), 0, NREL - 1)].T
    out["zero_cols"] = np.zeros((P, KT), np.float32)
    out["ident"] = np.eye(P, dtype=np.float32)
    out["iota1"] = np.broadcast_to(np.arange(1, S + 1, dtype=np.float32), (P, S))
    out["iota8"] = np.broadcast_to(np.arange(NE, dtype=np.float32), (P, NE))
    out["prior_idx"] = a["itok_Sx32_0_1023"]
    out["prior_valid"] = a["mask_Sx32_bk1"].view(np.uint8)
    out["prior_mask"] = a["mask_SxS_bk0"].view(np.int32)
    out["uprev"] = np.broadcast_to(a["condB_uprev"].reshape(1, B), (P, B))
    out["lang"] = a["itok_B_0_8"].reshape(1, B)
    out["W1"], out["W2"] = a["L0_cond2_W1"], a["L0_cond2_W2"]
    by_p = [a["L0_cond2_b1"].reshape(LANGS, 1, P)]
    by_p += [a[f"L0_cond2_{n}"].reshape(LANGS, KT, P) for n in ("b2", "gamma", "beta")]
    out["adcols"] = np.concatenate(by_p, axis=1).transpose(0, 2, 1)
    out["gateT"] = a["L0_ffn_gate_w"].T
    out["weight"] = a["L0_ffn_weight"]
    return {k: np.ascontiguousarray(v) for k, v in out.items()}


def kernel(**inputs):
    import concourse.bacc as _bacc
    from concourse.bass_utils import run_bass_kernel_spmd as _run

    nc = _bacc.Bacc("TRN2", target_bir_lowering=False, num_devices=1)
    arrays, io = {}, {}
    for name, a in _layout(inputs).items():
        arrays[f"in_{name}"] = a
        io[name] = nc.dram_tensor(f"in_{name}", a.shape, mybir.dt.from_np(a.dtype), kind="ExternalInput").ap()
    out_d = nc.dram_tensor("out_0", (B, S, D), F32, kind="ExternalOutput").ap()
    build_program(nc, io, out_d)
    r = _run(nc, [arrays], core_ids=[0])
    return r.results[0]["out_0"]
```

```python
from contextlib import ExitStack

import concourse.bass as bass
from concourse import mybir

F32 = mybir.dt.float32
F32R = mybir.dt.float32r
F16 = mybir.dt.float16
BF16 = mybir.dt.bfloat16
I32 = mybir.dt.int32
U8 = mybir.dt.uint8
U32 = mybir.dt.uint32
ALU = mybir.AluOpType
ACT = mybir.ActivationFunctionType

P = 128
B, S, D = 4, 1024, 512
H, DH = 16, 32
HG = P // DH
NG = H // HG
KT = D // P
CH = 512
NQ = S // P
NI = B * NG
SCALE = float(DH) ** -0.5
NSPARSE = 32
LAM_MAX, ALPHA, THRESHOLD = 10.0, 5.0, 1.0
MAXLEN = 512
NREL = 2 * MAXLEN - 1
RELW = 2 * S
UW = S + P
NE, TOPK = 8, 2
LANGS, AD = 10, 128
LN_EPS = 1e-5
MASKED = -1e30
ONE = 1


class Memory:

    def __init__(self, nc, ctx, tag):
        self.nc, self.ctx, self.tag = nc, ctx, tag
        self.sems = []
        ctx.callback(self.free_semaphores)

    def sb(self, name, shape, dt=F32):
        return self.ctx.enter_context(self.nc.sbuf_tensor(f"{self.tag}_{name}", shape, dt))

    def ps(self, name, shape, dt=F32):
        return self.ctx.enter_context(self.nc.psum_tensor(f"{self.tag}_{name}", shape, dt))

    def sem(self, name):
        self.sems.append(self.nc.alloc_semaphore(f"{self.tag}_{name}"))
        return self.sems[-1]

    def free_semaphores(self):
        self.nc.clear_and_free_semaphores(self.sems)
        self.nc.all_engine_barrier()


def prior_block(nc, io, bias_d):
    NSAME = 8
    with ExitStack() as ctx:
        m = Memory(nc, ctx, "pr")
        iota1 = m.sb("iota1", [P, S])
        named_i = m.sb("named_i", [P, NQ, NSPARSE], I32)
        valid_u = m.sb("valid_u", [P, NQ, NSPARSE], U8)
        named_f = m.sb("named_f", [P, NQ, NSPARSE])
        valid_f = m.sb("valid_f", [P, NQ, NSPARSE])
        key1 = m.sb("key1", [P, NQ, NSPARSE])
        mask_w = m.sb("mask_w", [P, NQ, S // 4], I32)
        mask_u = mask_w[:, :, :].bitcast(U8)
        up = m.sb("up", [P, B])
        lam = m.sb("lam", [P, B])
        sparse = m.sb("sparse", [P, B])
        dense_lam = m.sb("dense_lam", [P, B])
        lam1 = m.sb("lam1", [P, B])
        is_dense = m.sb("is_dense", [P, B])
        iota16 = m.sb("iota16", [P, S], F16)
        ident = m.sb("ident", [P, P])
        ident16 = m.sb("ident16", [P, P], BF16)
        same = m.sb("same", [P, NSAME, S], BF16)
        floor = m.sb("floor", [P, 2, S])
        lnc = m.sb("lnc", [P, 2, S])
        pen = m.sb("pen", [P, 2, S])
        off = m.sb("off", [P, S])
        dense_part = m.sb("dense_part", [P, B, S])
        sparse_part = m.sb("sparse_part", [P, B, S])
        bias = m.sb("bias", [P, B, S])
        loaded, lam_exp, chain = m.sem("loaded"), m.sem("lam_exp"), m.sem("chain")
        floor_ready, ln_ready, bias_ready = m.sem("floor_ready"), m.sem("ln_ready"), m.sem("bias_ready")
        stored = m.sem("stored")
        same_ready, same_used = m.sem("same_ready"), m.sem("same_used")
        count_used = m.sem("count_used")
        off_ready, part_ready, sparse_ready = m.sem("off_ready"), m.sem("part_ready"), m.sem("sparse_ready")
        count = [m.ps(f"count{i}", [P, S]) for i in range(2)]
        with nc.Block() as block:

            @block.sync
            def _(sp):
                for dst, src in (
                    (iota1[:, :], io["iota1"]),
                    (named_i[:, :, :], io["prior_idx"].rearrange("(t p) j -> p t j", p=P)),
                    (valid_u[:, :, :], io["prior_valid"].rearrange("(t p) j -> p t j", p=P)),
                    (mask_w[:, :, :], io["prior_mask"].rearrange("(t p) k -> p t k", p=P)),
                    (up[:, :], io["uprev"]),
                    (ident[:, :], io["ident"]),
                ):
                    sp.dma_start(dst, src).then_inc(loaded, 16)
                for t in range(NQ):
                    for b in range(B):
                        sp.wait_ge(bias_ready, t * B + b + 1)
                        sp.dma_start(bias_d[b, t * P:(t + 1) * P, :], bias[:, b, :]).then_inc(stored, 16)
                sp.wait_ge(stored, 16 * B * NQ)

            @block.scalar
            def _(act):
                act.wait_ge(loaded, 96)
                act.activation(lam[:, :], up[:, :], ACT.Exp, scale=-ALPHA).then_inc(lam_exp, 1)
                for t in range(NQ):
                    act.wait_ge(floor_ready, t + 1)
                    act.activation(lnc[:, t % 2, :], floor[:, t % 2, :], ACT.Ln).then_inc(ln_ready, 1)
                    act.wait_ge(off_ready, t + 1)
                    if t > 0:
                        act.wait_ge(bias_ready, B * t)
                    for b in range(B):
                        act.activation(dense_part[:, b, :], off[:, :], ACT.Copy, scale=dense_lam[:, b:b + 1])\
                            .then_inc(part_ready, 1)
                        if b == 0:
                            act.wait_ge(sparse_ready, t + 1)
                        act.activation(sparse_part[:, b, :], lnc[:, t % 2, :], ACT.Copy, scale=sparse[:, b:b + 1])\
                            .then_inc(part_ready, 1)

            @block.vector
            def _(dve):
                done = [0]

                def then(ins):
                    done[0] += 1
                    ins.then_inc(chain, 1)
                    dve.wait_ge(chain, done[0])

                dve.wait_ge(loaded, 96)
                dve.tensor_copy(iota16[:, :], iota1[:, :])
                dve.tensor_copy(ident16[:, :], ident[:, :])
                dve.tensor_copy(named_f[:, :, :], named_i[:, :, :])
                then(dve.tensor_copy(valid_f[:, :, :], valid_u[:, :, :]))
                then(dve.scalar_tensor_tensor(out=key1[:, :, :], in0=named_f[:, :, :], scalar=1.0,
                                              in1=valid_f[:, :, :], op0=ALU.add, op1=ALU.mult))
                dve.wait_ge(lam_exp, 1)
                then(dve.tensor_scalar(lam1[:, :], lam[:, :], LAM_MAX, None, ALU.mult))
                dve.tensor_scalar(sparse[:, :], lam1[:, :], THRESHOLD, None, ALU.is_ge)
                then(dve.tensor_scalar(is_dense[:, :], lam1[:, :], THRESHOLD, None, ALU.is_lt))
                then(dve.scalar_tensor_tensor(out=dense_lam[:, :], in0=lam1[:, :], scalar=THRESHOLD,
                                              in1=is_dense[:, :], op0=ALU.min, op1=ALU.mult))

                def compare(t):
                    for j in range(NSPARSE):
                        n = t * NSPARSE + j
                        if n >= NSAME:
                            dve.wait_ge(same_used, n - NSAME + 1)
                        dve.tensor_scalar(same[:, n % NSAME, :], iota16[:, :], key1[:, t, j:j + 1], None,
                                          ALU.is_equal).then_inc(same_ready, 1)

                compare(0)
                for t in range(NQ):
                    w = t % 2
                    if t + 1 < NQ:
                        compare(t + 1)
                    dve.wait_ge(same_used, NSPARSE * (t + 1))
                    dve.tensor_scalar(floor[:, w, :], count[w][:, :], 0.5, None, ALU.max).then_inc(floor_ready, 1)
                    dve.tensor_scalar(pen[:, w, :], count[w][:, :], 0.5, MASKED, ALU.is_lt, ALU.mult)\
                        .then_inc(count_used, 1)
                    if t > 0:
                        dve.wait_ge(part_ready, 2 * B * t)
                    dve.tensor_scalar(off[:, :], mask_u[:, t, :], 1.0, 1.0 / SCALE,
                                      ALU.subtract, ALU.mult).then_inc(off_ready, 1)
                    dve.wait_ge(ln_ready, t + 1)
                    dve.wait_ge(count_used, t + 1)
                    dve.scalar_tensor_tensor(out=lnc[:, w, :], in0=lnc[:, w, :], scalar=1.0 / SCALE,
                                             in1=pen[:, w, :], op0=ALU.mult, op1=ALU.add)\
                        .then_inc(sparse_ready, 1)

            @block.gpsimd
            def _(pool):
                for t in range(NQ):
                    if t > 0:
                        pool.wait_ge(stored, 16 * B * t)
                    for b in range(B):
                        pool.wait_ge(part_ready, 2 * (t * B + b + 1))
                        pool.tensor_tensor(bias[:, b, :], sparse_part[:, b, :], dense_part[:, b, :], ALU.add)\
                            .then_inc(bias_ready, 1)

            @block.tensor
            def _(pe):
                for t in range(NQ):
                    if t >= 2:
                        pe.wait_ge(count_used, t - 1)
                    for j in range(NSPARSE):
                        n = t * NSPARSE + j
                        pe.wait_ge(same_ready, n + 1)
                        for c in range(2):
                            last = pe.matmul(count[t % 2][:, c * CH:(c + 1) * CH], ident16[:, :],
                                             same[:, n % NSAME, c * CH:(c + 1) * CH],
                                             start=(j == 0), stop=(j == NSPARSE - 1))
                        last.then_inc(same_used, 1)


def projection_block(nc, io, tag, source, weights, biases, out, q_d, k_d, v_d):
    wq_d, wk_d, wv_d = weights
    stages = (["o"] if out else []) + ["q", "k", "v"]
    with ExitStack() as ctx:
        m = Memory(nc, ctx, tag)
        w_in = [m.sb(f"w_in{i}", [P, KT, D]) for i in range(2)]
        w_hi = {n: m.sb(f"w{n}_hi", [P, KT, D], F32R) for n in stages}
        w_lo = {n: m.sb(f"w{n}_lo", [P, KT, D], F32R) for n in stages}
        cols = m.sb("cols", [P, 4, KT])
        x_in = [m.sb(f"x_in{s}", [P, KT, CH]) for s in range(2)]
        x_hi = [m.sb(f"x_hi{s}", [P, KT, CH], F32R) for s in range(2)]
        x_lo = [m.sb(f"x_lo{s}", [P, KT, CH], F32R) for s in range(2)]
        c_hi = m.sb("c_hi", [P, KT, CH], F32R)
        c_lo = m.sb("c_lo", [P, KT, CH], F32R)
        NST = 4
        st_hi = [m.sb(f"st_hi{i}", [P, CH], F32R) for i in range(NST)]
        st_lo = [m.sb(f"st_lo{i}", [P, CH], F32R) for i in range(NST)]
        st_v = [m.sb(f"st_v{i}", [P, CH]) for i in range(NST)]
        NBANK = 4
        bank = [m.ps(f"bank{i}", [P, CH]) for i in range(NBANK)]
        w_loaded = [m.sem(f"w_loaded{i}") for i in range(2)]
        w_hi_done, w_lo_done, cols_loaded = m.sem("w_hi_done"), m.sem("w_lo_done"), m.sem("cols_loaded")
        x_loaded = [m.sem(f"x_loaded{s}") for s in range(2)]
        x_hi_done = m.sem("x_hi_done")
        x_lo_done = [m.sem(f"x_lo_done{s}") for s in range(2)]
        chunk_done = [m.sem(f"chunk_done{s}") for s in range(2)]
        group_done, hi_done, bank_free = m.sem("group_done"), m.sem("hi_done"), m.sem("bank_free")
        stored = [m.sem(f"stored{i}") for i in range(NST)]
        passed = io["passed"]

        groups = [(n, j) for n in stages for j in range(4)]
        body = [(s, n, j) for s in range(2) for n, j in groups]
        GT = len(body)
        exported = [g for g, (_, n, _) in enumerate(body) if n != "o"]
        with_hi = [g for g, (_, n, _) in enumerate(body) if n != "v"]
        NEX, NHI = len(exported), len(with_hi)
        w_d = {"o": out[0] if out else None, "q": wq_d, "k": wk_d, "v": wv_d}
        bias_col = {"o": 1, "q": 2, "k": 3}

        with nc.Block() as block:

            @block.gpsimd
            def _(pool):
                for sem in x_lo_done + chunk_done + stored:
                    pool.sem_inc(sem, ONE)
                with pool.Fori(0, B) as b:
                    for s in range(2):
                        pool.wait_ge(x_lo_done[s], b + ONE)
                        pool.sem_inc(passed)
                        pool.dma_start(x_in[s][:, :, :], source(b, s)).then_inc(x_loaded[s], 16)

            @block.sync
            def _(sp):
                for n, src in enumerate(biases):
                    sp.dma_start(cols[:, n, :], src).then_inc(cols_loaded, 16)
                for n, name in enumerate(stages):
                    sp.wait_ge(w_lo_done, max(0, n - 1))
                    sp.dma_start(w_in[n % 2][:, :, :], w_d[name].rearrange("(k p) n -> p k n", p=P))\
                        .then_inc(w_loaded[n % 2], 16)
                with sp.Fori(0, B) as b:
                    for e, g in enumerate(exported):
                        s, name, j = body[g]
                        i = e % NST
                        sp.wait_ge(bank_free, b * GT + (NBANK + g + 1))
                        sp.sem_inc(passed)
                        if name == "v":
                            rows = slice(s * CH + j * P, s * CH + (j + 1) * P)
                            for a in range(2):
                                sp.dma_start(v_d[bass.ds(b * NG + 2 * a, 2), rows, :].rearrange("g p c -> p g c"),
                                             st_v[i][:, 2 * a * P:2 * (a + 1) * P].rearrange("p (g c) -> p g c", g=2))\
                                    .then_inc(stored[i], 16)
                        else:
                            d = q_d if name == "q" else k_d
                            for a, st in enumerate((st_hi, st_lo)):
                                sp.dma_start(d[a, b * NG + j, :, s * CH:(s + 1) * CH],
                                             st[i][:, :].bitcast(F32)).then_inc(stored[i], 16)
                for i in range(NST):
                    sp.wait_ge(stored[i], 32 * B * NEX // NST + ONE)

            @block.scalar
            def _(act):
                for n, name in enumerate(stages):
                    act.wait_ge(w_loaded[n % 2], 16 * (n // 2 + 1))
                    act.activation(w_hi[name][:, :, :], w_in[n % 2][:, :, :], ACT.Identity)\
                        .then_inc(w_hi_done, 1)
                act.wait_ge(cols_loaded, 16 * len(biases))

                def split(b, s):
                    act.wait_ge(x_loaded[s], b * 16 + 16)
                    act.wait_ge(chunk_done[s], b + ONE)
                    for k in range(KT):
                        act.activation(x_hi[s][:, k, :], x_in[s][:, k, :], ACT.Identity,
                                       bias=cols[:, 0, k:k + 1]).then_inc(x_hi_done, 1)

                with act.Fori(0, B) as b:
                    split(b, 0)
                    for g, (s, name, j) in enumerate(body):
                        if g == GT // 4:
                            split(b, 1)
                        if name == "v":
                            continue
                        if name != "o":
                            e = exported.index(g)
                            act.wait_ge(stored[e % NST], b * (32 * NEX // NST) + (32 * (e // NST) + ONE))
                            dst = st_hi[e % NST][:, :]
                        else:
                            dst = c_hi[:, j, :]
                        act.wait_ge(group_done, b * GT + (g + 1))
                        act.activation(dst, bank[g % NBANK][:, :], ACT.Identity,
                                       bias=cols[:, bias_col[name], j:j + 1]).then_inc(hi_done, 1)

            @block.vector
            def _(dve):
                for n, name in enumerate(stages):
                    dve.wait_ge(w_hi_done, n + 1)
                    dve.tensor_tensor(w_lo[name][:, :, :], w_in[n % 2][:, :, :],
                                      w_hi[name][:, :, :].bitcast(F32), ALU.subtract).then_inc(w_lo_done, 1)
                dve.wait_ge(cols_loaded, 16 * len(biases))
                dve.sem_inc(bank_free, NBANK)

                def split(b, s):
                    dve.wait_ge(x_hi_done, b * (2 * KT) + (s + 1) * KT)
                    for k in range(KT):
                        ins = dve.scalar_tensor_tensor(out=x_lo[s][:, k, :], in0=x_in[s][:, k, :],
                                                       scalar=cols[:, 0, k:k + 1],
                                                       in1=x_hi[s][:, k, :].bitcast(F32),
                                                       op0=ALU.add, op1=ALU.subtract)
                    ins.then_inc(x_lo_done[s], 1)

                with dve.Fori(0, B) as b:
                    split(b, 0)
                    for g, (s, name, j) in enumerate(body):
                        if g == GT // 4:
                            split(b, 1)
                        src = bank[g % NBANK][:, :]
                        if name == "v":
                            e = exported.index(g)
                            dve.wait_ge(stored[e % NST], b * (32 * NEX // NST) + (32 * (e // NST) + ONE))
                            dve.wait_ge(group_done, b * GT + (g + 1))
                            dve.tensor_copy(st_v[e % NST][:, :], src).then_inc(bank_free, 1)
                            continue
                        if name == "o":
                            hi, lo = c_hi[:, j, :], c_lo[:, j, :]
                        else:
                            e = exported.index(g)
                            hi, lo = st_hi[e % NST][:, :], st_lo[e % NST][:, :]
                        dve.wait_ge(hi_done, b * NHI + (with_hi.index(g) + 1))
                        dve.scalar_tensor_tensor(out=lo, in0=src, scalar=cols[:, bias_col[name], j:j + 1],
                                                 in1=hi.bitcast(F32), op0=ALU.add, op1=ALU.subtract)\
                            .then_inc(bank_free, 1)

            @block.tensor
            def _(pe):
                pe.wait_ge(w_lo_done, len(stages))
                with pe.Fori(0, B) as b:
                    for g, (s, name, j) in enumerate(body):
                        if g % len(groups) == 0:
                            pe.wait_ge(x_lo_done[s], b + (1 + ONE))
                        if out and g % len(groups) == 4:
                            pe.wait_ge(bank_free, b * GT + (NBANK + g))
                        pe.wait_ge(bank_free, b * GT + (g + 1))
                        a_hi, a_lo = (c_hi, c_lo) if out and name != "o" else (x_hi[s], x_lo[s])
                        tile = slice(j * P, (j + 1) * P)
                        last = None
                        for k in range(KT):
                            for wa, xa in ((w_hi, a_hi), (w_hi, a_lo), (w_lo, a_hi)):
                                if name == "v":
                                    lhs, rhs = xa[:, k, tile], wa[name][:, k, :]
                                else:
                                    lhs, rhs = wa[name][:, k, tile], xa[:, k, :]
                                first = last is None
                                last = pe.matmul(bank[g % NBANK][:, :], lhs, rhs, start=first,
                                                 stop=(k == KT - 1 and wa is w_lo))
                        last.then_inc(group_done, 1)
                        if g % len(groups) == len(groups) - 1:
                            pe.drain().then_inc(chunk_done[s], 1)


def attention_block(nc, io, tag, q_d, k_d, v_d, o_d, bias_d=None, skew_d=None):
    rel = skew_d is not None
    NT = 2 * NQ
    NU = NT * HG
    NIT = NI // 2
    LAG = 2
    NRING = 3
    NP = 4
    NADD = 4 if rel else 2
    ULAG = 6
    RLAG = 2
    NUS = 4
    NSK = skew_d.shape[0] if rel else 0
    SK = 64
    STORED = 16 * P // SK

    def parts(u):
        return u // (NU // 2) % 2, u // HG % NQ, u % HG, u // HG

    def band(u):
        t = parts(u)[1]
        return (max(0, t - MAXLEN // P) * P, min(NQ, t + MAXLEN // P + 1) * P) if rel else (0, S)

    def pieces(u):
        lo, hi = band(u)
        width = hi - lo + P
        n = -(-width // 512)
        return n, width // n

    def in_step(step):
        x, w = step - LAG, step + ULAG
        t = [("T", x, half) for half in range(2)]
        up = [("U", w, c) for c in range(pieces(w)[0])] if rel else []
        return t[:1] + up[:1] + t[1:] + up[1:]

    STEPS = range(LAG, NU + LAG)
    early = [("U", w, c) for w in range(LAG + ULAG) for c in range(pieces(w)[0])] if rel else []
    turn = [item for step in STEPS for item in in_step(step)]
    RT = len(turn)
    at = {item: q for q, item in enumerate(early + turn)}

    def slot(item):
        return (at[item] - len(early)) % NRING

    def taker(item):
        kind, _, n = item
        return "dve" if (kind, n) in (("T", 1), ("U", 2)) else "act"

    taken = {item: sum(taker(i) == taker(item) for i in (early + turn)[:q + 1]) for item, q in at.items()}
    before, total = ({who: sum(taker(i) == who for i in items) for who in ("act", "dve")}
                     for items in (early, turn))

    with ExitStack() as ctx:
        m = Memory(nc, ctx, tag)
        q4 = [m.sb(f"q4_{s}", [P, HG, S], F32R) for s in range(2)]
        k4 = [m.sb(f"k4_{s}", [P, HG, S], F32R) for s in range(2)]
        v = [m.sb(f"v{s}", [P, NQ, P]) for s in range(2)]
        added = [m.sb(f"added{i}", [P, S]) for i in range(NADD)]
        prob = [m.sb(f"prob{i}", [P, S]) for i in range(NP)]
        probT = [m.sb(f"probT{i}", [P, HG, NQ, P]) for i in range(2)]
        o_sb = [m.sb(f"o_sb{s}", [P, S]) for s in range(2)]
        ident = m.sb("ident", [P, P])
        negmax = m.sb("negmax", [P, 4])
        den = m.sb("den", [P, 2, HG])
        rden = m.sb("rden", [P, 2, HG])
        rden_wide = m.sb("rden_wide", [P, 2, HG, DH])
        rT = m.sb("rT", [P, P])
        scores = [m.ps(f"scores{i}", [P, S]) for i in range(2)]
        bank = [m.ps(f"bank{i}", [P, 512]) for i in range(NRING)]
        oT = m.ps("oT", [P, 512])
        if rel:
            table = probT[0][:, :, :, :].rearrange("p h k n -> p (h k n)")
            r_in, r_hi = table[:, 0:RELW], table[:, RELW:2 * RELW].bitcast(F32R)
            r4 = m.sb("r4", [P, RELW], F32R)
            zeros = m.sb("zeros", [P, S - (MAXLEN // P + 1) * P])
            far = m.sb("far", [P, 4])
            u_sb = [m.sb(f"u_sb{i}", [P, UW]) for i in range(NUS)]
            r_hi_done, r4_done, far_done = m.sem("r_hi_done"), m.sem("r4_done"), m.sem("far_done")
            u_stored = [m.sem(f"u_stored{i}") for i in range(NUS)]
        passed = io["passed"]
        consts = m.sem("consts")
        in_loaded = [m.sem(f"in_loaded{s}") for s in range(2)]
        keys_loaded = [m.sem(f"keys_loaded{s}") for s in range(2)]
        slot_done = [m.sem(f"slot_done{s}") for s in range(2)]
        add_loaded = [m.sem(f"add_loaded{i}") for i in range(NADD)]
        scores_ready, added_done, probs_ready = m.sem("scores_ready"), m.sem("added_done"), m.sem("probs_ready")
        ring_ready = m.sem("ring_ready")
        left = {"dve": m.sem("left_dve"), "act": m.sem("left_act")}
        rden_done, rden_ready, o_ready = m.sem("rden_done"), m.sem("rden_ready"), m.sem("o_ready")
        rT_ready, o_done = m.sem("rT_ready"), m.sem("o_done")
        o_stored = [m.sem(f"o_stored{s}") for s in range(2)]
        o_free = [m.sem(f"o_free{s}") for s in range(2)]
        NC = 5 if rel else 1
        from_one = slot_done + [added_done, o_done] + list(left.values()) + o_free + (u_stored if rel else [])

        with nc.Block() as block:

            @block.gpsimd
            def _(pool):
                for sem in from_one:
                    pool.sem_inc(sem, ONE)
                if rel:
                    pool.memset(zeros[:, :], 0.0).then_inc(far_done, 1)

                def load_inputs(s, i):
                    for g in range(4):
                        pool.dma_start(q4[s][g * DH:(g + 1) * DH, :, :].bitcast(F32),
                                       q_d[(0, 0, 1, 1)[g], i, :, :].rearrange("(h d) n -> d h n", h=HG))\
                            .then_inc(in_loaded[s], 16)
                    pool.dma_start(v[s][:, :, :], v_d[i, :, :].rearrange("(t p) c -> p t c", p=P))\
                        .then_inc(in_loaded[s], 16)

                load_inputs(0, 0)
                with pool.Fori(0, NIT) as it:
                    pool.wait_ge(slot_done[1], it + ONE)
                    pool.sem_inc(passed)
                    load_inputs(1, it * 2 + 1)
                    pool.wait_ge(slot_done[0], it + (1 + ONE))
                    pool.sem_inc(passed)
                    load_inputs(0, (it * 2 + 2) % NI)
                    for s in range(2):
                        pool.wait_ge(o_done, it * NT + (NQ * (s + 1) + ONE))
                        pool.sem_inc(passed)
                        pool.dma_start(o_d[it * 2 + s, :, :], o_sb[s][:, :]).then_inc(o_stored[s], 16)
                        pool.wait_ge(o_stored[s], it * 16 + 16)
                        pool.sem_inc(o_free[s])
                pool.wait_ge(in_loaded[0], 16 * 5 * (NIT + 1))

            @block.sync
            def _(sp):
                sp.dma_start(ident[:, :], io["ident"]).then_inc(consts, 16)
                if rel:
                    for g in range(4):
                        sp.dma_start(r_in[g * DH:(g + 1) * DH, :], io["relT"]).then_inc(consts, 16)

                def load_keys(s, i):
                    for g in range(4):
                        sp.dma_start(k4[s][g * DH:(g + 1) * DH, :, :].bitcast(F32),
                                     k_d[(0, 1, 0, 1)[g], i, :, :].rearrange("(h d) n -> d h n", h=HG))\
                            .then_inc(keys_loaded[s], 16)

                def next_keys(it, s):
                    sp.wait_ge(slot_done[s], it + (ONE + 1 - s))
                    sp.sem_inc(passed)
                    load_keys(s, it * 2 + 1 if s else (it * 2 + 2) % NI)

                def store_position_scores(it, w):
                    lo, hi = band(w)
                    width = hi - lo + SK
                    for c in range(pieces(w)[0])[-2:]:
                        who = taker(("U", w, c))
                        sp.wait_ge(left[who], it * total[who] + (taken["U", w, c] + ONE))
                        sp.sem_inc(passed)
                    if w >= NSK:
                        sp.wait_ge(add_loaded[w % NADD], it * (16 * NU // NADD) + 16 * ((w - NSK) // NADD + 1))
                        sp.sem_inc(passed)
                    for g in range(P // SK):
                        rows, first = slice(g * SK, (g + 1) * SK), P - (g + 1) * SK
                        sp.dma_start(skew_d[w % NSK, g * SK * width:(g + 1) * SK * width]
                                     .rearrange("(p c) -> p c", p=SK),
                                     u_sb[w % NUS][rows, first:first + width]).then_inc(u_stored[w % NUS], 16)

                def read_skewed(it, r):
                    lo, hi = band(r)
                    width = hi - lo + SK
                    if r >= NADD:
                        sp.wait_ge(added_done, it * NU + (r - NADD + 1 + ONE))
                        sp.sem_inc(passed)
                    sp.wait_ge(u_stored[r % NUS], it * (STORED * NU // NUS) + (STORED * (r // NUS + 1) + ONE))
                    sp.sem_inc(passed)
                    sp.dma_start(added[r % NADD][:, lo:hi],
                                 bass.AP(skew_d.tensor, (r % NSK) * P * UW + SK - 1,
                                         [[SK * width, P // SK], [width - 1, SK], [1, hi - lo]]))\
                        .then_inc(add_loaded[r % NADD], 16)

                def load_bias(it, tt):
                    sp.dma_start(added[tt % 2][:, :], bias_d[(it + tt // NT) // 2 % B, parts(HG * tt)[1] * P:][:P])\
                        .then_inc(add_loaded[tt % 2], 16)

                load_keys(0, 0)
                if rel:
                    for w in range(LAG + ULAG):
                        store_position_scores(0, w)
                        if w >= RLAG:
                            read_skewed(0, w - RLAG)
                else:
                    for tt in range(2):
                        load_bias(0, tt)
                with sp.Fori(0, NIT) as it:
                    if rel:
                        for w in range(LAG + ULAG, NU + LAG + ULAG):
                            store_position_scores(it, w)
                            read_skewed(it, w - RLAG)
                            if w == NU // 4:
                                next_keys(it, 1)
                            if w == NU * 3 // 4 + 4:
                                next_keys(it, 0)
                    else:
                        for tt in range(2, NT + 2):
                            sp.wait_ge(added_done, it * NU + (HG * (tt - 1) + ONE))
                            sp.sem_inc(passed)
                            load_bias(it, tt)
                            if tt == NT // 4:
                                next_keys(it, 1)
                            if tt == NT * 3 // 4:
                                next_keys(it, 0)
                sp.wait_ge(keys_loaded[0], 16 * 4 * (NIT + 1))
                if rel:
                    for i in range(4):
                        sp.wait_ge(u_stored[i], STORED * (NIT * NU + LAG + ULAG) // NUS + ONE)
                    last_reads = NIT * NU + LAG + ULAG - RLAG
                else:
                    last_reads = NIT * NT + 2
                for i in range(NADD):
                    sp.wait_ge(add_loaded[i], 16 * len(range(i, last_reads, NADD)))

            @block.scalar
            def _(act):
                act.wait_ge(consts, 16 * NC)
                if rel:
                    act.activation(r_hi, r_in, ACT.Identity).then_inc(r_hi_done, 1)

                def take(it, item):
                    act.wait_ge(ring_ready, it * RT + (at[item] + 1))
                    kind, n, c = item
                    src = bank[slot(item)]
                    if kind == "T":
                        dst, src = probT[parts(n)[3] % 2][:, parts(n)[2], 4 * c:4 * c + 4, :], src[:, :].rearrange("p (k n) -> p k n", k=4)
                    else:
                        width = pieces(n)[1]
                        dst, src = u_sb[n % NUS][:, c * width:(c + 1) * width], src[:, 0:width]
                    act.activation(dst, src, ACT.Copy).then_inc(left["act"], 1)

                def take_all(it, items):
                    for item in items:
                        kind, n, c = item
                        if kind == "U" and c == 0:
                            act.wait_ge(u_stored[n % NUS], it * (STORED * NU // NUS) + (STORED * (n // NUS) + ONE))
                        if kind == "T" and parts(n)[3] >= 2 and parts(n)[2] == 0:
                            act.wait_ge(o_ready, it * NT + (parts(n)[3] - 1))
                        if taker(item) == "act":
                            take(it, item)

                def turn_den(it, tt):
                    act.wait_ge(o_ready, it * NT + (tt + 1))
                    act.activation(rT[:, :], oT[:, 256:384], ACT.Copy).then_inc(rT_ready, 1)

                def exponential(it, u):
                    s, t, h, tt = parts(u)
                    if u >= NP:
                        act.wait_ge(ring_ready, it * RT + (at["T", u - NP, 1] + 1))
                    act.wait_ge(added_done, it * NU + (u + 1 + ONE))
                    act.activation(prob[u % NP][:, :], scores[u % 2][:, :], ACT.Exp,
                                   bias=negmax[:, u % 4:u % 4 + 1], scale=-1.0,
                                   accum_out=den[:, tt % 2, h:h + 1]).then_inc(probs_ready, 1)

                take_all(0, early)
                for u in range(LAG):
                    exponential(0, u)
                with act.Fori(0, NIT) as it:
                    for step in STEPS:
                        x = step - LAG
                        if x >= 8 and x % 4 == 0:
                            turn_den(it, x // 4 - 2)
                        take_all(it, in_step(step))
                        exponential(it, step)
                    for tt in range(NT - 2, NT):
                        turn_den(it, tt)

            @block.vector
            def _(dve):
                dve.wait_ge(consts, 16 * NC)
                if rel:
                    dve.wait_ge(r_hi_done, 1)
                    for g in range(4):
                        rows = slice(g * DH, (g + 1) * DH)
                        if g % 2 == 0:
                            dve.tensor_copy(r4[rows, :], r_hi[rows, :].bitcast(F32)).then_inc(r4_done, 1)
                        else:
                            dve.tensor_tensor(r4[rows, :], r_in[rows, :], r_hi[rows, :].bitcast(F32),
                                              ALU.subtract).then_inc(r4_done, 1)
                    dve.wait_ge(far_done, 1)

                def normalise(it, tt):
                    s, t = tt // NQ, tt % NQ
                    if t == 0:
                        dve.wait_ge(o_free[s], it + ONE)
                    dve.wait_ge(rT_ready, it * NT + (tt + 1))
                    dve.tensor_tensor(o_sb[s][:, t * P:(t + 1) * P], oT[:, 0:P], rT[:, :], ALU.mult)\
                        .then_inc(o_done, 1)

                def third(it, w):
                    width = pieces(w)[1]
                    dve.wait_ge(u_stored[w % NUS], it * (STORED * NU // NUS) + (STORED * (w // NUS) + ONE))
                    dve.wait_ge(ring_ready, it * RT + (at["U", w, 2] + 1))
                    dve.tensor_copy(u_sb[w % NUS][:, 2 * width:3 * width], bank[slot(("U", w, 2))][:, 0:width])\
                        .then_inc(left["dve"], 1)

                def scale_min(dst, lo, hi, add, first, least):
                    return dve.tensor_tensor_reduce(out=dst[:, lo:hi], in0=dst[:, lo:hi], in1=add, scale=-SCALE,
                                                    scalar=first, op0=ALU.add, op1=ALU.min, accum_out=least)

                NFAR = sum(band(u) != (0, S) for u in range(NU))

                def add_scale_min(it, u):
                    s, t, h, tt = parts(u)
                    lo, hi = band(u)
                    dst, least = scores[u % 2], negmax[:, u % 4:u % 4 + 1]
                    dve.wait_ge(scores_ready, it * NU + (u + 1))
                    dve.sem_inc(passed)
                    first = 3e38
                    if (lo, hi) != (0, S):
                        a, b = (0, lo) if lo else (hi, S)
                        first = far[:, u % 4:u % 4 + 1]
                        scale_min(dst, a, b, zeros[:, 0:b - a], 3e38, first).then_inc(far_done, 1)
                        fars = sum(band(n) != (0, S) for n in range(u + 1))
                        dve.wait_ge(far_done, it * NFAR + (fars + 1))
                    if rel:
                        dve.wait_ge(add_loaded[u % NADD], it * (16 * NU // NADD) + 16 * (u // NADD + 1))
                    elif h == 0:
                        dve.wait_ge(add_loaded[tt % 2], it * (16 * NQ) + 16 * (tt // 2 + 1))
                    dve.sem_inc(passed)
                    scale_min(dst, lo, hi, added[(u if rel else tt) % NADD][:, lo:hi], first, least)\
                        .then_inc(added_done, 1)

                for u in range(LAG):
                    add_scale_min(0, u)
                with dve.Fori(0, NIT) as it:
                    for step in STEPS:
                        x = step - LAG
                        add_scale_min(it, step)
                        if x >= 8 and x % 4 == 0:
                            normalise(it, x // 4 - 2)
                        s, t, h, tt = parts(x)
                        if tt >= 2 and h == 0:
                            dve.wait_ge(o_ready, it * NT + (tt - 1))
                        dve.wait_ge(ring_ready, it * RT + (at["T", x, 1] + 1))
                        dve.tensor_copy(probT[tt % 2][:, h, 4:8, :],
                                        bank[slot(("T", x, 1))][:, :].rearrange("p (k n) -> p k n", k=4))\
                            .then_inc(left["dve"], 1)
                        if ("U", step + ULAG, 2) in at:
                            third(it, step + ULAG)
                        if h == HG - 1:
                            dve.wait_ge(probs_ready, it * NU + (x + 1))
                            dve.reciprocal(rden[:, tt % 2, :], den[:, tt % 2, :]).then_inc(rden_done, 1)
                            dve.wait_ge(rden_done, it * NT + (tt + 1))
                            dve.tensor_copy(rden_wide[:, tt % 2, :, :],
                                            rden[:, tt % 2, :].rearrange("p (h a) -> p h a", a=1)
                                            .to_broadcast([P, HG, DH])).then_inc(rden_ready, 1)
                    for tt in range(NT - 2, NT):
                        normalise(it, tt)

            @block.tensor
            def _(pe):
                pe.wait_ge(consts, 16 * NC)
                if rel:
                    pe.wait_ge(r4_done, 4)

                def into_ring(it, item):
                    q = at[item]
                    kind, n, c = item
                    if item == turn[0]:
                        for who in left:
                            pe.wait_ge(left[who], it * total[who] + (before[who] + ONE))
                    elif item not in turn[:NRING] and q >= NRING:
                        last = (early + turn)[q - NRING]
                        pe.wait_ge(left[taker(last)], it * total[taker(last)] + (taken[last] + ONE))
                    if kind == "T":
                        for j in range(4):
                            a = (4 * c + j) * P
                            last = pe.transpose(bank[slot(item)][:, j * P:(j + 1) * P], prob[n % NP][:, a:a + P],
                                                ident[:, :])
                    else:
                        s, t, h, _ = parts(n)
                        width = pieces(n)[1]
                        if n % (NU // 2) == 0 and c == 0:
                            pe.wait_ge(in_loaded[s], (it + (1 + n // NU)) * (16 * 5))
                        a = S - P - P * t + band(n)[0] + c * width
                        last = pe.matmul(bank[slot(item)][:, 0:width], q4[s][:, h, t * P:(t + 1) * P],
                                         r4[:, a:a + width], start=True, stop=True)
                    last.then_inc(ring_ready, 1)

                def product(it, u):
                    s, t, h, tt = parts(u)
                    if u % (NU // 2) == 0:
                        pe.wait_ge(in_loaded[s], (it + (1 + u // NU)) * (16 * 5))
                        pe.wait_ge(keys_loaded[s], (it + (1 + u // NU)) * (16 * 4))
                    if u >= 2:
                        pe.wait_ge(probs_ready, it * NU + (u - 1))
                    lo, hi = band(u)
                    query = q4[s][:, h, t * P:(t + 1) * P]
                    for n in range(2):
                        c = n * CH
                        a, b, row = (0, min(lo, CH), 0) if n == 0 else (max(hi, CH), S, RELW - MAXLEN)
                        last = pe.matmul(scores[u % 2][:, c:c + CH], query, k4[s][:, h, c:c + CH],
                                         start=True, stop=(a == b))
                        if a < b:
                            last = pe.matmul(scores[u % 2][:, a:b], query, r4[:, row:row + b - a],
                                             start=False, stop=True)
                    last.then_inc(scores_ready, 1)

                def values(it, tt, part):
                    s = tt // NQ
                    if part == 1:
                        for half in range(2):
                            who = taker(("T", 0, half))
                            pe.wait_ge(left[who], it * total[who] + (taken["T", HG * (tt + 1) - 1, half] + ONE))
                        pe.wait_ge(o_done, it * NT + (tt + ONE))
                    for k in range(3 * (part - 1), min(3 * part, NQ)):
                        for h in range(HG):
                            last = pe.matmul(oT[h * DH:(h + 1) * DH, 0:P], v[s][:, k, h * DH:(h + 1) * DH],
                                             probT[tt % 2][:, h, k, :], start=(k == 0), stop=(k == NQ - 1))
                    if part == 3:
                        if tt % NQ == NQ - 1:
                            last.then_inc(slot_done[s], 1)
                        pe.wait_ge(rden_ready, it * NT + (tt + 1))
                        pe.transpose(oT[:, 256:384], rden_wide[:, tt % 2, :, :].rearrange("p h d -> p (h d)"),
                                     ident[:, :]).then_inc(o_ready, 1)

                for item in early:
                    into_ring(0, item)
                for u in range(LAG):
                    product(0, u)
                with pe.Fori(0, NIT) as it:
                    for step in STEPS:
                        x = step - LAG
                        product(it, step)
                        pe.wait_ge(probs_ready, it * NU + (x + 1))
                        for item in in_step(step):
                            into_ring(it, item)
                        if x >= 4 and x % 4:
                            values(it, x // 4 - 1, x % 4)
                    for part in range(1, 4):
                        values(it, NT - 1, part)


def adapter_block(nc, io, o_d, x1_d, y_d, gates_d):
    NCH = B * 2

    def of(chunk, per, n):
        c, later = chunk
        return c * per + (later * per + n) if per > 1 else c + (later + n)

    def turns(eng, work):
        work(None, (0, 0))
        with eng.Fori(0, NCH - 1) as c:
            work((c, 0), (c, 1))
        work((NCH - 1, 0), None)

    with ExitStack() as ctx:
        m = Memory(nc, ctx, "ad")
        w_in = m.sb("w_in", [P, KT, D])
        wo_hi, wo_lo = m.sb("wo_hi", [P, KT, D], F32R), m.sb("wo_lo", [P, KT, D], F32R)
        g_in = m.sb("g_in", [P, KT, NE])
        g_hi, g_lo = m.sb("g_hi", [P, KT, NE], F32R), m.sb("g_lo", [P, KT, NE], F32R)
        cols = m.sb("cols", [P, 2, KT])
        ident = m.sb("ident", [P, P])
        iota8 = m.sb("iota8", [P, NE])
        ids = m.sb("ids", [1, B], I32)
        w1_in, w2_in = m.sb("w1_in", [P, KT, AD]), m.sb("w2_in", [P, D])
        w1_hi, w1_lo = m.sb("w1_hi", [P, KT, AD], F32R), m.sb("w1_lo", [P, KT, AD], F32R)
        w2_hi, w2_lo = m.sb("w2_hi", [P, D], F32R), m.sb("w2_lo", [P, D], F32R)
        b_cols = m.sb("b_cols", [P, 1 + KT])
        gb_cols = m.sb("gb_cols", [P, 2 * KT])
        o_in, xT = m.sb("o_in", [P, KT, CH]), m.sb("xT", [P, KT, CH])
        o_hi, o_lo = m.sb("o_hi", [P, KT, CH], F32R), m.sb("o_lo", [P, KT, CH], F32R)
        x1 = m.sb("x1", [P, KT, CH])
        x1_hi, x1_lo = m.sb("x1_hi", [P, KT, CH], F32R), m.sb("x1_lo", [P, KT, CH], F32R)
        h = m.sb("h", [P, CH])
        h_hi, h_lo = m.sb("h_hi", [P, CH], F32R), m.sb("h_lo", [P, CH], F32R)
        xx = m.sb("xx", [P, KT, CH])
        x1n = [m.sb(f"x1n{i}", [P, D]) for i in range(4)]
        stats = m.sb("stats", [P, 4, 6])
        mv = m.sb("mv", [P, 4, 2])
        var, rvar, root, rstd = (m.sb(n, [P, 4]) for n in ("var", "rvar", "root", "rstd"))
        yn = [m.sb(f"yn{i}", [P, D]) for i in range(4)]
        yT = m.sb("yT", [P, KT, CH])
        y_hi, y_lo = m.sb("y_hi", [P, KT, CH], F32R), m.sb("y_lo", [P, KT, CH], F32R)
        lgT = m.sb("lgT", [NE, CH])
        lg = m.sb("lg", [P, 4, NE])
        top = m.sb("top", [P, 4, 8])
        top_i = m.sb("top_i", [P, 4, 8], U32)
        top_f = m.sb("top_f", [P, 4, 8])
        diff, e2 = m.sb("diff", [P, 4]), m.sb("e2", [P, 4])
        tot, wt = m.sb("tot", [P, 4]), m.sb("wt", [P, 2, 4])
        hot = m.sb("hot", [P, 4, NE])
        gates = m.sb("gates", [P, 4, NE])
        bank = [m.ps(f"bank{i}", [P, CH]) for i in range(8)]
        names = ("consts w_hi_done w_lo_done ad_loaded o_loaded xT_loaded o_hi_done o_lo_done adw_hi_done "
                 "adw_lo_done o_groups x1_done x1_hi_done x1_lo_done up_done h_done h_hi_done h_lo_done "
                 "down_done xx_done x1_turned x1n_done xx_turned rvar_ready root_ready yn_done y_turned yT_done y_hi_done y_lo_done "
                 "logits_done lgT_done lg_turned lg_done gb_loaded diff_ready e2_ready gates_done chain").split()
        sm = {n: m.sem(n) for n in names}
        x1_stored = m.sem("x1_stored")
        y_stored, gates_stored = m.sem("y_stored"), m.sem("gates_stored")
        passed = io["passed"]
        NCONST = 7
        from_one = [sm[n] for n in ("o_lo_done", "x1_done", "yT_done", "o_groups", "down_done", "adw_lo_done",
                                   "xx_done", "lg_done")]
        from_one += [x1_stored, y_stored, gates_stored]
        with nc.Block() as block:

            @block.gpsimd
            def _(pool):
                for sem in from_one:
                    pool.sem_inc(sem, ONE)

                def load_o(chunk):
                    pool.wait_ge(sm["o_lo_done"], of(chunk, 1, ONE))
                    pool.sem_inc(passed)
                    i = (chunk[0] + chunk[1]) % NCH
                    pool.dma_start(o_in[:, :, :], o_d[bass.ds(i // 2 * NG, NG), :, bass.ds(i % 2 * CH, CH)]
                                   .rearrange("k p n -> p k n")).then_inc(sm["o_loaded"], 16)

                def work(k, n):
                    if n:
                        pool.wait_ge(sm["x1_done"], of(n, 4, ONE))
                        pool.sem_inc(passed)
                        pool.dma_start(xT[:, :, :], io["xT"][:, bass.ds((n[0] + n[1]) * CH, CH)]
                                       .rearrange("(k p) n -> p k n", p=P)).then_inc(sm["xT_loaded"], 16)
                        load_o((n[0], n[1] + 1))

                load_o((0, 0))
                turns(pool, work)
                pool.wait_ge(sm["o_loaded"], 16 * (NCH + 1))

            @block.sync
            def _(sp):
                for dst, src in (
                    (ids[:, :], io["lang"]), (w_in[:, :, :], io["bWo"].rearrange("(k p) n -> p k n", p=P)),
                    (g_in[:, :, :], io["gateT"].rearrange("(k p) n -> p k n", p=P)),
                    (cols[:, 0, :], io["bbv"]), (cols[:, 1, :], io["bbo"]), (ident[:, :], io["ident"]),
                    (iota8[:, :], io["iota8"]),
                ):
                    sp.dma_start(dst, src).then_inc(sm["consts"], 16)
                sp.wait_ge(sm["consts"], 16 * NCONST)

                def language(chunk):
                    return sp.value_load(ids[0:1, bass.ds((chunk[0] + chunk[1]) // 2, 1)], min_val=0,
                                         max_val=LANGS - 1)

                def work(k, n):
                    if n:
                        lang = language(n)
                        for name, per in (("adw_lo_done", 1), ("xx_done", 4)):
                            sp.wait_ge(sm[name], of(n, per, ONE))
                            sp.sem_inc(passed)
                        sp.dma_start(w1_in[:, :, :], io["W1"][bass.ds(lang, 1), :, :]
                                     .rearrange("a (k p) n -> p (a k) n", p=P)).then_inc(sm["ad_loaded"], 16)
                        sp.dma_start(w2_in[:, :], io["W2"][bass.ds(lang, 1), :, :]
                                     .rearrange("a p n -> p (a n)")).then_inc(sm["ad_loaded"], 16)
                        sp.dma_start(b_cols[:, :], io["adcols"][bass.ds(lang, 1), :, 0:1 + KT]
                                     .rearrange("a p n -> p (a n)")).then_inc(sm["ad_loaded"], 16)
                    if k:
                        lang = language(k)
                        sp.wait_ge(sm["yT_done"], of(k, 4, ONE))
                        sp.sem_inc(passed)
                        sp.dma_start(gb_cols[:, :], io["adcols"][bass.ds(lang, 1), :, 1 + KT:1 + 3 * KT]
                                     .rearrange("a p n -> p (a n)")).then_inc(sm["gb_loaded"], 16)
                    for r in range(4) if n else ():
                        sp.wait_ge(sm["x1n_done"], of(n, 4, r + 1))
                        sp.sem_inc(passed)
                        sp.dma_start(x1_d[n[0] + n[1], :, r, :], x1n[r][:, :]).then_inc(x1_stored, 16)
                    if k:
                        sp.wait_ge(sm["y_lo_done"], of(k, 1, 1))
                        sp.sem_inc(passed)
                        sp.dma_start(y_d[0, k[0], :, :, :], y_hi[:, :, :].bitcast(F32)).then_inc(y_stored, 16)
                        sp.dma_start(y_d[1, k[0], :, :, :], y_lo[:, :, :].bitcast(F32)).then_inc(y_stored, 16)
                        sp.wait_ge(sm["gates_done"], of(k, 1, 1))
                        sp.sem_inc(passed)
                        sp.dma_start(gates_d[k[0], :, :, :], gates[:, :, :]).then_inc(gates_stored, 16)

                turns(sp, work)
                sp.wait_ge(x1_stored, 16 * 4 * NCH + ONE)
                sp.wait_ge(y_stored, 32 * NCH + ONE)
                sp.wait_ge(gates_stored, 16 * NCH + ONE)

            @block.scalar
            def _(act):
                ident_fn = ACT.Identity
                act.wait_ge(sm["consts"], 16 * NCONST)
                act.activation(wo_hi[:, :, :], w_in[:, :, :], ident_fn)
                act.activation(g_hi[:, :, :], g_in[:, :, :], ident_fn).then_inc(sm["w_hi_done"], 1)

                def split_o(chunk):
                    act.wait_ge(sm["o_loaded"], of(chunk, 16, 16))
                    act.wait_ge(sm["o_groups"], of(chunk, 4, ONE))
                    for k in range(KT):
                        last = act.activation(o_hi[:, k, :], o_in[:, k, :], ident_fn, bias=cols[:, 0, k:k + 1])
                    last.then_inc(sm["o_hi_done"], 1)

                def work(k, n):
                    if k:
                        act.wait_ge(sm["rvar_ready"], of(k, 1, 1))
                        act.activation(root[:, :], rvar[:, :], ACT.Sqrt).then_inc(sm["root_ready"], 1)
                    if n:
                        act.wait_ge(sm["ad_loaded"], of(n, 48, 48))
                        act.wait_ge(sm["down_done"], of(n, 4, ONE))
                        act.activation(w1_hi[:, :, :], w1_in[:, :, :], ident_fn)
                        act.activation(w2_hi[:, :], w2_in[:, :], ident_fn).then_inc(sm["adw_hi_done"], 1)
                        for j in range(KT):
                            act.wait_ge(sm["x1_done"], of(n, 4, j + 1 + ONE))
                            act.activation(x1_hi[:, j, :], x1[:, j, :], ident_fn).then_inc(sm["x1_hi_done"], 1)
                    if k:
                        act.wait_ge(sm["gb_loaded"], of(k, 16, 16))
                        for r in range(4):
                            act.wait_ge(sm["y_turned"], of(k, 4, r + 1))
                            for j in range(KT):
                                last = act.activation(yT[:, j, r * P:(r + 1) * P], bank[r][:, j * P:(j + 1) * P],
                                                      ident_fn, scale=gb_cols[:, j:j + 1],
                                                      bias=gb_cols[:, KT + j:KT + j + 1])
                            last.then_inc(sm["yT_done"], 1)
                    if n:
                        act.wait_ge(sm["up_done"], of(n, 1, 1))
                        act.activation(h[:, :], bank[4][:, :], ACT.Relu, bias=b_cols[:, 0:1])\
                            .then_inc(sm["h_done"], 1)
                        act.wait_ge(sm["h_done"], of(n, 1, 1))
                        act.activation(h_hi[:, :], h[:, :], ident_fn).then_inc(sm["h_hi_done"], 1)
                        act.wait_ge(x1_stored, of(n, 64, ONE))
                        for r in range(4):
                            act.wait_ge(sm["x1_turned"], of(n, 4, r + 1))
                            act.activation(x1n[r][:, :], bank[5 + r % 3][:, :], ACT.Copy)\
                                .then_inc(sm["x1n_done"], 1)
                    if k:
                        act.wait_ge(sm["yT_done"], of(k, 4, 4 + ONE))
                        act.wait_ge(y_stored, of(k, 32, ONE))
                        act.activation(y_hi[:, :, :], yT[:, :, :], ident_fn).then_inc(sm["y_hi_done"], 1)
                    if n:
                        split_o((n[0], n[1] + 1))
                    if k:
                        act.wait_ge(sm["diff_ready"], of(k, 1, 1))
                        act.activation(e2[:, :], diff[:, :], ACT.Exp).then_inc(sm["e2_ready"], 1)

                split_o((0, 0))
                turns(act, work)

            @block.vector
            def _(dve):
                f32 = lambda t: t.bitcast(F32)
                dve.wait_ge(sm["w_hi_done"], 1)
                dve.tensor_tensor(wo_lo[:, :, :], w_in[:, :, :], f32(wo_hi[:, :, :]), ALU.subtract)
                dve.tensor_tensor(g_lo[:, :, :], g_in[:, :, :], f32(g_hi[:, :, :]), ALU.subtract)\
                    .then_inc(sm["w_lo_done"], 1)
                NCHAIN = 7 + 12

                def split_o(chunk):
                    dve.wait_ge(sm["o_hi_done"], of(chunk, 1, 1))
                    for j in range(KT):
                        last = dve.scalar_tensor_tensor(out=o_lo[:, j, :], in0=o_in[:, j, :],
                                                        scalar=cols[:, 0, j:j + 1], in1=f32(o_hi[:, j, :]),
                                                        op0=ALU.add, op1=ALU.subtract)
                    last.then_inc(sm["o_lo_done"], 1)

                links = [0]

                def then(k, ins):
                    links[0] += 1
                    ins.then_inc(sm["chain"], 1)
                    dve.wait_ge(sm["chain"], of(k, NCHAIN, links[0]))
                    dve.sem_inc(passed)

                def normalise(k):
                    for r in range(4):
                        dve.wait_ge(sm["xx_turned"], of(k, 4, r + 1))
                        dve.sem_inc(passed)
                        last = dve.bn_stats(stats[:, r, :], bank[r][:, :])
                    then(k, last)
                    for r in range(4):
                        last = dve.bn_aggr(mv[:, r, :], stats[:, r, :])
                    then(k, last)
                    then(k, dve.tensor_scalar(var[:, :], mv[:, :, 1], LN_EPS, None, ALU.add))
                    dve.reciprocal(rvar[:, :], var[:, :]).then_inc(sm["rvar_ready"], 1)
                    dve.wait_ge(sm["root_ready"], of(k, 1, 1))
                    then(k, dve.tensor_tensor(rstd[:, :], root[:, :], root[:, :], ALU.mult))
                    then(k, dve.tensor_tensor(rstd[:, :], rstd[:, :], var[:, :], ALU.mult))
                    then(k, dve.tensor_scalar(rstd[:, :], rstd[:, :], -0.5, 1.5, ALU.mult, ALU.add))
                    then(k, dve.tensor_tensor(rstd[:, :], rstd[:, :], root[:, :], ALU.mult))
                    for r in range(4):
                        dve.tensor_scalar(yn[r][:, :], bank[r][:, :], mv[:, r, 0:1], rstd[:, r:r + 1],
                                          ALU.subtract, ALU.mult).then_inc(sm["yn_done"], 1)

                def to_adapter(n):
                    dve.wait_ge(sm["adw_hi_done"], of(n, 1, 1))
                    dve.tensor_tensor(w1_lo[:, :, :], w1_in[:, :, :], f32(w1_hi[:, :, :]), ALU.subtract)
                    dve.tensor_tensor(w2_lo[:, :], w2_in[:, :], f32(w2_hi[:, :]), ALU.subtract)\
                        .then_inc(sm["adw_lo_done"], 1)
                    dve.wait_ge(sm["xT_loaded"], of(n, 16, 16))
                    for j in range(KT):
                        dve.wait_ge(sm["o_groups"], of(n, 4, j + 1 + ONE))
                        dve.scalar_tensor_tensor(out=x1[:, j, :], in0=bank[4 + j][:, :],
                                                 scalar=cols[:, 1, j:j + 1], in1=xT[:, j, :],
                                                 op0=ALU.add, op1=ALU.add).then_inc(sm["x1_done"], 1)
                    for j in range(KT):
                        dve.wait_ge(sm["x1_hi_done"], of(n, 4, j + 1))
                        dve.tensor_tensor(x1_lo[:, j, :], x1[:, j, :], f32(x1_hi[:, j, :]), ALU.subtract)\
                            .then_inc(sm["x1_lo_done"], 1)

                def from_adapter(n):
                    dve.wait_ge(sm["h_hi_done"], of(n, 1, 1))
                    dve.tensor_tensor(h_lo[:, :], h[:, :], f32(h_hi[:, :]), ALU.subtract)\
                        .then_inc(sm["h_lo_done"], 1)
                    for j in range(KT):
                        dve.wait_ge(sm["down_done"], of(n, 4, j + 1 + ONE))
                        dve.scalar_tensor_tensor(out=xx[:, j, :], in0=bank[4 + j][:, :],
                                                 scalar=b_cols[:, 1 + j:2 + j], in1=x1[:, j, :],
                                                 op0=ALU.add, op1=ALU.add).then_inc(sm["xx_done"], 1)

                def split_y(k):
                    dve.wait_ge(sm["y_hi_done"], of(k, 1, 1))
                    dve.tensor_tensor(y_lo[:, :, :], yT[:, :, :], f32(y_hi[:, :, :]), ALU.subtract)\
                        .then_inc(sm["y_lo_done"], 1)

                def choose(k):
                    dve.wait_ge(sm["logits_done"], of(k, 1, 1))
                    dve.tensor_copy(lgT[:, :], bank[3][0:NE, :]).then_inc(sm["lgT_done"], 1)
                    dve.wait_ge(sm["lg_turned"], of(k, 1, 1))
                    dve.tensor_copy(lg[:, :, :], bank[3][:, 0:4 * NE].rearrange("p (r e) -> p r e", r=4))\
                        .then_inc(sm["lg_done"], 1)
                    dve.wait_ge(sm["lg_done"], of(k, 1, 1 + ONE))
                    dve.sem_inc(passed)
                    for r in range(4):
                        last = dve.max(top[:, r, :], lg[:, r, :])
                    then(k, last)
                    for r in range(4):
                        last = dve.max_index(top_i[:, r, :], top[:, r, :], lg[:, r, :])
                    then(k, last)
                    dve.tensor_tensor(diff[:, :], top[:, :, 1], top[:, :, 0], ALU.subtract)\
                        .then_inc(sm["diff_ready"], 1)
                    then(k, dve.tensor_copy(top_f[:, :, :], top_i[:, :, :]))
                    dve.wait_ge(sm["e2_ready"], of(k, 1, 1))
                    then(k, dve.tensor_scalar(tot[:, :], e2[:, :], 1.0, None, ALU.add))
                    then(k, dve.reciprocal(wt[:, 0, :], tot[:, :]))
                    then(k, dve.tensor_tensor(wt[:, 1, :], wt[:, 0, :], e2[:, :], ALU.mult))
                    dve.wait_ge(gates_stored, of(k, 16, ONE))
                    for r in range(4):
                        last = dve.tensor_scalar(hot[:, r, :], iota8[:, :], top_f[:, r, 1:2], wt[:, 1, r:r + 1],
                                                 ALU.is_equal, ALU.mult)
                    then(k, last)
                    for r in range(4):
                        last = dve.tensor_scalar(gates[:, r, :], iota8[:, :], top_f[:, r, 0:1],
                                                 wt[:, 0, r:r + 1], ALU.is_equal, ALU.mult)
                    then(k, last)
                    dve.tensor_tensor(gates[:, :, :], gates[:, :, :], hot[:, :, :], ALU.add)\
                        .then_inc(sm["gates_done"], 1)
                    for _ in range(NCHAIN - links[0]):
                        dve.sem_inc(sm["chain"], 1)

                def work(k, n):
                    links[0] = 0
                    if k:
                        normalise(k)
                    if n:
                        to_adapter(n)
                        from_adapter(n)
                    if k:
                        split_y(k)
                    if n:
                        split_o((n[0], n[1] + 1))
                    if k:
                        choose(k)

                split_o((0, 0))
                turns(dve, work)

            @block.tensor
            def _(pe):
                pe.wait_ge(sm["w_lo_done"], 1)

                def product(out, pairs):
                    n = len(pairs)
                    for i, (lhs, rhs) in enumerate(pairs):
                        last = pe.matmul(out, lhs, rhs, start=(i == 0), stop=(i == n - 1))
                    return last

                def turn(dst, src):
                    for k in range(KT):
                        last = pe.transpose(dst[:, k * P:(k + 1) * P], src(k), ident[:, :])
                    return last

                def tile(k):
                    return slice(k * P, (k + 1) * P)

                def part_two_starts(k):
                    pe.wait_ge(sm["xx_done"], of(k, 4, 4 + ONE))
                    for r in range(4):
                        if r == 3:
                            pe.wait_ge(sm["lg_done"], of(k, 1, ONE))
                        turn(bank[r], lambda j: xx[:, j, tile(r)]).then_inc(sm["xx_turned"], 1)

                def output_projection(n):
                    pe.wait_ge(sm["o_lo_done"], of(n, 1, 1 + ONE))
                    for j in range(KT):
                        product(bank[4 + j][:, :], [(w[:, i, tile(j)], a[:, i, :]) for i in range(KT)
                                                    for w, a in ((wo_hi, o_hi), (wo_hi, o_lo), (wo_lo, o_hi))])\
                            .then_inc(sm["o_groups"], 1)

                def turn_y(k):
                    for r in range(4):
                        pe.wait_ge(sm["yn_done"], of(k, 4, r + 1))
                        turn(bank[r], lambda j: yn[r][:, tile(j)]).then_inc(sm["y_turned"], 1)

                def adapter(n):
                    pe.wait_ge(sm["adw_lo_done"], of(n, 1, 1 + ONE))
                    pe.wait_ge(sm["x1_lo_done"], of(n, 4, 4))
                    product(bank[4][:, :], [(w[:, j, :], a[:, j, :]) for j in range(KT)
                                            for w, a in ((w1_hi, x1_hi), (w1_hi, x1_lo), (w1_lo, x1_hi))])\
                        .then_inc(sm["up_done"], 1)
                    for r in range(4):
                        if r == 3:
                            pe.wait_ge(sm["x1n_done"], of(n, 4, 1))
                        turn(bank[5 + r % 3], lambda j: x1[:, j, tile(r)]).then_inc(sm["x1_turned"], 1)
                    pe.wait_ge(sm["h_lo_done"], of(n, 1, 1))
                    pe.wait_ge(sm["x1n_done"], of(n, 4, 4))
                    for j in range(KT):
                        product(bank[4 + j][:, :], [(w[:, tile(j)], a[:, :])
                                                    for w, a in ((w2_hi, h_hi), (w2_hi, h_lo), (w2_lo, h_hi))])\
                            .then_inc(sm["down_done"], 1)

                def logits(k):
                    pe.wait_ge(sm["y_lo_done"], of(k, 1, 1))
                    product(bank[3][0:NE, :], [(w[:, j, :], a[:, j, :]) for j in range(KT)
                                               for w, a in ((g_hi, y_hi), (g_hi, y_lo), (g_lo, y_hi))])\
                        .then_inc(sm["logits_done"], 1)
                    pe.wait_ge(sm["lgT_done"], of(k, 1, 1))
                    pe.sem_inc(passed)
                    for r in range(4):
                        last = pe.transpose(bank[3][:, r * NE:(r + 1) * NE], lgT[:, tile(r)], ident[0:NE, 0:NE])
                    last.then_inc(sm["lg_turned"], 1)

                def work(k, n):
                    if k:
                        part_two_starts(k)
                    if n:
                        output_projection(n)
                    if k:
                        turn_y(k)
                    if n:
                        adapter(n)
                    if k:
                        logits(k)

                turns(pe, work)


def experts_block(nc, io, x1_d, y_d, gates_d, out_d):
    with ExitStack() as ctx:
        m = Memory(nc, ctx, "ex")
        w_hi = [m.sb(f"w_hi{e}", [P, KT, D], F32R) for e in range(NE)]
        w_lo = [m.sb(f"w_lo{e}", [P, KT, D], F32R) for e in range(NE)]
        w_in = m.sb("w_in", [P, KT, D])
        y = [[m.sb(f"y{s}_{a}", [P, KT, CH], F32R) for a in range(2)] for s in range(2)]
        x1 = [m.sb(f"x1_{s}", [P, 4, D]) for s in range(2)]
        gates = [m.sb(f"gates{s}", [P, 4, NE]) for s in range(2)]
        sums = m.sb("sums", [P, 4, D])
        acc, out_sb = [sums[:, i, :] for i in range(2)], [sums[:, 2 + i, :] for i in range(2)]
        w_ins = [w_in[:, :, :], sums[:, :, :], x1[1][:, :, :]]
        NW = len(w_ins)
        NBANK = 8
        bank = [m.ps(f"bank{i}", [P, D]) for i in range(NBANK)]
        w_loaded = [m.sem(f"w_loaded{i}") for i in range(NW)]
        w_hi_done, w_lo_done = m.sem("w_hi_done"), m.sem("w_lo_done")
        loaded = [m.sem(f"loaded{s}") for s in range(2)]
        group_done, added = m.sem("group_done"), m.sem("added")
        chunk_done = [m.sem(f"chunk_done{s}") for s in range(2)]
        summed = [m.sem(f"summed{s}") for s in range(2)]
        stored = [m.sem(f"stored{i}") for i in range(2)]
        passed = io["passed"]
        GC = 4 * NE
        GT = 2 * GC
        with nc.Block() as block:

            @block.gpsimd
            def _(pool):
                for sem in [added] + chunk_done + summed + stored:
                    pool.sem_inc(sem, ONE)
                with pool.Fori(0, B) as b:
                    for s in range(2):
                        pool.wait_ge(chunk_done[s], b + ONE)
                        pool.sem_inc(passed)
                        pool.wait_ge(summed[s], b + ONE)
                        pool.sem_inc(passed)
                        if s == 1:
                            pool.wait_ge(w_lo_done, NE)
                        c = b * 2 + s
                        for a in range(2):
                            pool.dma_start(y[s][a][:, :, :].bitcast(F32), y_d[a, c, :, :, :]).then_inc(loaded[s], 16)
                        pool.dma_start(x1[s][:, :, :], x1_d[c, :, :, :]).then_inc(loaded[s], 16)
                        pool.dma_start(gates[s][:, :, :], gates_d[c, :, :, :]).then_inc(loaded[s], 16)

            @block.sync
            def _(sp):
                for e in range(NE):
                    if e >= NW:
                        sp.wait_ge(w_lo_done, e - NW + 1)
                    sp.dma_start(w_ins[e % NW], io["weight"][e, :, :].rearrange("(k p) n -> p k n", p=P))\
                        .then_inc(w_loaded[e % NW], 16)
                with sp.Fori(0, B) as b:
                    for s in range(2):
                        for r in range(4):
                            sp.wait_ge(added, b * GT + (s * GC + (r + 1) * NE + ONE))
                            sp.sem_inc(passed)
                            sp.dma_start(out_d[b, s * CH + r * P:s * CH + (r + 1) * P, :], out_sb[r % 2])\
                                .then_inc(stored[r % 2], 16)
                for i in range(2):
                    sp.wait_ge(stored[i], 16 * 4 * B + ONE)

            @block.scalar
            def _(act):
                for e in range(NE):
                    act.wait_ge(w_loaded[e % NW], 16 * (e // NW + 1))
                    act.activation(w_hi[e][:, :, :], w_ins[e % NW], ACT.Identity).then_inc(w_hi_done, 1)

            @block.vector
            def _(dve):
                for e in range(NE):
                    dve.wait_ge(w_hi_done, e + 1)
                    dve.tensor_tensor(w_lo[e][:, :, :], w_ins[e % NW], w_hi[e][:, :, :].bitcast(F32),
                                      ALU.subtract).then_inc(w_lo_done, 1)
                dve.wait_ge(w_lo_done, NE)
                with dve.Fori(0, B) as b:
                    for g in range(GT):
                        s, r, e = g // GC, g // NE % 4, g % NE
                        if g % GC == 0:
                            dve.wait_ge(loaded[s], b * 64 + 64)
                        if e == NE - 1:
                            dve.wait_ge(stored[r % 2], b * 64 + (16 * ((s * 4 + r) // 2) + ONE))
                        dve.wait_ge(added, b * GT + (g + ONE))
                        dve.wait_ge(group_done, b * GT + (g + 1))
                        src = x1[s][:, r, :] if e == 0 else acc[(e + 1) % 2]
                        dst = out_sb[r % 2] if e == NE - 1 else acc[e % 2]
                        dve.scalar_tensor_tensor(out=dst, in0=bank[g % NBANK][:, :], scalar=gates[s][:, r, e:e + 1],
                                                 in1=src, op0=ALU.mult, op1=ALU.add).then_inc(added, 1)
                        if g % GC == GC - 1:
                            dve.drain().then_inc(summed[s], 1)

            @block.tensor
            def _(pe):
                with pe.Fori(0, B) as b:
                    for g in range(GT):
                        s, r, e = g // GC, g // NE % 4, g % NE
                        if g % GC == 0:
                            pe.wait_ge(loaded[s], b * 64 + 64)
                        if r == 0 and s == 0:
                            pe.wait_ge(w_lo_done, e + 1)
                        if g >= NBANK:
                            pe.wait_ge(added, b * GT + (g - NBANK + 1 + ONE))
                        else:
                            pe.wait_ge(added, b * GT + ONE)
                        n = 0
                        for k in range(KT):
                            for a, w in ((0, w_hi), (0, w_lo), (1, w_hi)):
                                last = pe.matmul(bank[g % NBANK][:, :], y[s][a][:, k, r * P:(r + 1) * P],
                                                 w[e][:, k, :], start=(n == 0), stop=(n == 3 * KT - 1))
                                n += 1
                        last.then_inc(group_done, 1)
                        if g % GC == GC - 1:
                            pe.drain().then_inc(chunk_done[s], 1)


def build_program(nc, io, out_d):
    def scratch(name, shape):
        return nc.dram_tensor(name, shape, F32, kind="Internal").ap()

    q_d, k_d = scratch("q_parts", (2, NI, P, S)), scratch("k_parts", (2, NI, P, S))
    v_d = scratch("values", (NI, S, P))
    q2_d, k2_d = scratch("q2_parts", (2, NI, P, S)), scratch("k2_parts", (2, NI, P, S))
    v2_d = scratch("values2", (NI, S, P))
    bias_d = scratch("prior_bias", (B, S, S))
    o_d, o2_d = scratch("attended", (NI, P, S)), scratch("attended2", (NI, P, S))
    skew_d = scratch("position_scores", (8, P * UW))
    x1_d = scratch("x1", (B * 2, P, 4, D))
    y_d = scratch("normed", (2, B * 2, P, KT, CH))
    gates_d = scratch("gates", (B * 2, P, 4, NE))

    io["passed"] = nc.alloc_semaphore("passed")
    prior_block(nc, io, bias_d)
    projection_block(
        nc, io, "pa",
        lambda b, s: io["xT"][:, bass.ds(b * S + s * CH, CH)].rearrange("(k p) n -> p k n", p=P),
        (io["aWq"], io["aWk"], io["aWv"]), (io["zero_cols"], io["zero_cols"], io["abq"], io["abk"]),
        None, q_d, k_d, v_d)
    attention_block(nc, io, "aa", q_d, k_d, v_d, o_d, bias_d=bias_d)
    projection_block(
        nc, io, "pb",
        lambda b, s: o_d[bass.ds(b * NG, NG), :, s * CH:(s + 1) * CH].rearrange("k p n -> p k n"),
        (io["bWq"], io["bWk"], io["bWv"]), (io["abv"], io["abo"], io["bbq"], io["bbk"]),
        (io["aWo"],), q2_d, k2_d, v2_d)
    attention_block(nc, io, "ab", q2_d, k2_d, v2_d, o2_d, skew_d=skew_d)
    adapter_block(nc, io, o2_d, x1_d, y_d, gates_d)
    experts_block(nc, io, x1_d, y_d, gates_d, out_d)




def _layout(inputs):
    import numpy as np

    a = {k: np.asarray(v) for k, v in inputs.items()}

    def cols(v):
        return v.reshape(-1, P).T

    x = a["x"].reshape(B * S, D)
    out = {"xT": x.T}
    for short, name in (("a", "L0_cond_"), ("b", "L0_attn_")):
        for n in "qkvo":
            out[f"{short}W{n}"] = a[f"{name}W{n}"].T
            out[f"{short}b{n}"] = cols(a[f"{name}b{n}"])
    w = np.arange(RELW)
    out["relT"] = a["L0_attn_rel_table"][np.clip(NREL - 1 - (w - MAXLEN), 0, NREL - 1)].T
    out["zero_cols"] = np.zeros((P, KT), np.float32)
    out["ident"] = np.eye(P, dtype=np.float32)
    out["iota1"] = np.broadcast_to(np.arange(1, S + 1, dtype=np.float32), (P, S))
    out["iota8"] = np.broadcast_to(np.arange(NE, dtype=np.float32), (P, NE))
    out["prior_idx"] = a["itok_Sx32_0_1023"]
    out["prior_valid"] = a["mask_Sx32_bk1"].view(np.uint8)
    out["prior_mask"] = a["mask_SxS_bk0"].view(np.int32)
    out["uprev"] = np.broadcast_to(a["condB_uprev"].reshape(1, B), (P, B))
    out["lang"] = a["itok_B_0_8"].reshape(1, B)
    out["W1"], out["W2"] = a["L0_cond2_W1"], a["L0_cond2_W2"]
    by_p = [a["L0_cond2_b1"].reshape(LANGS, 1, P)]
    by_p += [a[f"L0_cond2_{n}"].reshape(LANGS, KT, P) for n in ("b2", "gamma", "beta")]
    out["adcols"] = np.concatenate(by_p, axis=1).transpose(0, 2, 1)
    out["gateT"] = a["L0_ffn_gate_w"].T
    out["weight"] = a["L0_ffn_weight"]
    return {k: np.ascontiguousarray(v) for k, v in out.items()}


def kernel(**inputs):
    import concourse.bacc as _bacc
    from concourse.bass_utils import run_bass_kernel_spmd as _run

    nc = _bacc.Bacc("TRN2", target_bir_lowering=False, num_devices=1)
    arrays, io = {}, {}
    for name, a in _layout(inputs).items():
        arrays[f"in_{name}"] = a
        io[name] = nc.dram_tensor(f"in_{name}", a.shape, mybir.dt.from_np(a.dtype), kind="ExternalInput").ap()
    out_d = nc.dram_tensor("out_0", (B, S, D), F32, kind="ExternalOutput").ap()
    build_program(nc, io, out_d)
    r = _run(nc, [arrays], core_ids=[0])
    return r.results[0]["out_0"]
```
